# Optimizing a Trainium2 kernel written in Bass

```python
import numpy as np
import jax
import jax.numpy as jnp

def _softmax(x, axis=-1):
    return jax.nn.softmax(x, axis=axis)

def _gelu(x):
    return jax.nn.gelu(x, approximate=True)

def _silu(x):
    return jax.nn.silu(x)

def _sigmoid(x):
    return jax.nn.sigmoid(x)

def _layernorm(x, axis=-1, eps=1e-05):
    m = jnp.mean(x, axis=axis, keepdims=True)
    v = jnp.var(x, axis=axis, keepdims=True)
    return (x - m) / jnp.sqrt(v + eps)

def _scatter_add(tgt, idx, src, axis=0):
    return tgt.at[idx].add(src)

def _segment_sum(src, seg, n):
    return jax.ops.segment_sum(src, seg, n)
kernel_name = 'mk_xattn_ffn_d2_seqx_r8_0e7dd9'

def setup_inputs(seed: int=0):
    np.random.seed(seed)
    _w = jnp.asarray

    def _rec_inputs():
        import jax
        import jax.numpy as jnp
        _rk = jax.random.key(seed)
        x = 2.818e-05 + 1 * jax.random.normal(jax.random.fold_in(_rk, 1), (4, 256, 256), jnp.float32)
        _lenS = 256 - jax.random.randint(jax.random.fold_in(_rk, 7), (4,), 0, max(1, 256 // 4) + 1, jnp.int32)
        _lenS2 = 256 - jax.random.randint(jax.random.fold_in(_rk, 8), (4,), 0, max(1, 256 // 4) + 1, jnp.int32)
        _ctx_1024P = jax.random.normal(jax.random.fold_in(_rk, 11), (4, 16, 128), jnp.float32)
        _ctx_1024c = jax.random.dirichlet(jax.random.fold_in(_rk, 511), 0.3 * jnp.ones((16,), jnp.float32), (4, 256))
        _ctx_1024t = jnp.einsum('bsk,bkd->bsd', _ctx_1024c, _ctx_1024P)
        _ctx_1024t = _ctx_1024t * jax.lax.rsqrt(jnp.mean(jnp.square(_ctx_1024t)) + 1e-12) * 0.953939
        ctx_1024 = 7.22013e-05 + 1.00017 * (_ctx_1024t + 0.3 * jax.random.normal(jax.random.fold_in(_rk, 611), (4, 256, 128), jnp.float32))
        return (x, ctx_1024)
    x, ctx_1024 = _rec_inputs()

    def _L0_xattn_setup():
        import jax, jax.numpy as jnp
        import numpy as np
        B_, L_, D_MODEL = (4, 256, 128)
        D_STATE, D_CONV, EXPAND = (16, 4, 2)
        D_INNER = EXPAND * D_MODEL
        DT_RANK = (D_MODEL + 15) // 16

        def silu(x):
            return x * jax.nn.sigmoid(x)
        key = jax.random.key(seed)
        ks = jax.random.split(key, 10)
        f32 = jnp.float32
        hidden_states = jax.random.normal(ks[0], (B_, L_, D_MODEL), dtype=f32)
        z = jax.random.normal(ks[1], (B_, D_INNER, L_), dtype=f32)
        in_proj_w = jax.random.normal(ks[2], (D_INNER, D_MODEL), dtype=f32) * 0.02
        conv_w = jax.random.normal(ks[3], (D_INNER, 1, D_CONV), dtype=f32) * 0.1
        conv_b = jax.random.normal(ks[4], (D_INNER,), dtype=f32) * 0.02
        x_proj_w = jax.random.normal(ks[5], (DT_RANK + 2 * D_STATE, D_INNER), dtype=f32) * 0.02
        dt_proj_w = jax.random.uniform(ks[6], (D_INNER, DT_RANK), dtype=f32, minval=-DT_RANK ** (-0.5), maxval=DT_RANK ** (-0.5))
        dt = jnp.exp(jax.random.uniform(ks[7], (D_INNER,), dtype=f32, minval=np.log(0.001), maxval=np.log(0.1)))
        dt_proj_b = jnp.log(jnp.expm1(dt))
        A_log = jnp.log(jnp.broadcast_to(jnp.arange(1, D_STATE + 1, dtype=f32), (D_INNER, D_STATE)))
        D = jnp.ones((D_INNER,), f32)
        return {'hidden_states': hidden_states, 'z': z, 'in_proj_w': in_proj_w, 'conv_w': conv_w, 'conv_b': conv_b, 'x_proj_w': x_proj_w, 'dt_proj_w': dt_proj_w, 'dt_proj_b': dt_proj_b, 'A_log': A_log, 'D': D}
    _L0_xattn_all = _L0_xattn_setup()
    _L0_xattn_in = {k: v for k, v in _L0_xattn_all.items() if k in ('in_proj_w', 'conv_w', 'conv_b', 'x_proj_w', 'dt_proj_w', 'dt_proj_b', 'A_log', 'D')}
    del _L0_xattn_all

    def _L0_ffn_setup():
        import jax, jax.numpy as jnp
        import numpy as np
        E, K = (16, 4)
        C, H = (256, 448)
        B, T = (2, 64)
        STD = 0.02
        key = jax.random.key(seed)
        ks = jax.random.split(key, 5)
        x = jax.random.normal(ks[0], (B, T, C), jnp.float32)
        W_up = jax.random.normal(ks[1], (E, H, C), jnp.float32) * STD
        W_gate = jax.random.normal(ks[2], (E, H, C), jnp.float32) * STD
        W_down = jax.random.normal(ks[3], (E, C, H), jnp.float32) * STD
        gate_inp = jax.random.normal(ks[4], (E, C), jnp.float32) * STD
        return {'x': x, 'W_up': W_up, 'W_gate': W_gate, 'W_down': W_down, 'gate_inp': gate_inp}
    _L0_ffn_all = _L0_ffn_setup()
    _L0_ffn_in = {k: v for k, v in _L0_ffn_all.items() if k in ('W_up', 'W_gate', 'W_down', 'gate_inp')}
    del _L0_ffn_all

    def _L1_xattn_setup():
        import jax, jax.numpy as jnp
        import numpy as np
        import math
        B, L, DM = (2, 256, 128)
        DS, DC, EXP = (16, 4, 2)
        DI = EXP * DM
        DR = math.ceil(DM / 16)
        DT_MIN, DT_MAX, DT_FLOOR = (0.001, 0.1, 0.0001)

        def _ssm_forward(hidden_states, z, in_proj_w, conv_w, conv_b, x_proj_w, dt_proj_w, dt_proj_b, A_log, D):
            b = hidden_states.shape[0]
            x = jnp.einsum('ed,bld->bel', in_proj_w, hidden_states)
            xp = jnp.pad(x, ((0, 0), (0, 0), (DC - 1, 0)))
            xc = jax.lax.conv_general_dilated(xp, conv_w[:, None, :], window_strides=(1,), padding='VALID', dimension_numbers=('NCH', 'OIH', 'NCH'), feature_group_count=DI)
            u = jax.nn.silu(xc + conv_b[None, :, None])
            x_dbl = jnp.einsum('ke,bel->bkl', x_proj_w, u)
            dt_lo = x_dbl[:, :DR]
            Bm = x_dbl[:, DR:DR + DS]
            Cm = x_dbl[:, DR + DS:]
            delta = jax.nn.softplus(jnp.einsum('er,brl->bel', dt_proj_w, dt_lo) + dt_proj_b[None, :, None])
            A = -jnp.exp(A_log)

            def step(state, xs):
                d_t, B_t, C_t, u_t = xs
                dA = jnp.exp(d_t[..., None] * A)
                state = state * dA + (d_t * u_t)[..., None] * B_t[:, None, :]
                y_t = jnp.einsum('ben,bn->be', state, C_t)
                return (state, y_t)
            xs = (jnp.moveaxis(delta, -1, 0), jnp.moveaxis(Bm, -1, 0), jnp.moveaxis(Cm, -1, 0), jnp.moveaxis(u, -1, 0))
            state0 = jnp.zeros((b, DI, DS), delta.dtype)
            _, ys = jax.lax.scan(step, state0, xs)
            y = jnp.moveaxis(ys, 0, -1)
            y = y + D[None, :, None] * u
            y = y * jax.nn.silu(z)
            return jnp.swapaxes(y, 1, 2)
        key = jax.random.key(seed)
        ks = jax.random.split(key, 8)
        hidden_states = jax.random.normal(ks[0], (B, L, DM), jnp.float32)
        z = jax.random.normal(ks[1], (B, DI, L), jnp.float32)
        in_proj_w = jax.random.normal(ks[2], (DI, DM), jnp.float32) * DM ** (-0.5)
        conv_w = jax.random.normal(ks[3], (DI, DC), jnp.float32) * DC ** (-0.5)
        conv_b = jnp.zeros((DI,), jnp.float32)
        x_proj_w = jax.random.normal(ks[4], (DR + 2 * DS, DI), jnp.float32) * DI ** (-0.5)
        dt_std = DR ** (-0.5)
        dt_proj_w = jax.random.uniform(ks[5], (DI, DR), jnp.float32, -dt_std, dt_std)
        dt = jnp.exp(jax.random.uniform(ks[6], (DI,), jnp.float32) * (math.log(DT_MAX) - math.log(DT_MIN)) + math.log(DT_MIN))
        dt = jnp.clip(dt, DT_FLOOR)
        dt_proj_b = dt + jnp.log(-jnp.expm1(-dt))
        A_log = jnp.log(jnp.broadcast_to(jnp.arange(1, DS + 1, dtype=jnp.float32), (DI, DS)))
        D = jnp.ones((DI,), jnp.float32)
        return dict(hidden_states=hidden_states, z=z, in_proj_w=in_proj_w, conv_w=conv_w, conv_b=conv_b, x_proj_w=x_proj_w, dt_proj_w=dt_proj_w, dt_proj_b=dt_proj_b, A_log=A_log, D=D)
    _L1_xattn_all = _L1_xattn_setup()
    _L1_xattn_in = {k: v for k, v in _L1_xattn_all.items() if k in ('in_proj_w', 'conv_w', 'conv_b', 'x_proj_w', 'dt_proj_w', 'dt_proj_b', 'A_log', 'D')}
    del _L1_xattn_all

    def _L1_ffn_setup():
        import jax, jax.numpy as jnp
        import numpy as np
        TOPK = 6
        CAP = 128
        ROUTE_SCALE = 1.0
        key = jax.random.key(seed)
        k = jax.random.split(key, 6)
        B, T, C = (2, 256, 256)
        E, H, HS = (64, 32, 64)
        std = 0.01
        return {'x': jax.random.normal(k[0], (B, T, C), jnp.float32), 'w_gate': jax.random.normal(k[1], (C, E), jnp.float32) * std, 'w_shared_up': jax.random.normal(k[2], (C, 2 * HS), jnp.float32) * std, 'w_shared_down': jax.random.normal(k[3], (HS, C), jnp.float32) * std, 'w_up': jax.random.normal(k[4], (E, C, 2 * H), jnp.float32) * std, 'w_down': jax.random.normal(k[5], (E, H, C), jnp.float32) * std}
    _L1_ffn_all = _L1_ffn_setup()
    _L1_ffn_in = {k: v for k, v in _L1_ffn_all.items() if k in ('w_gate', 'w_shared_up', 'w_shared_down', 'w_up', 'w_down')}
    del _L1_ffn_all
    return {'x': x, 'ctx_1024': ctx_1024, 'L0_xattn_in_proj_w': _L0_xattn_in['in_proj_w'], 'L0_xattn_conv_w': _L0_xattn_in['conv_w'], 'L0_xattn_conv_b': _L0_xattn_in['conv_b'], 'L0_xattn_x_proj_w': _L0_xattn_in['x_proj_w'], 'L0_xattn_dt_proj_w': _L0_xattn_in['dt_proj_w'], 'L0_xattn_dt_proj_b': _L0_xattn_in['dt_proj_b'], 'L0_xattn_A_log': _L0_xattn_in['A_log'], 'L0_xattn_D': _L0_xattn_in['D'], 'L0_ffn_W_up': _L0_ffn_in['W_up'], 'L0_ffn_W_gate': _L0_ffn_in['W_gate'], 'L0_ffn_W_down': _L0_ffn_in['W_down'], 'L0_ffn_gate_inp': _L0_ffn_in['gate_inp'], 'L1_xattn_in_proj_w': _L1_xattn_in['in_proj_w'], 'L1_xattn_conv_w': _L1_xattn_in['conv_w'], 'L1_xattn_conv_b': _L1_xattn_in['conv_b'], 'L1_xattn_x_proj_w': _L1_xattn_in['x_proj_w'], 'L1_xattn_dt_proj_w': _L1_xattn_in['dt_proj_w'], 'L1_xattn_dt_proj_b': _L1_xattn_in['dt_proj_b'], 'L1_xattn_A_log': _L1_xattn_in['A_log'], 'L1_xattn_D': _L1_xattn_in['D'], 'L1_ffn_w_gate': _L1_ffn_in['w_gate'], 'L1_ffn_w_shared_up': _L1_ffn_in['w_shared_up'], 'L1_ffn_w_shared_down': _L1_ffn_in['w_shared_down'], 'L1_ffn_w_up': _L1_ffn_in['w_up'], 'L1_ffn_w_down': _L1_ffn_in['w_down']}

def reference(x, ctx_1024, L0_xattn_in_proj_w, L0_xattn_conv_w, L0_xattn_conv_b, L0_xattn_x_proj_w, L0_xattn_dt_proj_w, L0_xattn_dt_proj_b, L0_xattn_A_log, L0_xattn_D, L0_ffn_W_up, L0_ffn_W_gate, L0_ffn_W_down, L0_ffn_gate_inp, L1_xattn_in_proj_w, L1_xattn_conv_w, L1_xattn_conv_b, L1_xattn_x_proj_w, L1_xattn_dt_proj_w, L1_xattn_dt_proj_b, L1_xattn_A_log, L1_xattn_D, L1_ffn_w_gate, L1_ffn_w_shared_up, L1_ffn_w_shared_down, L1_ffn_w_up, L1_ffn_w_down):
    import jax
    import jax.numpy as jnp

    def _L0_xattn_ref(hidden_states, z, in_proj_w, conv_w, conv_b, x_proj_w, dt_proj_w, dt_proj_b, A_log, D):
        import jax, jax.numpy as jnp
        import numpy as np
        B_, L_, D_MODEL = (4, 256, 128)
        D_STATE, D_CONV, EXPAND = (16, 4, 2)
        D_INNER = EXPAND * D_MODEL
        DT_RANK = (D_MODEL + 15) // 16

        def silu(x):
            return x * jax.nn.sigmoid(x)
        Bsz, L, _ = hidden_states.shape
        d_inner, _, d_conv = conv_w.shape
        dt_rank = dt_proj_w.shape[1]
        d_state = A_log.shape[1]
        x = jnp.einsum('bld,ed->bel', hidden_states, in_proj_w)
        xc = jax.lax.conv_general_dilated(x, conv_w, window_strides=(1,), padding=[(d_conv - 1, 0)], feature_group_count=d_inner, dimension_numbers=('NCH', 'OIH', 'NCH'))
        x = silu(xc + conv_b[None, :, None])
        x_dbl = jnp.einsum('bdl,ed->bel', x, x_proj_w)
        dt_low, Bm, Cm = jnp.split(x_dbl, [dt_rank, dt_rank + d_state], axis=1)
        dt = jnp.einsum('brl,dr->bdl', dt_low, dt_proj_w)
        dt = jax.nn.softplus(dt + dt_proj_b[None, :, None])
        A = -jnp.exp(A_log)
        dt_t = jnp.moveaxis(dt, -1, 0)
        B_t = jnp.moveaxis(Bm, -1, 0)
        C_t = jnp.moveaxis(Cm, -1, 0)
        u_t = jnp.moveaxis(x, -1, 0)

        def step(state, inp):
            d, b, c, u = inp
            dA = jnp.exp(d[..., None] * A)
            state = state * dA + (d * u)[..., None] * b[:, None, :]
            y = jnp.einsum('bdn,bn->bd', state, c)
            return (state, y)
        state0 = jnp.zeros((Bsz, d_inner, d_state), x.dtype)
        _, ys = jax.lax.scan(step, state0, (dt_t, B_t, C_t, u_t))
        y = jnp.moveaxis(ys, 0, 2)
        y = y + D[None, :, None] * x
        y = y * silu(z)
        return jnp.swapaxes(y, 1, 2)

    def _L0_ffn_ref(x, W_up, W_gate, W_down, gate_inp):
        import jax, jax.numpy as jnp
        import numpy as np
        E, K = (16, 4)
        C, H = (256, 448)
        B, T = (2, 64)
        STD = 0.02
        b, t, c = x.shape
        xf = x.reshape(b * t, c)
        logits = xf @ gate_inp.T
        topv, topi = jax.lax.top_k(logits, K)
        w = jax.nn.softmax(topv.astype(jnp.float32), axis=-1).astype(x.dtype)
        n = xf.shape[0]
        dense_w = jnp.zeros((n, E), x.dtype).at[jnp.arange(n)[:, None], topi].set(w)
        u = jnp.einsum('nc,ehc->neh', xf, W_up)
        g = jnp.einsum('nc,ehc->neh', xf, W_gate)
        h = jax.nn.silu(g) * u
        y = jnp.einsum('neh,ech,ne->nc', h, W_down, dense_w)
        return y.reshape(b, t, c)

    def _L1_xattn_ref(hidden_states, z, in_proj_w, conv_w, conv_b, x_proj_w, dt_proj_w, dt_proj_b, A_log, D):
        import jax, jax.numpy as jnp
        import numpy as np
        import math
        B, L, DM = (2, 256, 128)
        DS, DC, EXP = (16, 4, 2)
        DI = EXP * DM
        DR = math.ceil(DM / 16)
        DT_MIN, DT_MAX, DT_FLOOR = (0.001, 0.1, 0.0001)

        def _ssm_forward(hidden_states, z, in_proj_w, conv_w, conv_b, x_proj_w, dt_proj_w, dt_proj_b, A_log, D):
            b = hidden_states.shape[0]
            x = jnp.einsum('ed,bld->bel', in_proj_w, hidden_states)
            xp = jnp.pad(x, ((0, 0), (0, 0), (DC - 1, 0)))
            xc = jax.lax.conv_general_dilated(xp, conv_w[:, None, :], window_strides=(1,), padding='VALID', dimension_numbers=('NCH', 'OIH', 'NCH'), feature_group_count=DI)
            u = jax.nn.silu(xc + conv_b[None, :, None])
            x_dbl = jnp.einsum('ke,bel->bkl', x_proj_w, u)
            dt_lo = x_dbl[:, :DR]
            Bm = x_dbl[:, DR:DR + DS]
            Cm = x_dbl[:, DR + DS:]
            delta = jax.nn.softplus(jnp.einsum('er,brl->bel', dt_proj_w, dt_lo) + dt_proj_b[None, :, None])
            A = -jnp.exp(A_log)

            def step(state, xs):
                d_t, B_t, C_t, u_t = xs
                dA = jnp.exp(d_t[..., None] * A)
                state = state * dA + (d_t * u_t)[..., None] * B_t[:, None, :]
                y_t = jnp.einsum('ben,bn->be', state, C_t)
                return (state, y_t)
            xs = (jnp.moveaxis(delta, -1, 0), jnp.moveaxis(Bm, -1, 0), jnp.moveaxis(Cm, -1, 0), jnp.moveaxis(u, -1, 0))
            state0 = jnp.zeros((b, DI, DS), delta.dtype)
            _, ys = jax.lax.scan(step, state0, xs)
            y = jnp.moveaxis(ys, 0, -1)
            y = y + D[None, :, None] * u
            y = y * jax.nn.silu(z)
            return jnp.swapaxes(y, 1, 2)
        return _ssm_forward(hidden_states, z, in_proj_w, conv_w, conv_b, x_proj_w, dt_proj_w, dt_proj_b, A_log, D)

    def _L1_ffn_ref(x, w_gate, w_shared_up, w_shared_down, w_up, w_down):
        import jax, jax.numpy as jnp
        import numpy as np
        TOPK = 6
        CAP = 128
        ROUTE_SCALE = 1.0
        B, T, C = x.shape
        E = w_gate.shape[1]
        x_flat = x.reshape(-1, C)
        N = x_flat.shape[0]
        su = x_flat @ w_shared_up
        y_s, g_s = jnp.split(su, 2, axis=-1)
        shared = jax.nn.silu(g_s) * y_s @ w_shared_down
        scores = jax.nn.sigmoid(x_flat @ w_gate)
        _, topk_idx = jax.lax.top_k(scores, TOPK)
        w = jnp.take_along_axis(scores, topk_idx, axis=-1)
        w = w / w.sum(-1, keepdims=True) * ROUTE_SCALE
        flat_e = topk_idx.reshape(-1)
        oh = jax.nn.one_hot(flat_e, E, dtype=jnp.int32)
        pos = jnp.take_along_axis(jnp.cumsum(oh, axis=0), flat_e[:, None], axis=1)[:, 0] - 1
        valid = pos < CAP
        pos_c = jnp.where(valid, pos, CAP - 1)
        token_ids = jnp.repeat(jnp.arange(N), TOPK)
        x_disp = jnp.zeros((E, CAP, C), x.dtype).at[flat_e, pos].set(x_flat[token_ids], mode='drop')
        up = jnp.einsum('ecd,edh->ech', x_disp, w_up)
        g_r, v_r = jnp.split(up, 2, axis=-1)
        h_r = jax.nn.silu(g_r) * v_r
        out_r = jnp.einsum('ech,ehd->ecd', h_r, w_down)
        y_ts = out_r[flat_e, pos_c]
        y_ts = jnp.where(valid[:, None], y_ts, 0.0)
        routed = (y_ts.reshape(N, TOPK, C) * w[:, :, None]).sum(axis=1)
        return (shared + routed).reshape(B, T, C)
    x = x + _L0_xattn_ref(ctx_1024, _layernorm(x, axis=-1), L0_xattn_in_proj_w, L0_xattn_conv_w, L0_xattn_conv_b, L0_xattn_x_proj_w, L0_xattn_dt_proj_w, L0_xattn_dt_proj_b, L0_xattn_A_log, L0_xattn_D)
    x = x + _L0_ffn_ref(_layernorm(x, axis=-1), L0_ffn_W_up, L0_ffn_W_gate, L0_ffn_W_down, L0_ffn_gate_inp)
    x = x + _L1_xattn_ref(ctx_1024, _layernorm(x, axis=-1), L1_xattn_in_proj_w, L1_xattn_conv_w, L1_xattn_conv_b, L1_xattn_x_proj_w, L1_xattn_dt_proj_w, L1_xattn_dt_proj_b, L1_xattn_A_log, L1_xattn_D)
    x = x + _L1_ffn_ref(_layernorm(x, axis=-1), L1_ffn_w_gate, L1_ffn_w_shared_up, L1_ffn_w_shared_down, L1_ffn_w_up, L1_ffn_w_down)
    return x

_drawn_inputs = setup_inputs


def setup_inputs(seed=0):
    import zlib

    import numpy as np

    out = dict(_drawn_inputs(seed))
    spreads = {'L0_xattn_D': (1.0, 0.6), 'L1_xattn_conv_b': (0.0, 0.307), 'L1_xattn_D': (1.0, 0.2)}
    factors = {'L0_xattn_in_proj_w': 4.241,
     'L0_xattn_conv_w': 4.451,
     'L0_xattn_conv_b': 8.0,
     'L0_xattn_x_proj_w': 8.0,
     'L0_xattn_dt_proj_w': 8.0,
     'L0_xattn_dt_proj_b': 8.0,
     'L0_xattn_A_log': 8.0,
     'L0_ffn_W_up': 4.935,
     'L0_ffn_W_gate': 4.966,
     'L0_ffn_W_down': 4.899,
     'L0_ffn_gate_inp': 5.684,
     'L1_xattn_dt_proj_w': 5.877,
     'L1_ffn_w_gate': 8.0,
     'L1_ffn_w_shared_up': 8.0,
     'L1_ffn_w_shared_down': 8.0,
     'L1_ffn_w_up': 8.0,
     'L1_ffn_w_down': 8.0}
    for name, (base, spread) in spreads.items():
        noise = np.random.default_rng([zlib.crc32(name.encode()), seed]).standard_normal(out[name].shape)
        drawn = base * np.exp(spread * noise) if base else spread * noise
        out[name] = jnp.asarray(drawn.astype(out[name].dtype))
    for name, factor in factors.items():
        out[name] = (out[name] * factor).astype(out[name].dtype)
    return out
```

```python
from contextlib import ExitStack

import concourse.bass as bass
from concourse import mybir

ALU = mybir.AluOpType
ACT = mybir.ActivationFunctionType
F32 = mybir.dt.float32
BF16 = mybir.dt.bfloat16
AX_X = mybir.AxisListType.X

P = 128
BANK = 512


class Stage:

    def __init__(self, sem):
        self.sem, self.n = sem, 0

    def mark(self, ins, by=1):
        ins.then_inc(self.sem, by)
        self.n += by
        return self.n


def build(nc, x, ctxT, in_projT, ssm_par, x_projT, dt_projT, gate0T, up0T, down0T,
          gate1T, sh_upT, sh_down, grp1, ident_in, sel3_in, tri_in, sel64_in, out):
    NL = 2
    B, L = 4, 256
    TOK = B * L
    TT = TOK // P
    C = x.shape[1]
    KC = C // P
    DI = in_projT.shape[2]
    ND = DI // P
    NS = 16
    DR = dt_projT.shape[1]
    HALF = TOK // 2
    E0 = up0T.shape[0]
    H0 = down0T.shape[1] * down0T.shape[2]
    HP = down0T.shape[1]
    HK = down0T.shape[2]
    TOPK0 = 4
    E1 = gate1T.shape[2]
    NG = grp1.shape[0]
    TOPK1 = 6
    CAP = 128
    EPS = 1e-5
    RING = 2
    STEPS = 2 * NS

    with ExitStack() as ctx:
        def sb(name, shape, dt=F32):
            return ctx.enter_context(nc.sbuf_tensor(name, shape, dt))

        def sem(name):
            return ctx.enter_context(nc.semaphore(name))

        ps = ctx.enter_context(nc.psum_tensor("ps", [P, 8, BANK], F32))

        ident = sb("ident", [P, P])
        sel3 = sb("sel3", [P, 2 * NS], BF16)
        tri = sb("tri", [P, 2, P], BF16)
        sel64 = sb("sel64", [P, NG * P], BF16)
        xs = sb("xs", [P, TT, C])
        ctx_sb = sb("ctx_sb", [P, TOK])
        inp = sb("inp", [P, NL, DI])
        par = sb("par", [P, NL, ND, 8])
        alog = sb("alog", [P, NL, ND, NS])
        xpr = sb("xpr", [P, NL, ND, P])
        dtp_w = sb("dtp_w", [DR, NL, DI])
        gate0 = sb("gate0", [P, KC, E0])
        gate1 = sb("gate1", [P, KC, E1])
        shu = sb("shu", [P, KC, P])
        shd = sb("shd", [P // 2, C])

        u = [sb(f"u{k}", [P, ND, TOK]) for k in range(NL)]
        delta = [sb(f"delta{k}", [P, ND, TOK]) for k in range(NL)]
        du = [sb(f"du{k}", [P, ND, TOK]) for k in range(NL)]
        bc3 = [sb(f"bc3{k}", [P, TOK], BF16) for k in range(NL)]
        negA = sb("negA", [P, NL, ND, NS])
        diagD = sb("diagD", [P, NL, ND, P])
        dtlo = sb("dtlo", [DR, TOK])
        t0 = sb("t0", [P, ND, TOK])
        t1 = sb("t1", [P, ND, TOK])
        dA = sb("dA", [P, RING, ND, HALF])
        dBu = sb("dBu", [P, RING, ND, HALF])
        hs = sb("hs", [P, RING, ND, HALF])
        hC = sb("hC", [P, RING, ND, HALF])
        Csb = sb("Csb", [P, RING, HALF])
        y1 = sb("y1", [P, ND, TOK])

        stats = sb("stats", [P, TT, 6])
        mv = sb("mv", [P, TT, 2])
        rstd = sb("rstd", [P, TT])
        expo = sb("expo", [P, TT])
        xnT = sb("xnT", [P, KC, TOK])
        lg = sb("lg", [P, TT, E1])
        top8 = sb("top8", [P, TT, 8])
        r0 = sb("r0", [P, TT, E1])
        r1 = sb("r1", [P, TT, E1])
        r2 = sb("r2", [P, TT, E1])
        rsum = sb("rsum", [P, TT])
        need = sb("need", [P, TT])
        first = sb("first", [P, TT, E1])
        maskb = sb("maskb", [P, TT, E1], BF16)
        w0 = sb("w0", [P, TT, E0])
        w2x = sb("w2x", [P, TT, 2, E1])
        wp12 = sb("wp12", [P, TOK], BF16)
        wp3 = sb("wp3", [P, TOK], BF16)
        wtmp, wmid = y1[:, 0, :], y1[0:E1, 1, :].bitcast(BF16)[:, 0:TOK]

        ug0 = sb("ug0", [P, RING, KC, 2 * H0])
        dn0 = sb("dn0", [HP, RING, HK, C])
        th, pg, hx, hT = hs[:, 0, :, :], hs[:, 1, :, :], hC[:, 0, :, :], hC[:, 1, :, :]
        GR = 4
        g1w = sb("g1w", [P, GR, grp1.shape[2]])

        s_in = [sem(f"s_in{i}") for i in range(6)]
        s_ug = [sem(f"s_ug{i}") for i in range(RING)]
        s_dn = [sem(f"s_dn{i}") for i in range(RING)]
        s_g1 = [sem(f"s_g1{i}") for i in range(GR)]
        s_store = sem("s_store")
        pe_s, act_s, dve_s, pool_s = Stage(sem("pe_s")), Stage(sem("act_s")), Stage(sem("dve_s")), Stage(sem("pool_s"))
        b_ready, c_ready = sem("b_ready"), sem("c_ready")
        da_ready, csb_ready = sem("da_ready"), sem("csb_ready")
        dbu_done, scan_done = sem("dbu_done"), sem("scan_done")
        hc_done, y_done = sem("hc_done"), sem("y_done")
        f_up, f_th, f_p, f_h, f_T, f_hT, f_dn, f_acc = (sem(f"f_{n}") for n in
            ("up", "th", "p", "h", "T", "hT", "dn", "acc"))
        g_g, g_v, g_w, g_th, g_p, g_q, g_h, g_dn = (sem(f"g_{n}") for n in
            ("g", "v", "w", "th", "p", "q", "h", "dn"))

        block = ctx.enter_context(nc.Block())

        x_t = x.rearrange("(j p) c -> p j c", p=P)
        out_t = out.rearrange("(j p) c -> p j c", p=P)

        PE_ORDER = [f"{n}{k}" for k in range(NL) for n in ("xin", "xdbl", "dtp")]
        PE_ORDER += ["y_init0_0", "y_init0_1", "y_all0", "y_init1_0", "y_init1_1", "y_all1",
                     "yT0", "xnT0", "logit0", "yT1", "xnT1", "logit1", "pos1", "wT1",
                     "sh_up0", "sh_up1", "sh_dn0", "sh_dn1", "ffn1"]
        PE = {n: i + 1 for i, n in enumerate(PE_ORDER)}

        seq = [f"conv0", "u0", "bc0", "v0", "w0", "delta0", "du0",
               "conv1", "u1", "bc1", "v1", "w1", "delta1", "du1", "consts",
               "zstat0", "zh0", "G0", "yz0", "xnew0", "nstat0", "xn0", "xnT0", "lsub0", "route0", "ffn0",
               "zstat1", "zh1", "G1", "yz1", "xnew1", "nstat1", "xn1", "xnT1", "lsub1", "sel1", "route1",
               "wparts1", "sh_h0", "sh_h1", "out"]
        DVE = {n: i + 1 for i, n in enumerate(seq)}
        aseq = ["negA", "th_u0", "hf_u0", "dtlo0", "abs0", "e0", "ln0",
                "th_u1", "hf_u1", "dtlo1", "abs1", "e1", "ln1",
                "zth0", "y1copy", "ex0", "zth1", "ex1", "sh_th0", "sh_th1"]
        AC = {n: i + 1 for i, n in enumerate(aseq)}
        POOL = {n: i + 1 for i, n in enumerate(["zero", "zr0", "nr0", "zr1", "nr1"])}

        @block.sync
        def _(sp):
            sp.dma_start(ctx_sb[:, :], ctxT).then_inc(s_in[0], 16)
            sp.dma_start(inp[:, :, :], in_projT.rearrange("k p d -> p k d")).then_inc(s_in[0], 16)
            sp.dma_start(par[:, :, :, :], ssm_par[:, :, :, 0:8]).then_inc(s_in[0], 16)
            sp.dma_start(alog[:, :, :, :], ssm_par[:, :, :, 8:8 + NS]).then_inc(s_in[1], 16)
            sp.dma_start(xpr[:, :, :, :], x_projT).then_inc(s_in[1], 16)
            sp.dma_start(dtp_w[:, :, :], dt_projT.rearrange("k r d -> r k d")).then_inc(s_in[1], 16)
            sp.dma_start(ident[:, :], ident_in).then_inc(s_in[2], 16)
            sp.dma_start(sel3[:, :], sel3_in).then_inc(s_in[2], 16)
            sp.dma_start(xs[:, :, :], x_t).then_inc(s_in[3], 16)
            sp.dma_start(tri[:, :, :], tri_in).then_inc(s_in[4], 16)
            sp.dma_start(sel64[:, :], sel64_in).then_inc(s_in[4], 16)
            sp.dma_start(gate0[:, :, :], gate0T).then_inc(s_in[4], 16)
            sp.dma_start(gate1[:, :, :], gate1T).then_inc(s_in[4], 16)
            sp.dma_start(shu[:, :, :], sh_upT).then_inc(s_in[4], 16)
            sp.dma_start(shd[:, :], sh_down).then_inc(s_in[4], 16)
            for q in range(RING):
                sp.dma_start(ug0[:, q, :, :], up0T[q]).then_inc(s_ug[q], 16)
                sp.dma_start(dn0[:, q, :, :], down0T[q]).then_inc(s_dn[q], 16)
            for q in range(GR):
                sp.dma_start(g1w[:, q, :], grp1[q]).then_inc(s_g1[q], 16)
            with sp.Fori(1, E0 // RING) as i:
                for q in range(RING):
                    sp.wait_ge(f_up, (i * RING + q - RING + 1) * TT)
                    sp.dma_start(ug0[:, q, :, :], up0T[bass.ds(i * RING + q, 1), :, :, :].rearrange("o p k n -> (o p) k n")).then_inc(s_ug[q], 16)
                    sp.wait_ge(f_dn, (i * RING + q - RING + 1) * TT)
                    sp.dma_start(dn0[:, q, :, :], down0T[bass.ds(i * RING + q, 1), :, :, :].rearrange("o p k n -> (o p) k n")).then_inc(s_dn[q], 16)
            with sp.Fori(1, NG // GR) as i:
                for q in range(GR):
                    sp.wait_ge(g_dn, (i * GR + q - GR + 1) * 2)
                    sp.dma_start(g1w[:, q, :], grp1[bass.ds(i * GR + q, 1), :, :].rearrange("o p n -> (o p) n")).then_inc(s_g1[q], 16)
            sp.wait_ge(dve_s.sem, DVE["out"])
            sp.dma_start(out_t, xs[:, :, :]).then_inc(s_store, 16)
            sp.wait_ge(s_store, 16)

        @block.tensor
        def _(pe):
            def mark(ins, name):
                assert PE[name] == pe_s.n + 1, name
                pe_s.mark(ins)

            def prep(k):
                if k == 0:
                    pe.wait_ge(s_in[0], 48)
                else:
                    pe.wait_ge(dve_s.sem, DVE["v0"])
                    pe.wait_ge(act_s.sem, AC["abs0"])
                for d in range(ND):
                    for h in range(2):
                        ins = pe.matmul(ps[:, 2 * d + h, :], inp[:, k, d * P:(d + 1) * P],
                                        ctx_sb[:, h * HALF:(h + 1) * HALF], start=True, stop=True)
                mark(ins, f"xin{k}")
                pe.wait_ge(dve_s.sem, DVE[f"u{k}"])
                if k == 0:
                    pe.wait_ge(s_in[1], 48)
                for h in range(2):
                    for d in range(ND):
                        ins = pe.matmul(ps[:, 4 + h, :], xpr[:, k, d, :], u[k][:, d, h * HALF:(h + 1) * HALF],
                                        start=(d == 0), stop=(d == ND - 1))
                mark(ins, f"xdbl{k}")
                pe.wait_ge(act_s.sem, AC[f"dtlo{k}"])
                for d in range(ND):
                    for h in range(2):
                        ins = pe.matmul(ps[:, 2 * d + h, :], dtp_w[:, k, d * P:(d + 1) * P],
                                        dtlo[:, h * HALF:(h + 1) * HALF], start=True, stop=True)
                mark(ins, f"dtp{k}")

            def rep(k, h, n, q, S):
                rhs = bc3[k][:, h * HALF:(h + 1) * HALF]
                pe.wait_ge(dbu_done, S + 1)
                pe.matmul(ps[:, 4 + q, :], sel3[:, bass.ds(n, 1)].to_broadcast([P, P]), rhs,
                          start=True, stop=True).then_inc(b_ready, 1)
                pe.wait_ge(csb_ready, S + 1)
                pe.matmul(ps[:, 6 + q, :], sel3[:, bass.ds(n + NS, 1)].to_broadcast([P, P]), rhs,
                          start=True, stop=True).then_inc(c_ready, 1)

            def ysum(h, q, S):
                pe.wait_ge(hc_done, S + RING + 1)
                for d in range(ND):
                    ins = pe.matmul(ps[:, 2 * h + d, :], ident[:, :], hC[:, q, d, :],
                                    start=False, stop=True, skip_group_check=True)
                ins.then_inc(y_done, 1)

            def mixer(k):
                for h in range(2):
                    base = k * STEPS + h * NS
                    if h == 0:
                        pe.wait_ge(dve_s.sem, DVE["consts"])
                        if k == 1:
                            pe.wait_ge(dve_s.sem, DVE["yz0"])
                    for d in range(ND):
                        ins = pe.matmul(ps[:, 2 * h + d, :], diagD[:, k, d, :],
                                        u[k][:, d, h * HALF:(h + 1) * HALF], start=True, stop=True)
                    mark(ins, f"y_init{k}_{h}")
                    for q in range(RING):
                        rep(k, h, q, q, base + q)
                    with pe.Fori(1, NS // RING) as j:
                        for q in range(RING):
                            rep(k, h, j * RING + q, q, base + j * RING + q)
                            ysum(h, q, base + j * RING + q - RING)
                    for q in range(RING):
                        ysum(h, q, base + NS - RING + q)
                pe.wait_ge(y_done, k * STEPS + STEPS + RING)
                mark(pe.matmul(ps[0:1, 4, 0:1], ident[:, 0:1], ident[:, 0:1], start=True, stop=True), f"y_all{k}")

            def transpose_in(k):
                pe.wait_ge(dve_s.sem, DVE[f"yz{k}"])
                for j in range(TT):
                    for d in range(ND):
                        ins = pe.transpose(ps[:, 4 + j // 2, (j % 2) * C + d * P:(j % 2) * C + (d + 1) * P],
                                           t0[:, d, j * P:(j + 1) * P], ident[:, :])
                mark(ins, f"yT{k}")
                pe.wait_ge(dve_s.sem, DVE[f"xn{k}"])
                if k == 0:
                    pe.wait_ge(act_s.sem, AC["y1copy"])
                for j in range(TT):
                    for c in range(KC):
                        ins = pe.transpose(ps[:, 2 * c + j // 4, (j % 4) * P:(j % 4 + 1) * P],
                                           t1[:, :, :].rearrange("p a b -> p (a b)")[:, j * C + c * P:j * C + (c + 1) * P],
                                           ident[:, :])
                mark(ins, f"xnT{k}")

            def logits(k, gate, E):
                pe.wait_ge(dve_s.sem, DVE[f"xnT{k}"])
                pe.wait_ge(s_in[4], 6 * 16)
                for j in range(TT):
                    for c in range(KC):
                        ins = pe.matmul(ps[:, 4, j * E:(j + 1) * E], xnT[:, c, j * P:(j + 1) * P], gate[:, c, :],
                                        start=(c == 0), stop=(c == KC - 1))
                mark(ins, f"logit{k}")

            def up0(j, q, n):
                pe.wait_ge(f_h, n)
                for part in range(2):
                    for c in range(KC):
                        ins = pe.matmul(ps[:, part, 0:H0], xnT[:, c, j * P:(j + 1) * P],
                                        ug0[:, q, c, part * H0:(part + 1) * H0], start=(c == 0), stop=(c == KC - 1))
                ins.then_inc(f_up, 1)

            def turn0(b, n):
                pe.wait_ge(f_h, n + 1)
                pe.wait_ge(f_hT, n)
                for m in range(HK):
                    ins = pe.transpose(ps[0:HP, 2, m * P:(m + 1) * P], hx[:, b, m * HP:(m + 1) * HP], ident[:, :])
                ins.then_inc(f_T, 1)

            def down0(b, q, n):
                pe.wait_ge(f_hT, n + 1)
                pe.wait_ge(f_acc, n)
                for m in range(HK):
                    ins = pe.matmul(ps[:, 3, 0:C], hT[0:HP, b, m * P:(m + 1) * P], dn0[:, q, m, :],
                                    start=(m == 0), stop=(m == HK - 1))
                ins.then_inc(f_dn, 1)

            def expert0(q, n0, first):
                if first and q == 0:
                    pass
                for j in range(TT):
                    if first and q == 0 and j == 0:
                        for part in range(2):
                            for c in range(KC):
                                ins = pe.matmul(ps[:, part, 0:H0], xnT[:, c, j * P:(j + 1) * P],
                                                ug0[:, q, c, part * H0:(part + 1) * H0], start=(c == 0), stop=(c == KC - 1))
                        ins.then_inc(f_up, 1)
                        pe.wait_ge(f_h, 1)
                        for m in range(HK):
                            ins = pe.transpose(ps[0:HP, 2, m * P:(m + 1) * P], hx[:, 0, m * HP:(m + 1) * HP], ident[:, :])
                        ins.then_inc(f_T, 1)
                        continue
                    up0(j, q, n0 + j)
                    if j > 0:
                        if first and q == 0 and j == 1:
                            pe.wait_ge(f_hT, 1)
                            for m in range(HK):
                                ins = pe.matmul(ps[:, 3, 0:C], hT[0:HP, 0, m * P:(m + 1) * P], dn0[:, q, m, :],
                                                start=(m == 0), stop=(m == HK - 1))
                            ins.then_inc(f_dn, 1)
                        else:
                            down0((j - 1) % 2, q, n0 + j - 1)
                    turn0(j % 2, n0 + j)
                down0((TT - 1) % 2, q, n0 + TT - 1)

            def ffn0():
                pe.wait_ge(dve_s.sem, DVE["route0"])
                for q in range(RING):
                    pe.wait_ge(s_ug[q], 16)
                    pe.wait_ge(s_dn[q], 16)
                    expert0(q, q * TT, True)
                with pe.Fori(1, E0 // RING) as i:
                    for q in range(RING):
                        pe.wait_ge(s_ug[q], (i + 1) * 16)
                        pe.wait_ge(s_dn[q], (i + 1) * 16)
                        expert0(q, (i * RING + q) * TT, False)

            def shared1():
                for h in range(2):
                    if h == 1:
                        pe.wait_ge(dve_s.sem, DVE["sh_h0"])
                    for c in range(KC):
                        ins = pe.matmul(ps[:, 4, :], shu[:, c, :], xnT[:, c, h * HALF:(h + 1) * HALF],
                                        start=(c == 0), stop=(c == KC - 1))
                    mark(ins, f"sh_up{h}")
                for h in range(2):
                    pe.wait_ge(dve_s.sem, DVE[f"sh_h{h}"])
                    for t in range(4):
                        j = 4 * h + t
                        ins = pe.matmul(ps[:, j // 2, (j % 2) * C:(j % 2 + 1) * C], hT[0:P // 2, h, t * P:(t + 1) * P],
                                        shd[:, :], start=(j % 2 == 0), stop=True, skip_group_check=True)
                    mark(ins, f"sh_dn{h}")

            def up1(q, h, g, n):
                if n is not None:
                    pe.wait_ge(g_p, n)
                for part, done in ((0, g_g), (1, g_v)):
                    if part == 1 and n is not None:
                        pe.wait_ge(g_q, n)
                    for c in range(KC):
                        ins = pe.matmul(ps[:, 4 + part, :], g1w[:, q, (2 * c + part) * P:(2 * c + part + 1) * P],
                                        xnT[:, c, h * HALF:(h + 1) * HALF], start=(c == 0), stop=(c == KC - 1))
                    ins.then_inc(done, 1)
                if n is not None:
                    pe.wait_ge(g_h, n)
                sel = sel64[:, bass.ds(g * P, P)]
                pe.matmul(ps[:, 6, :], sel,
                          wp12[:, h * HALF:(h + 1) * HALF], start=True, stop=False)
                pe.matmul(ps[:, 6, :], sel,
                          wp3[:, h * HALF:(h + 1) * HALF], start=False, stop=True).then_inc(g_w, 1)

            def down1(q, h, n):
                pe.wait_ge(g_h, n + 1)
                for t in range(4):
                    j = 4 * h + t
                    ins = pe.matmul(ps[:, j // 2, (j % 2) * C:(j % 2 + 1) * C], hT[:, h, t * P:(t + 1) * P],
                                    g1w[:, q, 4 * P:4 * P + C], start=False, stop=True, skip_group_check=True)
                ins.then_inc(g_dn, 1)

            def ffn1():
                pe.wait_ge(dve_s.sem, DVE["wparts1"])
                with pe.Fori(0, NG // GR) as i:
                    for q in range(GR):
                        pe.wait_ge(s_g1[q], i * 16 + 16)
                        for h in range(2):
                            n = (i * GR + q) * 2 + h
                            up1(q, h, i * GR + q, n + 1)
                            down1(q, h, n + 1)
                pe.wait_ge(g_dn, 2 * NG)
                mark(pe.matmul(ps[0:1, 4, 0:1], ident[:, 0:1], ident[:, 0:1], start=True, stop=True), "ffn1")

            for k in range(NL):
                prep(k)
            pe.sem_inc(y_done, RING)
            mixer(0)
            mixer(1)
            transpose_in(0)
            logits(0, gate0, E0)
            ffn0()
            transpose_in(1)
            logits(1, gate1, E1)
            pe.wait_ge(dve_s.sem, DVE["sel1"])
            for j in range(TT):
                for i in range(j + 1):
                    ins = pe.matmul(ps[:, 5, j * E1:(j + 1) * E1], tri[:, 0 if i == j else 1, :], maskb[:, i, :],
                                    start=(i == 0), stop=(i == j))
            mark(ins, "pos1")
            pe.wait_ge(dve_s.sem, DVE["route1"])
            for j in range(TT):
                ins = pe.transpose(ps[:, 6 + j // 4, (j % 4) * P:(j % 4 + 1) * P],
                                   w2x[:, j, :, :].rearrange("p a e -> p (a e)"), ident[:, :])
            mark(ins, "wT1")
            shared1()
            ffn1()

        @block.scalar
        def _(act):
            def mark(ins, name):
                assert AC[name] == act_s.n + 1, name
                act_s.mark(ins)

            def prep(k):
                act.wait_ge(dve_s.sem, DVE[f"conv{k}"])
                act.activation(t1[:, :, :], t0[:, :, :], ACT.Tanh, scale=0.5)
                ins = act.activation(u[k][:, :, :], t0[:, :, :], ACT.Copy, scale=0.5)
                mark(ins, f"th_u{k}")
                mark(act.activation(rsum[:, 0:1], rstd_zero, ACT.Copy), f"hf_u{k}")
                act.wait_ge(pe_s.sem, PE[f"xdbl{k}"])
                mark(act.activation(dtlo[:, :].rearrange("p (h t) -> p h t", h=2), ps[0:DR, 4:6, :], ACT.Copy), f"dtlo{k}")
                act.wait_ge(dve_s.sem, DVE[f"v{k}"])
                mark(act.activation(t1[:, :, :], delta[k][:, :, :], ACT.Abs), f"abs{k}")
                act.wait_ge(act_s.sem, AC[f"abs{k}"])
                mark(act.activation(t0[:, :, :], t1[:, :, :], ACT.Exp, scale=-1.0), f"e{k}")
                act.wait_ge(act_s.sem, AC[f"e{k}"])
                act.wait_ge(dve_s.sem, DVE[f"w{k}"])
                mark(act.activation(t1[:, :, :], t0[:, :, :], ACT.Ln, bias=1.0), f"ln{k}")

            rstd_zero = par[:, 0, 0, 0:1]

            def mixer(k):
                for h in range(2):
                    base = k * STEPS + h * NS
                    with act.Fori(0, NS // RING) as j:
                        for q in range(RING):
                            n = j * RING + q
                            S = n + base
                            act.wait_ge(scan_done, S + 1)
                            for d in range(ND):
                                ins = act.activation(
                                    dA[:, q, d, :].rearrange("p (b l) -> p b l", b=2)[:, :, 1:L],
                                    delta[k][:, d, h * HALF:(h + 1) * HALF].rearrange("p (b l) -> p b l", b=2)[:, :, 1:L],
                                    ACT.Exp, scale=negA[:, k, d, bass.ds(n, 1)])
                            ins.then_inc(da_ready, 1)
                            act.wait_ge(c_ready, S + 1)
                            act.wait_ge(hc_done, S + 1)
                            act.activation(Csb[:, q, :], ps[:, 6 + q, :], ACT.Copy).then_inc(csb_ready, 1)

            def gate_in(k):
                act.wait_ge(dve_s.sem, DVE[f"zh{k}"])
                mark(act.activation(t1[:, :, :], t0[:, :, :], ACT.Tanh), f"zth{k}")

            act.wait_ge(s_in[1], 48)
            ins = act.activation(negA[:, :, :, :], alog[:, :, :, :], ACT.Exp)
            mark(ins, "negA")
            prep(0)
            prep(1)
            gate_in(0)
            act.sem_inc(csb_ready, RING)
            act.wait_ge(dve_s.sem, DVE["consts"])
            act.wait_ge(pool_s.sem, POOL["zero"])
            mixer(0)
            mixer(1)
            act.wait_ge(pe_s.sem, PE["y_all1"])
            for h in range(2):
                ins = act.activation(y1[:, :, h * HALF:(h + 1) * HALF], ps[:, 2 * h:2 * h + 2, :], ACT.Copy)
            mark(ins, "y1copy")

            def route_exp(k, E):
                act.wait_ge(dve_s.sem, DVE[f"lsub{k}"])
                mark(act.activation(r0[:, :, 0:E], r1[:, :, 0:E], ACT.Exp), f"ex{k}")

            route_exp(0, E0)

            def ffn0_half(b, n, first):
                act.wait_ge(f_up, n + 1)
                if not first:
                    act.wait_ge(f_p, n)
                act.activation(th[:, b, 0:H0], ps[:, 1, 0:H0], ACT.Tanh, scale=0.5).then_inc(f_th, 1)
                act.wait_ge(f_T, n + 1)
                act.activation(hT[0:HP, b, :], ps[0:HP, 2, :], ACT.Copy).then_inc(f_hT, 1)

            for j in range(2):
                ffn0_half(j % 2, j, j == 0)
            with act.Fori(1, E0 * TT // 2) as i:
                for q in range(2):
                    ffn0_half(q, i * 2 + q, False)

            gate_in(1)
            route_exp(1, E1)
            for h in range(2):
                act.wait_ge(pe_s.sem, PE[f"sh_up{h}"])
                mark(act.activation(th[P // 2:P, h, :], ps[P // 2:P, 4, :], ACT.Tanh, scale=0.5), f"sh_th{h}")
            with act.Fori(0, NG) as i:
                for h in range(2):
                    n = i * 2 + h
                    act.wait_ge(g_g, n + 1)
                    act.wait_ge(g_p, n + 1)
                    act.activation(th[:, h, :], ps[:, 4, :], ACT.Tanh, scale=0.5).then_inc(g_th, 1)

        @block.gpsimd
        def _(pool):
            for q in range(RING):
                for d in range(ND):
                    ins = pool.memset(dA[:, q, d, :].rearrange("p (b l) -> p b l", b=2)[:, :, 0:1], 0.0)
            pool.memset(expo[:, :], -0.5)
            pool.memset(first[:, :, :], 1.0).then_inc(pool_s.sem, 1)
            pool_s.n += 1
            pool.sem_inc(hc_done, RING)

            def rstd_of(k, pre):
                pool.wait_ge(dve_s.sem, DVE[f"{pre}stat{k}"])
                pool.tensor_tensor(rstd[:, :], mv[:, :, 1], expo[:, :], ALU.pow).then_inc(pool_s.sem, 1)

            rstd_of(0, "z")
            with pool.Fori(0, NL * STEPS // RING) as i:
                for q in range(RING):
                    S = i * RING + q
                    pool.wait_ge(scan_done, S + RING + 1)
                    pool.wait_ge(csb_ready, S + RING + 1)
                    pool.wait_ge(y_done, S + 1)
                    pool.tensor_tensor(hC[:, q, :, :], hs[:, q, :, :],
                                       Csb[:, q, :].unsqueeze(1).to_broadcast([P, ND, HALF]), ALU.mult).then_inc(hc_done, 1)
            rstd_of(0, "n")
            rstd_of(1, "z")
            rstd_of(1, "n")

        @block.vector
        def _(dve):
            dch = Stage(sem("dch"))

            def link(ins):
                dch.mark(ins)
                dve.wait_ge(dch.sem, dch.n)

            def mark(ins, name, wait=False):
                assert DVE[name] == dve_s.n + 1, name
                dve_s.mark(ins)
                if wait:
                    dve.wait_ge(dve_s.sem, dve_s.n)

            def prep(k):
                dve.wait_ge(pe_s.sem, PE[f"xin{k}"])
                if k == 1:
                    dve.wait_ge(act_s.sem, AC["ln0"])
                for d in range(ND):
                    src = ps[:, 2 * d:2 * d + 2, :].rearrange("p h (b l) -> p (h b) l", b=2)
                    dst = t0[:, d, :].rearrange("p (b l) -> p b l", b=B)
                    link(dve.tensor_scalar(dst, src, par[:, k, d, 3:4], par[:, k, d, 4:5], ALU.mult, ALU.add))
                    for s in range(1, 4):
                        ins = dve.scalar_tensor_tensor(dst[:, :, s:L], src[:, :, 0:L - s], par[:, k, d, 3 - s:4 - s],
                                                       dst[:, :, s:L], ALU.mult, ALU.add)
                        if s < 3 or d == 0:
                            link(ins)
                mark(ins, f"conv{k}")
                dve.wait_ge(act_s.sem, AC[f"th_u{k}"])
                mark(dve.scalar_tensor_tensor(u[k][:, :, :].rearrange("p a b -> p (a b)"), t1[:, :, :].rearrange("p a b -> p (a b)"), 1.0,
                                              u[k][:, :, :].rearrange("p a b -> p (a b)"), ALU.add, ALU.mult), f"u{k}", True)
                dve.wait_ge(pe_s.sem, PE[f"xdbl{k}"])
                x2 = ps[:, 4:6, :]
                p3 = bc3[k][:, :].rearrange("p (h t) -> p h t", h=2)
                r = t0[:, 0, :].rearrange("p (h t) -> p h t", h=2)
                dve.wait_ge(act_s.sem, AC[f"dtlo{k}"])
                link(dve.tensor_copy(p3, x2))
                link(dve.tensor_tensor(r[64:P], x2[64:P], p3[64:P], ALU.subtract))
                link(dve.tensor_copy(p3[64:P], r[64:P]))
                mark(dve.tensor_tensor(p3[96:P], r[96:P], p3[96:P], ALU.subtract), f"bc{k}")
                dve.wait_ge(pe_s.sem, PE[f"dtp{k}"])
                for d in range(ND):
                    ins = dve.tensor_scalar(delta[k][:, d, :], ps[:, 2 * d:2 * d + 2, :].rearrange("p h t -> p (h t)"),
                                            par[:, k, d, 5:6], None, ALU.add)
                mark(ins, f"v{k}")
                dve.wait_ge(act_s.sem, AC[f"e{k}"])
                e2 = t0[:, :, :].rearrange("p a b -> p (a b)")
                w2 = du[k][:, :, :].rearrange("p a b -> p (a b)")
                d2 = delta[k][:, :, :].rearrange("p a b -> p (a b)")
                l2 = t1[:, :, :].rearrange("p a b -> p (a b)")
                link(dve.tensor_scalar(w2, e2, 1.0, None, ALU.add))
                mark(dve.scalar_tensor_tensor(w2, w2, 1.0, e2, ALU.subtract, ALU.subtract), f"w{k}", True)
                dve.wait_ge(act_s.sem, AC[f"ln{k}"])
                link(dve.tensor_tensor(l2, l2, w2, ALU.subtract))
                mark(dve.scalar_tensor_tensor(d2, d2, 0.0, l2, ALU.max, ALU.add), f"delta{k}", True)
                mark(dve.tensor_tensor(w2, d2, u[k][:, :, :].rearrange("p a b -> p (a b)"), ALU.mult), f"du{k}")

            dve.wait_ge(s_in[0], 48)
            prep(0)
            prep(1)
            dve.wait_ge(s_in[2], 32)
            for k in range(NL):
                for d in range(ND):
                    dve.tensor_scalar(diagD[:, k, d, :], ident[:, :], par[:, k, d, 6:7], None, ALU.mult)
            dve.wait_ge(act_s.sem, AC["negA"])
            dve.wait_ge(pool_s.sem, POOL["zero"])
            dve.memset(first[:, :, 0:1], 0.0)
            mark(dve.tensor_scalar(negA[:, :, :, :], negA[:, :, :, :], -1.0, None, ALU.mult), "consts", True)
            dve.sem_inc(dbu_done, RING)
            dve.sem_inc(scan_done, RING)

            def mixer(k):
                for h in range(2):
                    base = k * STEPS + h * NS
                    with dve.Fori(0, NS // RING) as j:
                        for q in range(RING):
                            S = j * RING + q + base
                            dve.wait_ge(b_ready, S + 1)
                            dve.tensor_tensor(dBu[:, q, :, :], du[k][:, :, h * HALF:(h + 1) * HALF],
                                              ps[:, 4 + q, :].unsqueeze(1).to_broadcast([P, ND, HALF]), ALU.mult).then_inc(dbu_done, 1)
                            dve.wait_ge(da_ready, S + 1)
                            dve.wait_ge(dbu_done, S + RING + 1)
                            dve.wait_ge(hc_done, S + 1)
                            dve.tensor_tensor_scan(hs[:, q, :, :].rearrange("p a b -> p (a b)"),
                                                   dA[:, q, :, :].rearrange("p a b -> p (a b)"),
                                                   dBu[:, q, :, :].rearrange("p a b -> p (a b)"),
                                                   0.0, ALU.mult, ALU.add).then_inc(scan_done, 1)

            def norm_stats(name):
                for j in range(TT):
                    ins = dve.bn_stats(stats[:, j, :], xs[:, j, :])
                link(ins)
                for j in range(TT):
                    ins = dve.bn_aggr(mv[:, j, :], stats[:, j, :])
                link(ins)
                mark(dve.tensor_scalar(mv[:, :, 1], mv[:, :, 1], EPS, None, ALU.add), name)

            def gate_in(k):
                if k == 0:
                    dve.wait_ge(s_in[3], 16)
                norm_stats(f"zstat{k}")
                dve.wait_ge(pool_s.sem, POOL[f"zr{k}"])
                link(dve.tensor_scalar(rstd[:, :], rstd[:, :], 0.5, None, ALU.mult))
                for j in range(TT):
                    ins = dve.tensor_scalar(t0[:, j % 2, (j // 2) * L:(j // 2 + 1) * L], xs[:, j, :], mv[:, j, 0:1],
                                            rstd[:, j:j + 1], ALU.subtract, ALU.mult)
                mark(ins, f"zh{k}", True)
                dve.wait_ge(act_s.sem, AC[f"zth{k}"])
                z = t0[:, :, :].rearrange("p a b -> p (a b)")
                g = t1[:, :, :].rearrange("p a b -> p (a b)")
                mark(dve.scalar_tensor_tensor(g, g, 1.0, z, ALU.add, ALU.mult), f"G{k}", True)

            def mixer_out(k):
                if k == 0:
                    dve.wait_ge(pe_s.sem, PE["y_all0"])
                else:
                    dve.wait_ge(act_s.sem, AC["y1copy"])
                for h in range(2):
                    t = slice(h * HALF, (h + 1) * HALF)
                    y = ps[:, 2 * h:2 * h + 2, :] if k == 0 else y1[:, :, t]
                    ins = dve.tensor_tensor(t0[:, :, t], y, t1[:, :, t], ALU.mult)
                mark(ins, f"yz{k}")

            def norm_out(k):
                dve.wait_ge(pe_s.sem, PE[f"yT{k}"])
                xf = xs[:, :, :].rearrange("p j c -> p (j c)")
                mark(dve.tensor_tensor(xf, xf, ps[:, 4:8, :].rearrange("p h t -> p (h t)"), ALU.add), f"xnew{k}", True)
                norm_stats(f"nstat{k}")
                dve.wait_ge(pool_s.sem, POOL[f"nr{k}"])
                tf = t1[:, :, :].rearrange("p a b -> p (a b)")
                for j in range(TT):
                    ins = dve.tensor_scalar(tf[:, j * C:(j + 1) * C], xs[:, j, :], mv[:, j, 0:1],
                                            rstd[:, j:j + 1], ALU.subtract, ALU.mult)
                mark(ins, f"xn{k}")
                dve.wait_ge(pe_s.sem, PE[f"xnT{k}"])
                mark(dve.tensor_copy(xnT[:, :, :].rearrange("p c t -> p (c t)"), ps[:, 0:4, :].rearrange("p h t -> p (h t)")), f"xnT{k}")

            def pick(score, E, top):
                for j in range(TT):
                    ins = dve.max(top8[:, j, :], score[:, j, :])
                link(ins)
                kth = top8[:, :, top - 1:top].to_broadcast([P, TT, E])
                gt, eq, cum = r2[:, :, 0:E], r1[:, :, 0:E], r0[:, :, 0:E]
                dve.tensor_tensor(gt, score, kth, ALU.is_gt)
                link(dve.tensor_tensor(eq, score, kth, ALU.is_equal))
                link(dve.tensor_reduce(need[:, :], gt, AX_X, ALU.add))
                link(dve.tensor_scalar(need[:, :], need[:, :], -1.0, float(top), ALU.mult, ALU.add))
                for j in range(TT):
                    ins = dve.tensor_tensor_scan(cum[:, j, :], first[:, j, 0:E], eq[:, j, :], 0.0, ALU.mult, ALU.add)
                link(ins)
                link(dve.tensor_tensor(cum, cum, need[:, :].unsqueeze(2).to_broadcast([P, TT, E]), ALU.is_le))
                link(dve.tensor_tensor(eq, eq, cum, ALU.mult))
                link(dve.tensor_tensor(gt, gt, eq, ALU.add))

            gate_in(0)
            mixer(0)
            mixer_out(0)
            mixer(1)
            norm_out(0)
            dve.wait_ge(pe_s.sem, PE["logit0"])
            l0 = lg[:, :, 0:E0]
            link(dve.tensor_copy(l0, ps[:, 4, 0:TT * E0].rearrange("p (j e) -> p j e", j=TT)))
            pick(l0, E0, TOPK0)
            mark(dve.tensor_tensor(r1[:, :, 0:E0], l0, top8[:, :, 0:1].to_broadcast([P, TT, E0]), ALU.subtract), "lsub0")
            dve.wait_ge(act_s.sem, AC["ex0"])
            link(dve.tensor_tensor(w0[:, :, :], r0[:, :, 0:E0], r2[:, :, 0:E0], ALU.mult))
            link(dve.tensor_reduce(need[:, :], w0[:, :, :], AX_X, ALU.add))
            link(dve.reciprocal(need[:, :], need[:, :]))
            mark(dve.tensor_tensor(w0[:, :, :], w0[:, :, :], need[:, :].unsqueeze(2).to_broadcast([P, TT, E0]), ALU.mult), "route0", True)

            def ffn0_block(b, j, e, n, first):
                dve.wait_ge(f_th, n + 1)
                if not first:
                    dve.wait_ge(f_T, n)
                dve.scalar_tensor_tensor(pg[:, b, 0:H0], th[:, b, 0:H0], 1.0, ps[:, 1, 0:H0], ALU.add, ALU.mult).then_inc(f_p, 1)
                dve.wait_ge(f_p, n + 1)
                dve.scalar_tensor_tensor(hx[:, b, 0:H0], pg[:, b, 0:H0], 0.5, ps[:, 0, 0:H0], ALU.mult, ALU.mult).then_inc(f_h, 1)
                dve.wait_ge(f_dn, n + 1)
                dve.scalar_tensor_tensor(xs[:, j, :], ps[:, 3, 0:C], w0[:, j, bass.ds(e, 1)], xs[:, j, :],
                                         ALU.mult, ALU.add).then_inc(f_acc, 1)

            def expert(e, n0, first):
                for j in range(TT):
                    n = n0 + j
                    b = j % 2
                    dve.wait_ge(f_th, n + 1)
                    if not (first and j == 0):
                        dve.wait_ge(f_T, n)
                    dve.scalar_tensor_tensor(pg[:, b, 0:H0], th[:, b, 0:H0], 1.0, ps[:, 1, 0:H0], ALU.add, ALU.mult).then_inc(f_p, 1)
                    dve.wait_ge(f_p, n + 1)
                    dve.scalar_tensor_tensor(hx[:, b, 0:H0], pg[:, b, 0:H0], 0.5, ps[:, 0, 0:H0], ALU.mult, ALU.mult).then_inc(f_h, 1)
                    if j > 0:
                        acc(j - 1, e, n - 1, first)
                acc(TT - 1, e, n0 + TT - 1, first)

            def acc(j, e, n, first):
                dve.wait_ge(f_dn, n + 1)
                if not first:
                    dve.wait_ge(f_acc, n - TT + 1)
                dve.scalar_tensor_tensor(xs[:, j, :], ps[:, 3, 0:C], w0[:, j, bass.ds(e, 1)], xs[:, j, :],
                                         ALU.mult, ALU.add).then_inc(f_acc, 1)

            expert(0, 0, True)
            with dve.Fori(1, E0) as e:
                expert(e, e * TT, False)
            dve.wait_ge(f_acc, E0 * TT)
            mark(dve.tensor_copy(need[:, :], need[:, :]), "ffn0", True)

            gate_in(1)
            mixer_out(1)
            norm_out(1)
            dve.wait_ge(pe_s.sem, PE["logit1"])
            mark(dve.tensor_scalar(r1[:, :, :], ps[:, 4, :].rearrange("p (j e) -> p j e", j=TT), -1.0, None, ALU.mult), "lsub1")
            dve.wait_ge(act_s.sem, AC["ex1"])
            link(dve.tensor_scalar(r0[:, :, :], r0[:, :, :], 1.0, None, ALU.add))
            link(dve.reciprocal(lg[:, :, :], r0[:, :, :]))
            pick(lg[:, :, :], E1, TOPK1)
            mark(dve.tensor_copy(maskb[:, :, :], r2[:, :, :]), "sel1")
            link(dve.tensor_tensor(r0[:, :, :], lg[:, :, :], r2[:, :, :], ALU.mult))
            link(dve.tensor_reduce(need[:, :], r0[:, :, :], AX_X, ALU.add))
            link(dve.reciprocal(need[:, :], need[:, :]))
            link(dve.tensor_tensor(r0[:, :, :], r0[:, :, :], need[:, :].unsqueeze(2).to_broadcast([P, TT, E1]), ALU.mult))
            dve.wait_ge(pe_s.sem, PE["pos1"])
            link(dve.tensor_scalar(r1[:, :, :], ps[:, 5, :].rearrange("p (j e) -> p j e", j=TT), float(CAP), None, ALU.is_lt))
            for a in range(2):
                ins = dve.tensor_tensor(w2x[:, :, a, :], r0[:, :, :], r1[:, :, :], ALU.mult)
            mark(ins, "route1", True)
            dve.wait_ge(pe_s.sem, PE["wT1"])
            wt = ps[:, 6:8, :].rearrange("p h t -> p (h t)")
            link(dve.tensor_copy(wp12[:, :], wt))
            link(dve.tensor_tensor(wtmp[:, :], wt, wp12[:, :], ALU.subtract))
            dve.tensor_copy(wp12[64:P, :], wtmp[64:P, :])
            link(dve.tensor_copy(wmid[:, :], wtmp[0:E1, :]))
            dve.memset(wp3[E1:P, :], 0.0)
            mark(dve.tensor_tensor(wp3[0:E1, :], wtmp[0:E1, :], wmid[:, :], ALU.subtract), "wparts1", True)
            for h in range(2):
                dve.wait_ge(act_s.sem, AC[f"sh_th{h}"])
                link(dve.scalar_tensor_tensor(pg[P // 2:P, h, :], th[P // 2:P, h, :], 1.0, ps[P // 2:P, 4, :], ALU.add, ALU.mult))
                mark(dve.scalar_tensor_tensor(hT[0:P // 2, h, :], pg[P // 2:P, h, :], 0.5, ps[0:P // 2, 4, :], ALU.mult, ALU.mult), f"sh_h{h}", True)
            dve.wait_ge(pe_s.sem, PE["sh_dn1"])
            for s in (g_p, g_q, g_h):
                dve.sem_inc(s, 1)
            with dve.Fori(0, NG) as i:
                for h in range(2):
                    n = i * 2 + h
                    dve.wait_ge(g_th, n + 1)
                    dve.scalar_tensor_tensor(pg[:, h, :], th[:, h, :], 1.0, ps[:, 4, :], ALU.add, ALU.mult).then_inc(g_p, 1)
                    dve.wait_ge(g_v, n + 1)
                    dve.wait_ge(g_p, n + 2)
                    dve.scalar_tensor_tensor(hx[:, h, :], pg[:, h, :], 0.5, ps[:, 5, :], ALU.mult, ALU.mult).then_inc(g_q, 1)
                    dve.wait_ge(g_w, n + 1)
                    dve.wait_ge(g_q, n + 2)
                    dve.tensor_tensor(hT[:, h, :], hx[:, h, :], ps[:, 6, :], ALU.mult).then_inc(g_h, 1)
            dve.wait_ge(pe_s.sem, PE["ffn1"])
            xf = xs[:, :, :].rearrange("p j c -> p (j c)")
            mark(dve.tensor_tensor(xf, xf, ps[:, 0:4, :].rearrange("p h t -> p (h t)"), ALU.add), "out")


def lay_out(inp):
    import numpy as np

    g = {k: np.asarray(v) for k, v in inp.items()}
    f = np.float32
    P = 128
    x = g["x"]
    B, L, C = x.shape
    ctxt = g["ctx_1024"].reshape(B * L, -1).T
    par = np.zeros((P, 2, 2, 24), f)
    xpr = np.zeros((P, 2, 2, P), f)
    inpT, dtT = [], []
    for k in range(2):
        p = f"L{k}_xattn_"
        di = g[p + "in_proj_w"].shape[0]
        inpT.append(g[p + "in_proj_w"].T)
        dtT.append(g[p + "dt_proj_w"].T)
        cw = g[p + "conv_w"].reshape(di, 4)
        for d in range(2):
            r = slice(d * P, (d + 1) * P)
            par[:, k, d, 0:4] = cw[r]
            par[:, k, d, 4] = g[p + "conv_b"][r]
            par[:, k, d, 5] = g[p + "dt_proj_b"][r]
            par[:, k, d, 6] = g[p + "D"][r]
            par[:, k, d, 8:24] = g[p + "A_log"][r]
            xw = g[p + "x_proj_w"][:, r].T
            xpr[:, k, d, 0:8] = xw[:, 0:8]
            for c in range(3):
                xpr[:, k, d, 32 + 32 * c:64 + 32 * c] = xw[:, 8:40]
    up, gt, dn = g["L0_ffn_W_up"], g["L0_ffn_W_gate"], g["L0_ffn_W_down"]
    E, H, _ = up.shape
    ug = np.concatenate([up, gt], axis=1).transpose(0, 2, 1).reshape(E, 2, P, 2 * H).transpose(0, 2, 1, 3)
    dT = dn.transpose(0, 2, 1).reshape(E, 4, H // 4, C).transpose(0, 2, 1, 3)
    gate0 = g["L0_ffn_gate_inp"].T.reshape(2, P, E).transpose(1, 0, 2)
    gate1 = g["L1_ffn_w_gate"].reshape(2, P, -1).transpose(1, 0, 2)
    shu = g["L1_ffn_w_shared_up"].reshape(2, P, P).transpose(1, 0, 2)
    wu, wd = g["L1_ffn_w_up"], g["L1_ffn_w_down"]
    E1, _, H2 = wu.shape
    H1 = H2 // 2
    EG = P // H1
    NG = E1 // EG
    w = wu.reshape(NG, EG, 2, P, 2, H1).transpose(0, 3, 2, 4, 1, 5).reshape(NG, P, 4 * P)
    grp = np.concatenate([w, wd.reshape(NG, P, C)], axis=2)
    sel3 = np.zeros((P, 32), f)
    for c in range(1, 4):
        sel3[32 * c:32 * c + 32] = np.eye(32)
    tri = np.zeros((P, 2, P), f)
    tri[:, 0] = np.triu(np.ones((P, P)), 1)
    tri[:, 1] = 1
    sel64 = np.repeat(np.concatenate([np.eye(E1), np.eye(E1)]), P // EG, axis=1).astype(f)
    bf = mybir.dt.np(mybir.dt.bfloat16)
    return {
        "x": x.reshape(B * L, C), "ctxT": ctxt, "in_projT": np.stack(inpT), "ssm_par": par, "x_projT": xpr,
        "dt_projT": np.stack(dtT), "gate0T": gate0, "up0T": ug, "down0T": dT, "gate1T": gate1, "sh_upT": shu,
        "sh_down": g["L1_ffn_w_shared_down"], "grp1": grp, "ident": np.eye(P, dtype=f),
        "sel3": sel3.astype(bf), "tri": tri.astype(bf), "sel64": sel64.astype(bf),
    }


def kernel(**inputs):
    import numpy as np
    import concourse.bacc as bacc
    from concourse.bass_utils import run_bass_kernel_spmd

    nc = bacc.Bacc("TRN2", target_bir_lowering=False, num_devices=1)
    arrays, args = {}, []
    for name, a in lay_out(inputs).items():
        a = np.ascontiguousarray(a)
        arrays[f"in_{name}"] = a
        args.append(nc.dram_tensor(f"in_{name}", a.shape, mybir.dt.from_np(a.dtype), kind="ExternalInput").ap())
    shape = inputs["x"].shape
    out = nc.dram_tensor("out_0", (shape[0] * shape[1], shape[2]), F32, kind="ExternalOutput").ap()
    build(nc, *args, out)
    r = run_bass_kernel_spmd(nc, [arrays], core_ids=[0])
    return r.results[0]["out_0"].reshape(shape)
```

```python
from contextlib import ExitStack

import concourse.bass as bass
from concourse import mybir

ALU = mybir.AluOpType
ACT = mybir.ActivationFunctionType
F32 = mybir.dt.float32
F32R = mybir.dt.float32r
BF16 = mybir.dt.bfloat16
AX_X = mybir.AxisListType.X

P = 128
BANK = 512


class Stage:

    def __init__(self, sem):
        self.sem, self.n = sem, 0

    def mark(self, ins, by=1):
        ins.then_inc(self.sem, by)
        self.n += by
        return self.n


def build(nc, x, ctxT, in_projT, ssm_par, x_projT, dt_projT, gate0T, up0T, down0T,
          gate1T, sh_upT, sh_down, grp1, ident_in, sel3_in, tri_in, sel64_in, steps_in, out):
    NL = 2
    B, L = 4, 256
    TOK = B * L
    TT = TOK // P
    C = x.shape[1]
    KC = C // P
    DI = in_projT.shape[2]
    ND = DI // P
    NS = 16
    DR = dt_projT.shape[1]
    HALF = TOK // 2
    E0 = up0T.shape[0]
    H0 = down0T.shape[1] * down0T.shape[2]
    HP = down0T.shape[1]
    HK = down0T.shape[2]
    TOPK0 = 4
    E1 = gate1T.shape[2]
    NG = grp1.shape[0]
    TOPK1 = 6
    CAP = 128
    EPS = 1e-5
    RING = 2
    STEPS = 2 * NS
    NB = (TOPK0 * TOK + E0 * (P - 1)) // P
    WR = 3
    BODY = 6
    BSTEP = 4

    with ExitStack() as ctx:
        def sb(name, shape, dt=F32):
            return ctx.enter_context(nc.sbuf_tensor(name, shape, dt))

        def sem(name):
            return ctx.enter_context(nc.semaphore(name))

        ps = ctx.enter_context(nc.psum_tensor("ps", [P, 8, BANK], F32))

        ident = sb("ident", [P, P])
        sel3 = sb("sel3", [P, 2 * NS], BF16)
        tri = sb("tri", [P, 2, P], BF16)
        sel64 = sb("sel64", [P, NG * P], BF16)
        xs = sb("xs", [P, TT, C])
        ctx_sb = sb("ctx_sb", [P, TOK])
        inp = sb("inp", [P, NL, DI])
        par = sb("par", [P, NL, ND, 8])
        alog = sb("alog", [P, NL, ND, NS])
        xpr = sb("xpr", [P, NL, ND, P])
        dtp_w = sb("dtp_w", [DR, NL, DI])
        gate0 = sb("gate0", [P, KC, E0])
        gate1 = sb("gate1", [P, KC, E1])
        shu = sb("shu", [P, KC, P])
        shd = sb("shd", [P // 2, C])

        delta = sb("delta", [P, ND, TOK])
        bc3 = sb("bc3", [P, TOK], BF16)
        negA = sb("negA", [P, NL, ND, NS])
        diagD = sb("diagD", [P, ND, P])
        dtlo = sb("dtlo", [DR, TOK])
        t0 = sb("t0", [P, ND, TOK])
        t1 = sb("t1", [P, ND, TOK])
        dA = sb("dA", [P, RING, ND, HALF])
        dBu = sb("dBu", [P, RING, ND, HALF])
        hs = sb("hs", [P, RING, ND, HALF])
        hC = sb("hC", [P, RING, ND, HALF])
        xn_rows = hs[:, :, :, :].rearrange("p r d t -> p (r d t)").rearrange("p (j c) -> p j c", c=C)
        Csb = sb("Csb", [P, RING, HALF])
        Bsb = sb("Bsb", [P, RING, HALF])
        y1 = sb("y1", [P, ND, TOK])

        stats = sb("stats", [P, TT, 6])
        mv = sb("mv", [P, TT, 2])
        rstd = sb("rstd", [P, TT])
        expo = sb("expo", [P, TT])
        xnT = sb("xnT", [P, KC, TOK])
        lg = sb("lg", [P, TT, E1])
        top8 = sb("top8", [P, TT, 8])
        r0 = sb("r0", [P, TT, E1])
        r1 = sb("r1", [P, TT, E1])
        r2 = sb("r2", [P, TT, E1])
        rsum = sb("rsum", [P, TT])
        need = sb("need", [P, TT])
        first1 = sb("first1", [P, TT, E1])
        first0 = sb("first0", [P, TT, E0])
        maskb = sb("maskb", [P, TT, E1], BF16)
        w2x = dBu[:, 0, :, :].rearrange("p d (j a e) -> p (d j) a e", a=2, e=E1)
        wp12 = sb("wp12", [P, TOK], BF16)
        wp3 = sb("wp3", [P, TOK], BF16)
        wtmp, wmid = y1[:, 0, :], y1[0:E1, 1, :].bitcast(BF16)[:, 0:TOK]

        th, pg, hx, hT = (sb(n, [P, RING, BANK]) for n in ("th", "pg", "hx", "hT"))
        xd_sb = sb("xd_sb", [P, 3, C])
        xdT = sb("xdT", [P, RING, KC, P])
        ysb = sb("ysb", [P, RING, C])
        steps = sb("steps", [P, 96])
        slot_f = sb("slot_f", [P, TOPK0, TT])
        slot_u = sb("slot_u", [P, TOPK0, TT], mybir.dt.uint32)
        wk = sb("wk", [P, TOPK0, TT])
        nblk = sb("nblk", [P, E0])
        endb = sb("endb", [P, E0])
        startb = sb("startb", [P, E0])
        big = dBu[:, :, :, :].rearrange("p r d t -> p (r d t)")
        blk_f = sb("blk_f", [P, 3, 64])
        I32 = mybir.dt.int32
        blk_need = sb("blk_need", [1, 64], I32)
        blk_ring = sb("blk_ring", [1, 64], I32)
        end_i = sb("end_i", [1, E0], I32)
        zero = ysb[:, 0, :]
        gb = delta[:, :, :].rearrange("p d (r c) -> p (d r) c", c=C)
        xd = nc.dram_tensor("xd", ((NB + 1) * P, C), F32, kind="Internal").ap()
        yd = nc.dram_tensor("yd", (NB * P, C), F32, kind="Internal").ap()
        GR = 4
        GN = grp1.shape[2]
        with (nc.sbuf_tensor("ug0", [P, WR, KC, 2 * H0], F32) as ug0, nc.sbuf_tensor("dn0", [HP, WR, HK, C], F32) as dn0,
              nc.sbuf_tensor("u", [P, ND, TOK], F32) as u, nc.sbuf_tensor("du", [P, ND, TOK], F32) as du):
            pass
        g1w = sb("g1w", [P, GR, GN])
        w_hi, w_lo = sb("w_hi", [P, RING, GN], F32R), sb("w_lo", [P, RING, GN], F32R)
        x_hi, x_lo = sb("x_hi", [P, KC, TOK], F32R), sb("x_lo", [P, KC, TOK], F32R)
        h_hi, h_lo = sb("h_hi", [P, RING, BANK], F32R), sb("h_lo", [P, RING, BANK], F32R)

        s_in = [sem(f"s_in{i}") for i in range(6)]
        s_w = [sem(f"s_w{i}") for i in range(WR)]
        s_xd = [sem(f"s_xd{i}") for i in range(3)]
        s_y = [sem(f"s_y{i}") for i in range(RING)]
        s_gb = [sem(f"s_gb{i}") for i in range(8)]
        s_zero, s_scat = sem("s_zero"), sem("s_scat")
        s_g1 = [sem(f"s_g1{i}") for i in range(GR)]
        s_store = sem("s_store")
        pe_s, act_s, dve_s, pool_s = Stage(sem("pe_s")), Stage(sem("act_s")), Stage(sem("dve_s")), Stage(sem("pool_s"))
        b_ready, c_ready = sem("b_ready"), sem("c_ready")
        da_ready, csb_ready = sem("da_ready"), sem("csb_ready")
        dbu_done, scan_done = sem("dbu_done"), sem("scan_done")
        hc_done, y_done = sem("hc_done"), sem("y_done")
        bc_ps, bc_sb = sem("bc_ps"), sem("bc_sb")
        w_loaded = sem("w_loaded")
        x_turned, xdT_ready = sem("x_turned"), sem("xdT_ready")
        up_done, th_done, p_done, h_done = sem("up_done"), sem("th_done"), sem("p_done"), sem("h_done")
        h_turned, hT_ready, dn_done, y_evac = sem("h_turned"), sem("hT_ready"), sem("dn_done"), sem("y_evac")
        da1, dbu1, scan1, hc1, add1 = (sem(n) for n in ("da1", "dbu1", "scan1", "hc1", "add1"))
        s_comb = sem("s_comb")
        g_g, g_v, g_w, g_th, g_p, g_q, g_h, g_dn, g_hhi, g_hlo, g_whi, g_wlo = (sem(f"g_{n}") for n in
            ("g", "v", "w", "th", "p", "q", "h", "dn", "hhi", "hlo", "whi", "wlo"))

        block = ctx.enter_context(nc.Block())

        x_t = x.rearrange("(j p) c -> p j c", p=P)
        out_t = out.rearrange("(j p) c -> p j c", p=P)

        def places(*names):
            return {n: i + 1 for i, n in enumerate(" ".join(names).split())}

        PE = places("xin0 xdbl0 dtp0 y_init0 y_init1 y_all0 yT0 xnT0 logit0 xin1 pos0 xdbl1 dtp1",
                    "yT1 xnT1 logit1 pos1 wT1 sh_up0 sh_up1 sh_dn0 sh_dn1 ffn1")
        AC = places("negA th_u0 dtlo0 abs0 e0 ln0 zth0 ex0 th_u1 dtlo1 abs1 e1 ln1 y1init",
                    "zth1 xhi1 ex1 sh_th0 sh_th1")
        DVE = places("zero conv0 u0 bc0 v0 w0 delta0 du0 consts zstat0 zh0 G0 yz0 xnew0 nstat0 xn0 xnT0",
                     "lsub0 sel0 slots0 blocks0 route0 conv1 u1 bc1 v1 w1 delta1 du1 combined",
                     "zstat1 zh1 G1 yz1 xnew1 nstat1 xn1 xnT1 lsub1 xlo1 sel1 route1 wparts1 sh_h0 sh_h1 out")
        POOL = places("zero zr0 nr0 y1 zr1 nr1")

        def has(i, c):
            return not isinstance(i, int) or 0 <= BODY * i + c < NB

        def nth(i, c):
            return i * BODY + c

        def per(i, c, ring):
            return i * (BODY // ring) + c // ring

        BODIES = 2 * NS // BSTEP

        def bodies(eng, body):
            for h in range(2):
                first = h * BODIES // 2
                last = first + BODIES // 2 - h
                with eng.Fori(first, last) as i:
                    body(i, h, (i - first) * BSTEP)
                if h == 1:
                    body(BODIES - 1, h, NS - BSTEP)

        @block.sync
        def _(sp):
            sp.dma_start(ctx_sb[:, :], ctxT).then_inc(s_in[0], 16)
            sp.dma_start(inp[:, :, :], in_projT.rearrange("k p d -> p k d")).then_inc(s_in[0], 16)
            sp.dma_start(par[:, :, :, :], ssm_par[:, :, :, 0:8]).then_inc(s_in[0], 16)
            sp.dma_start(alog[:, :, :, :], ssm_par[:, :, :, 8:8 + NS]).then_inc(s_in[1], 16)
            sp.dma_start(xpr[:, :, :, :], x_projT).then_inc(s_in[1], 16)
            sp.dma_start(dtp_w[:, :, :], dt_projT.rearrange("k r d -> r k d")).then_inc(s_in[1], 16)
            sp.dma_start(ident[:, :], ident_in).then_inc(s_in[2], 16)
            sp.dma_start(sel3[:, :], sel3_in).then_inc(s_in[2], 16)
            sp.dma_start(xs[:, :, :], x_t).then_inc(s_in[3], 16)
            sp.dma_start(tri[:, :, :], tri_in).then_inc(s_in[4], 16)
            sp.dma_start(sel64[:, :], sel64_in).then_inc(s_in[4], 16)
            sp.dma_start(gate0[:, :, :], gate0T).then_inc(s_in[4], 16)
            sp.dma_start(gate1[:, :, :], gate1T).then_inc(s_in[4], 16)
            sp.dma_start(shu[:, :, :], sh_upT).then_inc(s_in[4], 16)
            sp.dma_start(shd[:, :], sh_down).then_inc(s_in[4], 16)
            sp.dma_start(steps[:, :], steps_in).then_inc(s_in[5], 16)
            sp.wait_ge(dve_s.sem, DVE["zero"])
            sp.dma_start(xd.rearrange("(b p) c -> p b c", p=P), zero[:, :].unsqueeze(1).to_broadcast([P, NB + 1, C])).then_inc(s_zero, 16)

            def load_expert(e, q):
                sp.dma_start(ug0[:, q, :, :], up0T[bass.ds(e, 1), :, :, :].rearrange("o p k n -> (o p) k n")).then_inc(s_w[q], 16)
                sp.dma_start(dn0[:, q, :, :], down0T[bass.ds(e, 1), :, :, :].rearrange("o p k n -> (o p) k n")).then_inc(s_w[q], 16)

            for q in range(WR):
                load_expert(q, q)
            for q in range(WR):
                sp.wait_ge(s_w[q], 32)
                sp.sem_inc(w_loaded, 1)
            sp.wait_ge(dve_s.sem, DVE["blocks0"])

            def next_expert(i, q):
                e = i * WR + q
                sp.wait_ge(dn_done, sp.value_load(end_i[0:1, bass.ds(e - WR, 1)], min_val=1, max_val=NB + 1))
                load_expert(e, q)
                sp.wait_ge(s_w[q], i * 32 + 32)
                sp.sem_inc(w_loaded, 1)

            with sp.Fori(1, E0 // WR) as i:
                for q in range(WR):
                    next_expert(i, q)
            for e in range(E0 // WR * WR, E0):
                next_expert(E0 // WR, e % WR)
            sp.wait_ge(dn_done, NB + 1)
            for q in range(GR):
                sp.dma_start(g1w[:, q, :], grp1[q]).then_inc(s_g1[q], 16)
            with sp.Fori(1, NG // GR) as i:
                for q in range(GR):
                    sp.wait_ge(g_wlo, i * GR + q - GR + 1)
                    sp.dma_start(g1w[:, q, :], grp1[bass.ds(i * GR + q, 1), :, :].rearrange("o p n -> (o p) n")).then_inc(s_g1[q], 16)
            sp.wait_ge(dve_s.sem, DVE["out"])
            sp.dma_start(out_t, xs[:, :, :]).then_inc(s_store, 16)
            sp.wait_ge(s_store, 16)

        @block.tensor
        def _(pe):
            def mark(ins, name):
                assert PE[name] == pe_s.n + 1, name
                pe_s.mark(ins)

            def project_in(k):
                for d in range(ND):
                    for h in range(2):
                        ins = pe.matmul(ps[:, 2 * d + h, :], inp[:, k, d * P:(d + 1) * P],
                                        ctx_sb[:, h * HALF:(h + 1) * HALF], start=True, stop=True)
                mark(ins, f"xin{k}")

            def prep(k):
                pe.wait_ge(dve_s.sem, DVE[f"u{k}"])
                for h in range(2):
                    for d in range(ND):
                        ins = pe.matmul(ps[:, 4 + h, :], xpr[:, k, d, :], u[:, d, h * HALF:(h + 1) * HALF],
                                        start=(d == 0), stop=(d == ND - 1))
                mark(ins, f"xdbl{k}")
                pe.wait_ge(act_s.sem, AC[f"dtlo{k}"])
                for d in range(ND):
                    for h in range(2):
                        ins = pe.matmul(ps[:, 2 * d + h, :], dtp_w[:, k, d * P:(d + 1) * P],
                                        dtlo[:, h * HALF:(h + 1) * HALF], start=True, stop=True)
                mark(ins, f"dtp{k}")

            def rep(h, n, q, S):
                rhs = bc3[:, h * HALF:(h + 1) * HALF]
                pe.wait_ge(dbu_done, S + 1)
                pe.matmul(ps[:, 4 + q, :], sel3[:, bass.ds(n, 1)].to_broadcast([P, P]), rhs,
                          start=True, stop=True).then_inc(b_ready, 1)
                pe.wait_ge(csb_ready, S + 1)
                pe.matmul(ps[:, 6 + q, :], sel3[:, bass.ds(n + NS, 1)].to_broadcast([P, P]), rhs,
                          start=True, stop=True).then_inc(c_ready, 1)

            def ysum(h, q, S):
                pe.wait_ge(hc_done, S + RING + 1)
                for d in range(ND):
                    ins = pe.matmul(ps[:, 2 * h + d, :], ident[:, :], hC[:, q, d, :],
                                    start=False, stop=True, skip_group_check=True)
                ins.then_inc(y_done, 1)

            def mixer0():
                for h in range(2):
                    base = h * NS
                    if h == 0:
                        pe.wait_ge(dve_s.sem, DVE["consts"])
                    for d in range(ND):
                        ins = pe.matmul(ps[:, 2 * h + d, :], diagD[:, d, :],
                                        u[:, d, h * HALF:(h + 1) * HALF], start=True, stop=True)
                    mark(ins, f"y_init{h}")
                    for q in range(RING):
                        rep(h, q, q, base + q)
                    with pe.Fori(1, NS // RING) as j:
                        for q in range(RING):
                            rep(h, j * RING + q, q, base + j * RING + q)
                            ysum(h, q, base + j * RING + q - RING)
                    for q in range(RING):
                        ysum(h, q, base + NS - RING + q)
                pe.wait_ge(y_done, STEPS + RING)
                mark(pe.matmul(ps[0:1, 4, 0:1], ident[:, 0:1], ident[:, 0:1], start=True, stop=True), "y_all0")

            def transpose_in(k):
                pe.wait_ge(dve_s.sem, DVE[f"yz{k}"])
                for j in range(TT):
                    for d in range(ND):
                        ins = pe.transpose(ps[:, 4 + j // 2, (j % 2) * C + d * P:(j % 2) * C + (d + 1) * P],
                                           t0[:, d, j * P:(j + 1) * P], ident[:, :])
                mark(ins, f"yT{k}")
                pe.wait_ge(dve_s.sem, DVE[f"xn{k}"])
                for j in range(TT):
                    for c in range(KC):
                        ins = pe.transpose(ps[:, 2 * c + j // 4, (j % 4) * P:(j % 4 + 1) * P],
                                           xn_rows[:, j, c * P:(c + 1) * P],
                                           ident[:, :])
                mark(ins, f"xnT{k}")

            def logits(k, gate, E):
                pe.wait_ge(dve_s.sem, DVE[f"xnT{k}"])
                pe.wait_ge(s_in[4], 6 * 16)
                for j in range(TT):
                    for c in range(KC):
                        ins = pe.matmul(ps[:, 4, j * E:(j + 1) * E], xnT[:, c, j * P:(j + 1) * P], gate[:, c, :],
                                        start=(c == 0), stop=(c == KC - 1))
                mark(ins, f"logit{k}")

            def table(t, i, c, high):
                return pe.value_load(t[0:1, bass.ds(nth(i, c), 1)], min_val=0, max_val=high)

            ug_flat = ug0[:, :, :, :].rearrange("p w k n -> p (w k n)")
            dn_flat = dn0[:, :, :, :].rearrange("p w k n -> p (w k n)")

            def expert_of(i, c):
                if not has(i, c):
                    return None
                return table(blk_need, i, c, E0), table(blk_ring, i, c, WR - 1)

            def up(i, c, held, w):
                if c >= RING or not isinstance(i, int):
                    pe.wait_ge(h_done, nth(i, c) - RING + 1)
                pe.wait_ge(xdT_ready, nth(i, c) + 1)
                pe.wait_ge(w_loaded, held)
                for part in range(2):
                    for kc in range(KC):
                        ins = pe.matmul(ps[:, 2 * part + c % 2, 0:H0], xdT[:, c % 2, kc, :],
                                        ug_flat[:, bass.ds(w * (KC * 2 * H0) + (kc * 2 + part) * H0, H0)],
                                        start=(kc == 0), stop=(kc == KC - 1))
                ins.then_inc(up_done, 1)

            def turn_x(i, c):
                if not has(i, c):
                    return
                pe.wait_ge(s_xd[c % 3], per(i, c, 3) * 16 + 16)
                if c >= 1 or not isinstance(i, int):
                    pe.wait_ge(xdT_ready, nth(i, c))
                for kc in range(KC):
                    ins = pe.transpose(ps[:, 6, kc * P:(kc + 1) * P], xd_sb[:, c % 3, kc * P:(kc + 1) * P], ident[:, :])
                ins.then_inc(x_turned, 1)

            def turn_h(i, c):
                if not has(i, c):
                    return
                pe.wait_ge(h_done, nth(i, c) + 1)
                if c >= 1 or not isinstance(i, int):
                    pe.wait_ge(hT_ready, nth(i, c))
                for m in range(HK):
                    ins = pe.transpose(ps[0:HP, 4, m * P:(m + 1) * P], hx[:, c % 2, m * HP:(m + 1) * HP], ident[:, :])
                ins.then_inc(h_turned, 1)

            def down(i, c, w):
                pe.wait_ge(hT_ready, nth(i, c) + 1)
                pe.wait_ge(y_evac, nth(i, c) + 1)
                for m in range(HK):
                    ins = pe.matmul(ps[:, 5, 0:C], hT[0:HP, c % 2, m * P:(m + 1) * P],
                                    dn_flat[:, bass.ds(w * (HK * C) + m * C, C)],
                                    start=(m == 0), stop=(m == HK - 1))
                ins.then_inc(dn_done, 1)

            def rep1(i, h, n, item):
                m, is_c = item // 2, item % 2
                pe.wait_ge(bc_sb, i * (2 * BSTEP) + item + 1)
                pe.matmul(ps[:, 7, :], sel3[:, bass.ds(n + m + NS * is_c, 1)].to_broadcast([P, P]),
                          bc3[:, h * HALF:(h + 1) * HALF], start=True, stop=True).then_inc(bc_ps, 1)

            def body(i, h, n):
                items = list(range(2 * BSTEP))
                this = expert_of(i, RING)
                for r in range(BODY):
                    c = r + RING
                    if has(i, c):
                        up(i, c, *this)
                    if r < BODY - 1:
                        this = expert_of(i, c + 1)
                    if has(i, c - 2):
                        w = table(blk_ring, i, c - 2, WR - 1)
                    if items:
                        rep1(i, h, n, items.pop(0))
                    turn_x(i, c + 1)
                    turn_h(i, c - 1)
                    if has(i, c - 2):
                        down(i, c - 2, w)
                    if items:
                        rep1(i, h, n, items.pop(0))

            def ffn0():
                pe.wait_ge(dve_s.sem, DVE["du1"])
                pe.sem_inc(dn_done, 1)
                turn_x(0, 0)
                up(0, 0, *expert_of(0, 0))
                turn_x(0, 1)
                up(0, 1, *expert_of(0, 1))
                turn_x(0, 2)
                turn_h(0, 0)
                bodies(pe, body)

            def shared1():
                for h in range(2):
                    if h == 1:
                        pe.wait_ge(dve_s.sem, DVE["sh_h0"])
                    for c in range(KC):
                        ins = pe.matmul(ps[:, 4, :], shu[:, c, :], xnT[:, c, h * HALF:(h + 1) * HALF],
                                        start=(c == 0), stop=(c == KC - 1))
                    mark(ins, f"sh_up{h}")
                for h in range(2):
                    pe.wait_ge(dve_s.sem, DVE[f"sh_h{h}"])
                    for t in range(4):
                        j = 4 * h + t
                        ins = pe.matmul(ps[:, j // 2, (j % 2) * C:(j % 2 + 1) * C], hT[0:P // 2, h, t * P:(t + 1) * P],
                                        shd[:, :], start=(j % 2 == 0), stop=True, skip_group_check=True)
                    mark(ins, f"sh_dn{h}")

            def parts(dst, a_hi, a_lo, b_hi, b_lo, where, start):
                for m, (at_a, at_b) in enumerate(where):
                    for p, (a, b) in enumerate(((a_hi, b_hi), (a_hi, b_lo), (a_lo, b_hi))):
                        ins = pe.matmul(dst, a[at_a], b[at_b], start=start and m + p == 0,
                                        stop=m == len(where) - 1 and p == 2, skip_group_check=not start)
                return ins

            def up1(q, h, g, n):
                if n is not None:
                    pe.wait_ge(g_p, n)
                for part, done in ((0, g_g), (1, g_v)):
                    if part == 1 and n is not None:
                        pe.wait_ge(g_q, n)
                    ins = parts(ps[:, 4 + part, :], w_hi, w_lo, x_hi, x_lo,
                                [((slice(None), q % RING, slice((2 * c + part) * P, (2 * c + part + 1) * P)),
                                  (slice(None), c, slice(h * HALF, (h + 1) * HALF))) for c in range(KC)], True)
                    ins.then_inc(done, 1)
                if n is not None:
                    pe.wait_ge(g_h, n)
                sel = sel64[:, bass.ds(g * P, P)]
                pe.matmul(ps[:, 6, :], sel,
                          wp12[:, h * HALF:(h + 1) * HALF], start=True, stop=False)
                pe.matmul(ps[:, 6, :], sel,
                          wp3[:, h * HALF:(h + 1) * HALF], start=False, stop=True).then_inc(g_w, 1)

            def down1(q, h, n):
                pe.wait_ge(g_hlo, n)
                for t in range(4):
                    j = 4 * h + t
                    ins = parts(ps[:, j // 2, (j % 2) * C:(j % 2 + 1) * C], h_hi, h_lo, w_hi, w_lo,
                                [((slice(None), h, slice(t * P, (t + 1) * P)),
                                  (slice(None), q % RING, slice(4 * P, 4 * P + C)))], False)
                ins.then_inc(g_dn, 1)

            def ffn1():
                pe.wait_ge(dve_s.sem, DVE["wparts1"])
                def group(i, q):
                    pe.wait_ge(g_wlo, i * GR + q + 1)
                    for h in range(2):
                        n = (i * GR + q) * 2 + h
                        up1(q, h, i * GR + q, n + 1)
                        if not isinstance(n, int) or n > 0:
                            down1((q + h - 1) % GR, 1 - h, n)

                for q in range(GR):
                    group(0, q)
                with pe.Fori(1, NG // GR) as i:
                    for q in range(GR):
                        group(i, q)
                down1(GR - 1, 1, 2 * NG)
                pe.wait_ge(g_dn, 2 * NG)
                mark(pe.matmul(ps[0:1, 4, 0:1], ident[:, 0:1], ident[:, 0:1], start=True, stop=True), "ffn1")

            def earlier(k, E):
                pe.wait_ge(dve_s.sem, DVE[f"sel{k}"])
                mk = maskb[:, :, :].rearrange("p j e -> p (j e)")
                for j in range(TT):
                    for i in range(j + 1):
                        ins = pe.matmul(ps[:, 5, j * E:(j + 1) * E], tri[:, 0 if i == j else 1, :], mk[:, i * E:(i + 1) * E],
                                        start=(i == 0), stop=(i == j))
                if k == 0:
                    for i in range(TT):
                        ins = pe.matmul(ps[:, 5, TT * E:(TT + 1) * E], tri[:, 1, :], mk[:, i * E:(i + 1) * E],
                                        start=(i == 0), stop=(i == TT - 1))
                mark(ins, f"pos{k}")

            pe.wait_ge(s_in[0], 48)
            project_in(0)
            pe.wait_ge(s_in[1], 48)
            prep(0)
            pe.sem_inc(y_done, RING)
            mixer0()
            transpose_in(0)
            logits(0, gate0, E0)
            project_in(1)
            earlier(0, E0)
            prep(1)
            ffn0()
            transpose_in(1)
            logits(1, gate1, E1)
            earlier(1, E1)
            pe.wait_ge(dve_s.sem, DVE["route1"])
            for j in range(TT):
                ins = pe.transpose(ps[:, 6 + j // 4, (j % 4) * P:(j % 4 + 1) * P],
                                   w2x[:, j, :, :].rearrange("p a e -> p (a e)"), ident[:, :])
            mark(ins, "wT1")
            shared1()
            ffn1()

        @block.scalar
        def _(act):
            def mark(ins, name):
                assert AC[name] == act_s.n + 1, name
                act_s.mark(ins)

            def prep(k):
                act.wait_ge(dve_s.sem, DVE[f"conv{k}"])
                act.activation(t0[:, :, :], u[:, :, :], ACT.Tanh, scale=0.5)
                mark(act.activation(u[:, :, :], u[:, :, :], ACT.Copy, scale=0.5), f"th_u{k}")
                act.wait_ge(pe_s.sem, PE[f"xdbl{k}"])
                mark(act.activation(dtlo[:, :].rearrange("p (h t) -> p h t", h=2), ps[0:DR, 4:6, :], ACT.Copy), f"dtlo{k}")
                act.wait_ge(dve_s.sem, DVE[f"v{k}"])
                mark(act.activation(t1[:, :, :], delta[:, :, :], ACT.Abs), f"abs{k}")
                act.wait_ge(act_s.sem, AC[f"abs{k}"])
                mark(act.activation(t0[:, :, :], t1[:, :, :], ACT.Exp, scale=-1.0), f"e{k}")
                act.wait_ge(act_s.sem, AC[f"e{k}"])
                act.wait_ge(dve_s.sem, DVE[f"w{k}"])
                mark(act.activation(t1[:, :, :], t0[:, :, :], ACT.Ln, bias=1.0), f"ln{k}")

            def mixer0():
                for h in range(2):
                    base = h * NS
                    with act.Fori(0, NS // RING) as j:
                        for q in range(RING):
                            n = j * RING + q
                            S = n + base
                            act.wait_ge(scan_done, S + 1)
                            decay(0, h, n, q).then_inc(da_ready, 1)
                            act.wait_ge(c_ready, S + 1)
                            act.wait_ge(hc_done, S + 1)
                            act.activation(Csb[:, q, :], ps[:, 6 + q, :], ACT.Copy).then_inc(csb_ready, 1)

            def decay(k, h, n, q):
                for d in range(ND):
                    ins = act.activation(
                        dA[:, q, d, :].rearrange("p (b l) -> p b l", b=2)[:, :, 1:L],
                        delta[:, d, h * HALF:(h + 1) * HALF].rearrange("p (b l) -> p b l", b=2)[:, :, 1:L],
                        ACT.Exp, scale=negA[:, k, d, bass.ds(n, 1)])
                return ins

            def gate_in(k):
                act.wait_ge(dve_s.sem, DVE[f"zh{k}"])
                mark(act.activation(t1[:, :, :], t0[:, :, :], ACT.Tanh), f"zth{k}")

            act.wait_ge(s_in[1], 48)
            ins = act.activation(negA[:, :, :, :], alog[:, :, :, :], ACT.Exp)
            mark(ins, "negA")
            prep(0)
            gate_in(0)
            act.sem_inc(csb_ready, RING)
            act.wait_ge(dve_s.sem, DVE["consts"])
            act.wait_ge(pool_s.sem, POOL["zero"])
            mixer0()

            def route_exp(k, E):
                act.wait_ge(dve_s.sem, DVE[f"lsub{k}"])
                n = TT * E
                mark(act.activation(r0[:, :, :].rearrange("p j e -> p (j e)")[:, 0:n],
                                    r1[:, :, :].rearrange("p j e -> p (j e)")[:, 0:n], ACT.Exp), f"ex{k}")

            route_exp(0, E0)

            def load_rows(i, c):
                if has(i, c):
                    act.dma_start(xd_sb[:, c % 3, :], xd[bass.ds(nth(i, c) * P, P), :]).then_inc(s_xd[c % 3], 16)

            def gate(i, c):
                if not has(i, c):
                    return
                act.wait_ge(up_done, nth(i, c) + 1)
                if c >= RING or not isinstance(i, int):
                    act.wait_ge(p_done, nth(i, c) - RING + 1)
                act.activation(th[:, c % 2, 0:H0], ps[:, 2 + c % 2, 0:H0], ACT.Tanh, scale=0.5).then_inc(th_done, 1)

            def take_xT(i, c):
                if not has(i, c):
                    return
                act.wait_ge(x_turned, nth(i, c) + 1)
                if c >= RING or not isinstance(i, int):
                    act.wait_ge(up_done, nth(i, c) - RING + 1)
                act.activation(xdT[:, c % 2, :, :].rearrange("p k t -> p (k t)"), ps[:, 6, 0:C], ACT.Copy).then_inc(xdT_ready, 1)
                load_rows(i, c + 3)

            def take_hT(i, c):
                if not has(i, c):
                    return
                act.wait_ge(h_turned, nth(i, c) + 1)
                if c >= 1 or not isinstance(i, int):
                    act.wait_ge(dn_done, nth(i, c))
                act.activation(hT[0:HP, c % 2, :], ps[0:HP, 4, :], ACT.Copy).then_inc(hT_ready, 1)

            def take_y(i, c):
                if not has(i, c):
                    return
                act.wait_ge(dn_done, nth(i, c) + 2)
                act.wait_ge(s_y[c % 2], per(i, c, 2) * 16 + 16)
                act.activation(ysb[:, c % 2, :], ps[:, 5, 0:C], ACT.Copy).then_inc(y_evac, 1)
                act.wait_ge(y_evac, nth(i, c) + 2)
                act.dma_start(yd[bass.ds(nth(i, c) * P, P), :], ysb[:, c % 2, :]).then_inc(s_y[c % 2], 16)

            def take_bc(i, item):
                m, is_c = item // 2, item % 2
                t = i * BSTEP + m
                act.wait_ge(bc_ps, i * (2 * BSTEP) + item + 1)
                if is_c:
                    act.wait_ge(hc1, t + 1)
                else:
                    act.wait_ge(dbu1, t + 1)
                act.activation((Csb if is_c else Bsb)[:, m % 2, :], ps[:, 7, :], ACT.Copy).then_inc(bc_sb, 1)

            def decay1(i, h, n, m):
                act.wait_ge(scan1, i * BSTEP + m + 1)
                decay(1, h, n + m, m % 2).then_inc(da1, 1)

            def body(i, h, n):
                items = list(range(2 * BSTEP))
                for r in range(BODY):
                    c = r + RING
                    gate(i, c)
                    if items:
                        take_bc(i, items.pop(0))
                    take_xT(i, c + 1)
                    take_hT(i, c - 1)
                    if r < BSTEP:
                        decay1(i, h, n, r)
                    take_y(i, c - 2)
                    if items:
                        take_bc(i, items.pop(0))

            prep(1)
            act.wait_ge(dve_s.sem, DVE["du1"])
            for d in range(ND):
                ins = act.activation(y1[:, d, :], u[:, d, :], ACT.Copy, scale=par[:, 1, d, 6:7])
            mark(ins, "y1init")
            act.sem_inc(bc_sb, 1)
            act.sem_inc(y_evac, 1)
            for q in range(RING):
                act.sem_inc(s_y[q], 16)
            act.wait_ge(s_scat, TOPK0 * TT * 16)
            for c in range(3):
                load_rows(0, c)
            take_xT(0, 0)
            gate(0, 0)
            take_xT(0, 1)
            gate(0, 1)
            take_xT(0, 2)
            take_hT(0, 0)
            bodies(act, body)
            for q in range(RING):
                act.wait_ge(s_y[q], ((NB + 1 - q) // 2) * 16 + 16)
            act.sem_inc(y_evac, 1)

            def weights_hi(i, q, free=None):
                act.wait_ge(s_g1[q], i * 16 + 16)
                if free is not None:
                    act.wait_ge(g_dn, free)
                act.activation(w_hi[:, q % RING, :], g1w[:, q, :], ACT.Copy).then_inc(g_whi, 1)

            weights_hi(0, 0)
            weights_hi(0, 1)
            gate_in(1)
            act.wait_ge(dve_s.sem, DVE["xnT1"])
            mark(act.activation(x_hi[:, :, :], xnT[:, :, :], ACT.Copy), "xhi1")
            route_exp(1, E1)
            for h in range(2):
                act.wait_ge(pe_s.sem, PE[f"sh_up{h}"])
                mark(act.activation(th[P // 2:P, h, :], ps[P // 2:P, 4, :], ACT.Tanh, scale=0.5), f"sh_th{h}")

            def half_group(h, n):
                act.wait_ge(g_g, n + 1)
                act.wait_ge(g_p, n + 1)
                act.activation(th[:, h, :], ps[:, 4, :], ACT.Tanh, scale=0.5).then_inc(g_th, 1)
                act.wait_ge(g_h, n + 2)
                if not isinstance(n, int) or n >= RING:
                    act.wait_ge(g_dn, n - RING + 1)
                act.activation(h_hi[:, h, :], hT[:, h, :], ACT.Copy).then_inc(g_hhi, 1)

            def group(i, q):
                for h in range(2):
                    half_group(h, (i * GR + q) * 2 + h)
                    if h == 0 and (not isinstance(i, int) or i or q):
                        weights_hi(i + (q + 1) // GR, (q + 1) % GR, (i * GR + q) * 2)

            for q in range(GR):
                group(0, q)
            with act.Fori(1, NG // GR - 1) as i:
                for q in range(GR):
                    group(i, q)
            last = NG // GR - 1
            for q in range(GR - 1):
                group(last, q)
            for h in range(2):
                half_group(h, (NG - 1) * 2 + h)

        @block.gpsimd
        def _(pool):
            for q in range(RING):
                for d in range(ND):
                    ins = pool.memset(dA[:, q, d, :].rearrange("p (b l) -> p b l", b=2)[:, :, 0:1], 0.0)
            pool.memset(expo[:, :], -0.5)
            pool.memset(first0[:, :, :], 1.0)
            pool.memset(first1[:, :, :], 1.0).then_inc(pool_s.sem, 1)
            pool.sem_inc(hc_done, RING)

            def rstd_of(k, pre):
                pool.wait_ge(dve_s.sem, DVE[f"{pre}stat{k}"])
                pool.tensor_tensor(rstd[:, :], mv[:, :, 1], expo[:, :], ALU.pow).then_inc(pool_s.sem, 1)

            def times_c(q):
                return pool.tensor_tensor(hC[:, q, :, :], hs[:, q, :, :],
                                          Csb[:, q, :].unsqueeze(1).to_broadcast([P, ND, HALF]), ALU.mult)

            rstd_of(0, "z")
            with pool.Fori(0, STEPS // RING) as i:
                for q in range(RING):
                    S = i * RING + q
                    pool.wait_ge(scan_done, S + RING + 1)
                    pool.wait_ge(csb_ready, S + RING + 1)
                    pool.wait_ge(y_done, S + 1)
                    times_c(q).then_inc(hc_done, 1)
            rstd_of(0, "n")
            pool.wait_ge(dve_s.sem, DVE["slots0"])
            pool.wait_ge(s_zero, 16)
            for j in range(TT):
                for k in range(TOPK0):
                    pool.indirect_dma_start(xd, bass.IndirectOffsetOnAxis(ap=slot_u[:, k, j:j + 1], axis=0),
                                            xn_rows[:, j, :], None).then_inc(s_scat, 16)
            pool.sem_inc(hc1, RING)
            pool.wait_ge(act_s.sem, AC["y1init"])
            pool.wait_ge(s_scat, TOPK0 * TT * 16)
            for h in range(2):
                with pool.Fori(0, NS // RING) as i:
                    for q in range(RING):
                        t = i * RING + q + h * NS
                        pool.wait_ge(scan1, t + RING + 1)
                        pool.wait_ge(bc_sb, t * 2 + 3)
                        times_c(q).then_inc(hc1, 1)
                        pool.wait_ge(hc1, t + RING + 1)
                        y = y1[:, :, h * HALF:(h + 1) * HALF]
                        pool.tensor_tensor(y, y, hC[:, q, :, :], ALU.add).then_inc(add1, 1)
                        pool.wait_ge(add1, t + 1)
            pool.sem_inc(pool_s.sem, 1)
            pool.wait_ge(y_evac, NB + 2)
            for q in range(RING):
                pool.wait_ge(s_y[q], ((NB + 1 - q) // 2) * 16 + 16)
            for j in range(TT):
                for k in range(TOPK0):
                    g = j * TOPK0 + k
                    if g >= 8:
                        pool.wait_ge(s_comb, g - 7)
                    pool.indirect_dma_start(gb[:, g % 8, :], None, yd,
                                            bass.IndirectOffsetOnAxis(ap=slot_u[:, k, j:j + 1], axis=0)).then_inc(s_gb[g % 8], 16)
            rstd_of(1, "z")
            rstd_of(1, "n")
            with pool.Fori(0, NG // GR) as i:
                for q in range(GR):
                    pool.wait_ge(g_whi, i * GR + q + 1)
                    pool.tensor_tensor(w_lo[:, q % RING, :], g1w[:, q, :], w_hi[:, q % RING, :].bitcast(F32), ALU.subtract).then_inc(g_wlo, 1)

        @block.vector
        def _(dve):
            dch = Stage(sem("dch"))

            def link(ins):
                dch.mark(ins)
                dve.wait_ge(dch.sem, dch.n)

            def mark(ins, name, wait=False):
                assert DVE[name] == dve_s.n + 1, name
                dve_s.mark(ins)
                if wait:
                    dve.wait_ge(dve_s.sem, dve_s.n)

            def prep(k):
                dve.wait_ge(pe_s.sem, PE[f"xin{k}"])
                for d in range(ND):
                    src = ps[:, 2 * d:2 * d + 2, :].rearrange("p h (b l) -> p (h b) l", b=2)
                    dst = u[:, d, :].rearrange("p (b l) -> p b l", b=B)
                    link(dve.tensor_scalar(dst, src, par[:, k, d, 3:4], par[:, k, d, 4:5], ALU.mult, ALU.add))
                    for s in range(1, 4):
                        ins = dve.scalar_tensor_tensor(dst[:, :, s:L], src[:, :, 0:L - s], par[:, k, d, 3 - s:4 - s],
                                                       dst[:, :, s:L], ALU.mult, ALU.add)
                        if s < 3 or d == 0:
                            link(ins)
                mark(ins, f"conv{k}")
                dve.wait_ge(act_s.sem, AC[f"th_u{k}"])
                mark(dve.scalar_tensor_tensor(u[:, :, :].rearrange("p a b -> p (a b)"), t0[:, :, :].rearrange("p a b -> p (a b)"), 1.0,
                                              u[:, :, :].rearrange("p a b -> p (a b)"), ALU.add, ALU.mult), f"u{k}", True)
                dve.wait_ge(pe_s.sem, PE[f"xdbl{k}"])
                x2 = ps[:, 4:6, :]
                p3 = bc3[:, :].rearrange("p (h t) -> p h t", h=2)
                r = t0[:, 0, :].rearrange("p (h t) -> p h t", h=2)
                dve.wait_ge(act_s.sem, AC[f"dtlo{k}"])
                link(dve.tensor_copy(p3, x2))
                link(dve.tensor_tensor(r[64:P], x2[64:P], p3[64:P], ALU.subtract))
                link(dve.tensor_copy(p3[64:P], r[64:P]))
                mark(dve.tensor_tensor(p3[96:P], r[96:P], p3[96:P], ALU.subtract), f"bc{k}")
                dve.wait_ge(pe_s.sem, PE[f"dtp{k}"])
                for d in range(ND):
                    ins = dve.tensor_scalar(delta[:, d, :], ps[:, 2 * d:2 * d + 2, :].rearrange("p h t -> p (h t)"),
                                            par[:, k, d, 5:6], None, ALU.add)
                mark(ins, f"v{k}")
                dve.wait_ge(act_s.sem, AC[f"e{k}"])
                e2 = t0[:, :, :].rearrange("p a b -> p (a b)")
                w2 = du[:, :, :].rearrange("p a b -> p (a b)")
                d2 = delta[:, :, :].rearrange("p a b -> p (a b)")
                l2 = t1[:, :, :].rearrange("p a b -> p (a b)")
                link(dve.tensor_scalar(w2, e2, 1.0, None, ALU.add))
                mark(dve.scalar_tensor_tensor(w2, w2, 1.0, e2, ALU.subtract, ALU.subtract), f"w{k}", True)
                dve.wait_ge(act_s.sem, AC[f"ln{k}"])
                link(dve.tensor_tensor(l2, l2, w2, ALU.subtract))
                mark(dve.scalar_tensor_tensor(d2, d2, 0.0, l2, ALU.max, ALU.add), f"delta{k}", True)
                mark(dve.tensor_tensor(w2, d2, u[:, :, :].rearrange("p a b -> p (a b)"), ALU.mult), f"du{k}")

            mark(dve.memset(zero[:, :], 0.0), "zero")
            dve.wait_ge(s_in[0], 48)
            prep(0)
            dve.wait_ge(s_in[2], 32)
            for d in range(ND):
                dve.tensor_scalar(diagD[:, d, :], ident[:, :], par[:, 0, d, 6:7], None, ALU.mult)
            dve.wait_ge(act_s.sem, AC["negA"])
            dve.wait_ge(pool_s.sem, POOL["zero"])
            dve.memset(first0[:, :, 0:1], 0.0)
            dve.memset(first1[:, :, 0:1], 0.0)
            mark(dve.tensor_scalar(negA[:, :, :, :], negA[:, :, :, :], -1.0, None, ALU.mult), "consts", True)
            dve.sem_inc(dbu_done, RING)
            dve.sem_inc(scan_done, RING)

            def drive(h, q, row):
                return dve.tensor_tensor(dBu[:, q, :, :], du[:, :, h * HALF:(h + 1) * HALF],
                                         row.unsqueeze(1).to_broadcast([P, ND, HALF]), ALU.mult)

            def scan(q):
                return dve.tensor_tensor_scan(hs[:, q, :, :].rearrange("p a b -> p (a b)"),
                                              dA[:, q, :, :].rearrange("p a b -> p (a b)"),
                                              dBu[:, q, :, :].rearrange("p a b -> p (a b)"), 0.0, ALU.mult, ALU.add)

            def mixer0():
                for h in range(2):
                    base = h * NS
                    with dve.Fori(0, NS // RING) as j:
                        for q in range(RING):
                            S = j * RING + q + base
                            dve.wait_ge(b_ready, S + 1)
                            drive(h, q, ps[:, 4 + q, :]).then_inc(dbu_done, 1)
                            dve.wait_ge(da_ready, S + 1)
                            dve.wait_ge(dbu_done, S + RING + 1)
                            dve.wait_ge(hc_done, S + 1)
                            scan(q).then_inc(scan_done, 1)

            def norm_stats(name):
                for j in range(TT):
                    ins = dve.bn_stats(stats[:, j, :], xs[:, j, :])
                link(ins)
                for j in range(TT):
                    ins = dve.bn_aggr(mv[:, j, :], stats[:, j, :])
                link(ins)
                mark(dve.tensor_scalar(mv[:, :, 1], mv[:, :, 1], EPS, None, ALU.add), name)

            def gate_in(k):
                if k == 0:
                    dve.wait_ge(s_in[3], 16)
                norm_stats(f"zstat{k}")
                dve.wait_ge(pool_s.sem, POOL[f"zr{k}"])
                link(dve.tensor_scalar(rstd[:, :], rstd[:, :], 0.5, None, ALU.mult))
                for j in range(TT):
                    ins = dve.tensor_scalar(t0[:, j % 2, (j // 2) * L:(j // 2 + 1) * L], xs[:, j, :], mv[:, j, 0:1],
                                            rstd[:, j:j + 1], ALU.subtract, ALU.mult)
                mark(ins, f"zh{k}", True)
                dve.wait_ge(act_s.sem, AC[f"zth{k}"])
                z = t0[:, :, :].rearrange("p a b -> p (a b)")
                g = t1[:, :, :].rearrange("p a b -> p (a b)")
                mark(dve.scalar_tensor_tensor(g, g, 1.0, z, ALU.add, ALU.mult), f"G{k}", True)

            def mixer_out(k):
                if k == 0:
                    dve.wait_ge(pe_s.sem, PE["y_all0"])
                else:
                    dve.wait_ge(pool_s.sem, POOL["y1"])
                for h in range(2):
                    t = slice(h * HALF, (h + 1) * HALF)
                    y = ps[:, 2 * h:2 * h + 2, :] if k == 0 else y1[:, :, t]
                    ins = dve.tensor_tensor(t0[:, :, t], y, t1[:, :, t], ALU.mult)
                mark(ins, f"yz{k}")

            def norm_out(k):
                dve.wait_ge(pe_s.sem, PE[f"yT{k}"])
                xf = xs[:, :, :].rearrange("p j c -> p (j c)")
                mark(dve.tensor_tensor(xf, xf, ps[:, 4:8, :].rearrange("p h t -> p (h t)"), ALU.add), f"xnew{k}", True)
                norm_stats(f"nstat{k}")
                dve.wait_ge(pool_s.sem, POOL[f"nr{k}"])
                tf = xn_rows[:, :, :].rearrange("p j c -> p (j c)")
                for j in range(TT):
                    ins = dve.tensor_scalar(tf[:, j * C:(j + 1) * C], xs[:, j, :], mv[:, j, 0:1],
                                            rstd[:, j:j + 1], ALU.subtract, ALU.mult)
                mark(ins, f"xn{k}")
                dve.wait_ge(pe_s.sem, PE[f"xnT{k}"])
                mark(dve.tensor_copy(xnT[:, :, :].rearrange("p c t -> p (c t)"), ps[:, 0:4, :].rearrange("p h t -> p (h t)")), f"xnT{k}")

            def by_e(t, E):
                return t[:, :, :].rearrange("p j e -> p (j e)")[:, 0:TT * E].rearrange("p (j e) -> p j e", e=E)

            def flat(t, E):
                return t[:, :, :].rearrange("p j e -> p (j e)")[:, 0:TT * E]

            def pick(score, E, top):
                for j in range(TT):
                    ins = dve.max(top8[:, j, :], score[:, j, :])
                link(ins)
                kth = top8[:, :, top - 1:top].to_broadcast([P, TT, E])
                gt, eq, cum = by_e(r2, E), by_e(r1, E), by_e(r0, E)
                dve.tensor_tensor(gt, score, kth, ALU.is_gt)
                link(dve.tensor_tensor(eq, score, kth, ALU.is_equal))
                dve.tensor_reduce(need[:, :], gt, AX_X, ALU.add)
                link(dve.tensor_tensor_scan(flat(r0, E), flat(first0 if E == E0 else first1, E), flat(r1, E), 0.0, ALU.mult, ALU.add))
                link(dve.tensor_scalar(need[:, :], need[:, :], -1.0, float(top), ALU.mult, ALU.add))
                link(dve.tensor_tensor(cum, cum, need[:, :].unsqueeze(2).to_broadcast([P, TT, E]), ALU.is_le))
                link(dve.tensor_tensor(eq, eq, cum, ALU.mult))
                link(dve.tensor_tensor(gt, gt, eq, ALU.add))

            gate_in(0)
            mixer0()
            mixer_out(0)
            norm_out(0)

            dve.wait_ge(pe_s.sem, PE["logit0"])
            l0 = by_e(lg, E0)
            link(dve.tensor_copy(flat(lg, E0), ps[:, 4, 0:TT * E0]))
            pick(l0, E0, TOPK0)
            mark(dve.tensor_tensor(by_e(r1, E0), l0, top8[:, :, 0:1].to_broadcast([P, TT, E0]), ALU.subtract), "lsub0")
            mark(dve.tensor_copy(flat(maskb, E0), flat(r2, E0)), "sel0")
            NE = TT * E0
            rank, place = big[:, 0:NE], big[:, NE:2 * NE]
            sel = big[:, 2 * NE:(2 + TOPK0) * NE].rearrange("p (k n) -> p k n", k=TOPK0)
            prod = big[:, (2 + TOPK0) * NE:(2 + 2 * TOPK0) * NE].rearrange("p (k n) -> p k n", k=TOPK0)
            by_sum = big[:, (2 + TOPK0) * NE:(2 + 2 * TOPK0) * NE].rearrange("p (a e) -> p a e", e=E0)
            ks = steps[:, 8:8 + TOPK0]

            def over_k(t):
                return t.unsqueeze(1).to_broadcast([P, TOPK0, NE])

            dve.wait_ge(s_in[5], 16)
            link(dve.tensor_tensor_scan(rank, flat(first0, E0), flat(r2, E0), 0.0, ALU.mult, ALU.add))
            link(dve.tensor_tensor(sel, over_k(rank), ks.unsqueeze(2).to_broadcast([P, TOPK0, NE]), ALU.is_equal))
            link(dve.tensor_tensor(sel, sel, over_k(flat(r2, E0)), ALU.mult))
            dve.wait_ge(pe_s.sem, PE["pos0"])
            cmp = prod.rearrange("p k n -> p (k n)")[:, 0:E0 * 8].rearrange("p (e m) -> p e m", m=8)
            link(dve.tensor_tensor(cmp, ps[:, 5, NE:NE + E0].unsqueeze(2).to_broadcast([P, E0, 8]),
                                   steps[:, 0:8].unsqueeze(1).to_broadcast([P, E0, 8]), ALU.is_gt))
            link(dve.tensor_reduce(nblk[:, :], cmp, AX_X, ALU.add))
            link(dve.tensor_tensor_scan(endb[:, :], first1[:, 0, 1:1 + E0], nblk[:, :], 0.0, ALU.mult, ALU.add))
            link(dve.tensor_tensor(startb[:, :], endb[:, :], nblk[:, :], ALU.subtract))
            link(dve.scalar_tensor_tensor(place.rearrange("p (j e) -> p j e", e=E0),
                                          startb[:, :].unsqueeze(1).to_broadcast([P, TT, E0]), float(P),
                                          ps[:, 5, 0:NE].rearrange("p (j e) -> p j e", e=E0), ALU.mult, ALU.add))
            link(dve.tensor_tensor(prod, sel, over_k(place), ALU.mult))
            sf = slot_f[:, :, :].rearrange("p k j -> p (k j)")
            link(dve.tensor_reduce(sf, by_sum, AX_X, ALU.add))
            mark(dve.tensor_copy(slot_u[:, :, :].rearrange("p k j -> p (k j)"), sf), "slots0")
            NBP = NB + 1
            eb, m3 = blk_f[0:1, 0, 0:NBP], blk_f[0:1, 1, 0:NBP]
            cmp = big[0:1, (2 + TOPK0) * NE:(2 + TOPK0) * NE + NBP * 8].rearrange("p (b e) -> p b e", e=8)
            ids = steps[0:1, 32:32 + NBP].unsqueeze(2)
            for part in range(2):
                link(dve.tensor_tensor(cmp, endb[0:1, 8 * part:8 * part + 8].unsqueeze(1).to_broadcast([1, NBP, 8]),
                                       ids.to_broadcast([1, NBP, 8]), ALU.is_le))
                link(dve.tensor_reduce(blk_f[0:1, part, 0:NBP], cmp, AX_X, ALU.add))
            link(dve.tensor_tensor(eb, eb, m3, ALU.add))
            link(dve.tensor_scalar(eb, eb, float(E0 - 1), None, ALU.min))
            dve.tensor_scalar(blk_need[:, 0:NBP], eb, 1.0, None, ALU.add)
            NM = (E0 - 1) // WR
            cmp = big[0:1, (2 + TOPK0) * NE:(2 + TOPK0) * NE + NBP * NM].rearrange("p (b e) -> p b e", e=NM)
            link(dve.tensor_tensor(cmp, eb.unsqueeze(2).to_broadcast([1, NBP, NM]),
                                   steps[0:1, 16:16 + NM].unsqueeze(1).to_broadcast([1, NBP, NM]), ALU.is_ge))
            link(dve.tensor_reduce(m3, cmp, AX_X, ALU.add))
            dve.scalar_tensor_tensor(blk_ring[:, 0:NBP], m3, -float(WR), eb, ALU.mult, ALU.add)
            mark(dve.tensor_scalar(end_i[:, :], endb[0:1, :], 1.0, None, ALU.add), "blocks0")
            dve.wait_ge(act_s.sem, AC["ex0"])
            link(dve.tensor_tensor(flat(r0, E0), flat(r0, E0), flat(r2, E0), ALU.mult))
            link(dve.tensor_reduce(need[:, :], by_e(r0, E0), AX_X, ALU.add))
            link(dve.reciprocal(need[:, :], need[:, :]))
            link(dve.tensor_tensor(by_e(r0, E0), by_e(r0, E0), need[:, :].unsqueeze(2).to_broadcast([P, TT, E0]), ALU.mult))
            link(dve.tensor_tensor(prod, sel, over_k(flat(r0, E0)), ALU.mult))
            mark(dve.tensor_reduce(wk[:, :, :].rearrange("p k j -> p (k j)"), by_sum, AX_X, ALU.add), "route0", True)

            prep(1)
            for s in (dbu1, scan1):
                dve.sem_inc(s, RING)

            def hidden(i, c):
                if not has(i, c):
                    return
                dve.wait_ge(th_done, nth(i, c) + 1)
                dve.scalar_tensor_tensor(pg[:, c % 2, 0:H0], th[:, c % 2, 0:H0], 1.0, ps[:, 2 + c % 2, 0:H0],
                                         ALU.add, ALU.mult).then_inc(p_done, 1)
                dve.wait_ge(p_done, nth(i, c) + 1)
                if c >= RING or not isinstance(i, int):
                    dve.wait_ge(h_turned, nth(i, c) - RING + 1)
                dve.scalar_tensor_tensor(hx[:, c % 2, 0:H0], pg[:, c % 2, 0:H0], 0.5, ps[:, c % 2, 0:H0],
                                         ALU.mult, ALU.mult).then_inc(h_done, 1)

            def body(i, h, n):
                for r in range(BODY):
                    if r < BSTEP:
                        t = i * BSTEP + r
                        dve.wait_ge(bc_sb, t * 2 + 2)
                        drive(h, r % 2, Bsb[:, r % 2, :]).then_inc(dbu1, 1)
                        dve.wait_ge(dbu1, t + RING + 1)
                        dve.wait_ge(da1, t + 1)
                        dve.wait_ge(hc1, t + 1)
                        scan(r % 2).then_inc(scan1, 1)
                    hidden(i, r + RING)

            dve.wait_ge(s_scat, TOPK0 * TT * 16)
            hidden(0, 0)
            hidden(0, 1)
            bodies(dve, body)
            for j in range(TT):
                for k in range(TOPK0):
                    g = j * TOPK0 + k
                    dve.wait_ge(s_gb[g % 8], (g // 8 + 1) * 16)
                    if k:
                        dve.wait_ge(s_comb, g)
                    ins = dve.scalar_tensor_tensor(xs[:, j, :], gb[:, g % 8, :], wk[:, k, j:j + 1], xs[:, j, :], ALU.mult, ALU.add)
                    ins.then_inc(s_comb, 1)
            dve.wait_ge(s_comb, TT * TOPK0)
            mark(dve.tensor_copy(need[:, :], need[:, :]), "combined", True)

            gate_in(1)
            mixer_out(1)
            norm_out(1)
            dve.wait_ge(pe_s.sem, PE["logit1"])
            mark(dve.tensor_scalar(r1[:, :, :], ps[:, 4, :].rearrange("p (j e) -> p j e", j=TT), -1.0, None, ALU.mult), "lsub1")
            dve.wait_ge(act_s.sem, AC["xhi1"])
            mark(dve.tensor_tensor(x_lo[:, :, :], xnT[:, :, :], x_hi[:, :, :].bitcast(F32), ALU.subtract), "xlo1")
            dve.wait_ge(act_s.sem, AC["ex1"])
            link(dve.tensor_scalar(r0[:, :, :], r0[:, :, :], 1.0, None, ALU.add))
            link(dve.reciprocal(lg[:, :, :], r0[:, :, :]))
            pick(lg[:, :, :], E1, TOPK1)
            mark(dve.tensor_copy(maskb[:, :, :], r2[:, :, :]), "sel1")
            link(dve.tensor_tensor(r0[:, :, :], lg[:, :, :], r2[:, :, :], ALU.mult))
            link(dve.tensor_reduce(need[:, :], r0[:, :, :], AX_X, ALU.add))
            link(dve.reciprocal(need[:, :], need[:, :]))
            link(dve.tensor_tensor(r0[:, :, :], r0[:, :, :], need[:, :].unsqueeze(2).to_broadcast([P, TT, E1]), ALU.mult))
            dve.wait_ge(pe_s.sem, PE["pos1"])
            link(dve.tensor_scalar(r1[:, :, :], ps[:, 5, :].rearrange("p (j e) -> p j e", j=TT), float(CAP), None, ALU.is_lt))
            for a in range(2):
                ins = dve.tensor_tensor(w2x[:, :, a, :], r0[:, :, :], r1[:, :, :], ALU.mult)
            mark(ins, "route1", True)
            dve.wait_ge(pe_s.sem, PE["wT1"])
            wt = ps[:, 6:8, :].rearrange("p h t -> p (h t)")
            link(dve.tensor_copy(wp12[:, :], wt))
            link(dve.tensor_tensor(wtmp[:, :], wt, wp12[:, :], ALU.subtract))
            dve.tensor_copy(wp12[64:P, :], wtmp[64:P, :])
            link(dve.tensor_copy(wmid[:, :], wtmp[0:E1, :]))
            dve.memset(wp3[E1:P, :], 0.0)
            mark(dve.tensor_tensor(wp3[0:E1, :], wtmp[0:E1, :], wmid[:, :], ALU.subtract), "wparts1", True)
            for h in range(2):
                dve.wait_ge(act_s.sem, AC[f"sh_th{h}"])
                link(dve.scalar_tensor_tensor(pg[P // 2:P, h, :], th[P // 2:P, h, :], 1.0, ps[P // 2:P, 4, :], ALU.add, ALU.mult))
                mark(dve.scalar_tensor_tensor(hT[0:P // 2, h, :], pg[P // 2:P, h, :], 0.5, ps[0:P // 2, 4, :], ALU.mult, ALU.mult), f"sh_h{h}", True)
            dve.wait_ge(pe_s.sem, PE["sh_dn1"])
            for s in (g_p, g_q, g_h):
                dve.sem_inc(s, 1)
            with dve.Fori(0, NG) as i:
                for h in range(2):
                    n = i * 2 + h
                    dve.wait_ge(g_th, n + 1)
                    dve.scalar_tensor_tensor(pg[:, h, :], th[:, h, :], 1.0, ps[:, 4, :], ALU.add, ALU.mult).then_inc(g_p, 1)
                    dve.wait_ge(g_v, n + 1)
                    dve.wait_ge(g_p, n + 2)
                    dve.scalar_tensor_tensor(hx[:, h, :], pg[:, h, :], 0.5, ps[:, 5, :], ALU.mult, ALU.mult).then_inc(g_q, 1)
                    dve.wait_ge(g_w, n + 1)
                    dve.wait_ge(g_q, n + 2)
                    dve.tensor_tensor(hT[:, h, :], hx[:, h, :], ps[:, 6, :], ALU.mult).then_inc(g_h, 1)
                    dve.wait_ge(g_hhi, n + 1)
                    dve.tensor_tensor(h_lo[:, h, :], hT[:, h, :], h_hi[:, h, :].bitcast(F32), ALU.subtract).then_inc(g_hlo, 1)
            dve.wait_ge(pe_s.sem, PE["ffn1"])
            xf = xs[:, :, :].rearrange("p j c -> p (j c)")
            mark(dve.tensor_tensor(xf, xf, ps[:, 0:4, :].rearrange("p h t -> p (h t)"), ALU.add), "out")


def lay_out(inp):
    import numpy as np

    g = {k: np.asarray(v) for k, v in inp.items()}
    f = np.float32
    P = 128
    x = g["x"]
    B, L, C = x.shape
    ctxt = g["ctx_1024"].reshape(B * L, -1).T
    par = np.zeros((P, 2, 2, 24), f)
    xpr = np.zeros((P, 2, 2, P), f)
    inpT, dtT = [], []
    for k in range(2):
        p = f"L{k}_xattn_"
        di = g[p + "in_proj_w"].shape[0]
        inpT.append(g[p + "in_proj_w"].T)
        dtT.append(g[p + "dt_proj_w"].T)
        cw = g[p + "conv_w"].reshape(di, 4)
        for d in range(2):
            r = slice(d * P, (d + 1) * P)
            par[:, k, d, 0:4] = cw[r]
            par[:, k, d, 4] = g[p + "conv_b"][r]
            par[:, k, d, 5] = g[p + "dt_proj_b"][r]
            par[:, k, d, 6] = g[p + "D"][r]
            par[:, k, d, 8:24] = g[p + "A_log"][r]
            xw = g[p + "x_proj_w"][:, r].T
            xpr[:, k, d, 0:8] = xw[:, 0:8]
            for c in range(3):
                xpr[:, k, d, 32 + 32 * c:64 + 32 * c] = xw[:, 8:40]
    up, gt, dn = g["L0_ffn_W_up"], g["L0_ffn_W_gate"], g["L0_ffn_W_down"]
    E, H, _ = up.shape
    ug = np.concatenate([up, gt], axis=1).transpose(0, 2, 1).reshape(E, 2, P, 2 * H).transpose(0, 2, 1, 3)
    dT = dn.transpose(0, 2, 1).reshape(E, 4, H // 4, C).transpose(0, 2, 1, 3)
    gate0 = g["L0_ffn_gate_inp"].T.reshape(2, P, E).transpose(1, 0, 2)
    gate1 = g["L1_ffn_w_gate"].reshape(2, P, -1).transpose(1, 0, 2)
    shu = g["L1_ffn_w_shared_up"].reshape(2, P, P).transpose(1, 0, 2)
    wu, wd = g["L1_ffn_w_up"], g["L1_ffn_w_down"]
    E1, _, H2 = wu.shape
    H1 = H2 // 2
    EG = P // H1
    NG = E1 // EG
    w = wu.reshape(NG, EG, 2, P, 2, H1).transpose(0, 3, 2, 4, 1, 5).reshape(NG, P, 4 * P)
    grp = np.concatenate([w, wd.reshape(NG, P, C)], axis=2)
    sel3 = np.zeros((P, 32), f)
    for c in range(1, 4):
        sel3[32 * c:32 * c + 32] = np.eye(32)
    tri = np.zeros((P, 2, P), f)
    tri[:, 0] = np.triu(np.ones((P, P)), 1)
    tri[:, 1] = 1
    steps = np.zeros((P, 96), f)
    steps[:, 0:8] = P * np.arange(8)
    steps[:, 8:12] = np.arange(1, 5)
    steps[:, 16:24] = 3 * np.arange(1, 9)
    steps[:, 32:96] = np.arange(64)
    sel64 = np.repeat(np.concatenate([np.eye(E1), np.eye(E1)]), P // EG, axis=1).astype(f)
    bf = mybir.dt.np(mybir.dt.bfloat16)
    return {
        "x": x.reshape(B * L, C), "ctxT": ctxt, "in_projT": np.stack(inpT), "ssm_par": par, "x_projT": xpr,
        "dt_projT": np.stack(dtT), "gate0T": gate0, "up0T": ug, "down0T": dT, "gate1T": gate1, "sh_upT": shu,
        "sh_down": g["L1_ffn_w_shared_down"], "grp1": grp, "ident": np.eye(P, dtype=f),
        "sel3": sel3.astype(bf), "tri": tri.astype(bf), "sel64": sel64.astype(bf), "steps": steps,
    }


def kernel(**inputs):
    import numpy as np
    import concourse.bacc as bacc
    from concourse.bass_utils import run_bass_kernel_spmd

    nc = bacc.Bacc("TRN2", target_bir_lowering=False, num_devices=1)
    arrays, args = {}, []
    for name, a in lay_out(inputs).items():
        a = np.ascontiguousarray(a)
        arrays[f"in_{name}"] = a
        args.append(nc.dram_tensor(f"in_{name}", a.shape, mybir.dt.from_np(a.dtype), kind="ExternalInput").ap())
    shape = inputs["x"].shape
    out = nc.dram_tensor("out_0", (shape[0] * shape[1], shape[2]), F32, kind="ExternalOutput").ap()
    build(nc, *args, out)
    r = run_bass_kernel_spmd(nc, [arrays], core_ids=[0])
    return r.results[0]["out_0"].reshape(shape)
```

```python
from contextlib import ExitStack

import concourse.bass as bass
from concourse import mybir

ALU = mybir.AluOpType
ACT = mybir.ActivationFunctionType
F32 = mybir.dt.float32
F32R = mybir.dt.float32r
BF16 = mybir.dt.bfloat16
AX_X = mybir.AxisListType.X

P = 128
BANK = 512


class Stage:

    def __init__(self, sem):
        self.sem, self.n = sem, 0

    def mark(self, ins, by=1):
        ins.then_inc(self.sem, by)
        self.n += by
        return self.n


def build(nc, x, ctxT, in_projT, ssm_par, x_projT, dt_projT, gate0T, up0T, down0T,
          gate1T, sh_upT, sh_down, grp1, ident_in, sel3_in, tri_in, sel64_in, steps_in, out):
    NL = 2
    B, L = 4, 256
    TOK = B * L
    TT = TOK // P
    C = x.shape[1]
    KC = C // P
    DI = in_projT.shape[2]
    ND = DI // P
    NS = 16
    DR = dt_projT.shape[1]
    HALF = TOK // 2
    E0 = up0T.shape[0]
    H0 = down0T.shape[1] * down0T.shape[2]
    HP = down0T.shape[1]
    HK = down0T.shape[2]
    TOPK0 = 4
    E1 = gate1T.shape[2]
    NG = grp1.shape[0]
    TOPK1 = 6
    CAP = 128
    EPS = 1e-5
    RING = 2
    STEPS = 2 * NS
    NB = (TOPK0 * TOK + E0 * (P - 1)) // P
    WR = 3
    LEAD = 7
    BODY = 4
    BSTEP = 4

    with ExitStack() as ctx:
        def sb(name, shape, dt=F32):
            return ctx.enter_context(nc.sbuf_tensor(name, shape, dt))

        def sem(name):
            return ctx.enter_context(nc.semaphore(name))

        ps = ctx.enter_context(nc.psum_tensor("ps", [P, 8, BANK], F32))

        ident = sb("ident", [P, P])
        sel3 = sb("sel3", [P, 2 * NS], BF16)
        tri = sb("tri", [P, 2, P], BF16)
        sel64 = sb("sel64", [P, NG * P], BF16)
        xs = sb("xs", [P, TT, C])
        ctx_sb = sb("ctx_sb", [P, TOK])
        inp = sb("inp", [P, NL, DI])
        par = sb("par", [P, NL, ND, 8])
        hpar = sb("hpar", [P, NL, ND, 8])
        alog = sb("alog", [P, NL, ND, NS])
        xpr = sb("xpr", [P, NL, ND, P])
        dtp_w = sb("dtp_w", [DR, NL, DI])
        gate0 = sb("gate0", [P, KC, E0])
        gate1 = sb("gate1", [P, KC, E1])
        shu = sb("shu", [P, KC, P])
        shd = sb("shd", [P // 2, C])

        delta = sb("delta", [P, ND, TOK])
        bc3 = sb("bc3", [P, TOK], BF16)
        negA = sb("negA", [P, NL, ND, NS])
        diagD = sb("diagD", [P, ND, P])
        dtlo = sb("dtlo", [DR, TOK])
        t0 = sb("t0", [P, ND, TOK])
        t1 = sb("t1", [P, ND, TOK])
        dA = sb("dA", [P, RING, ND, HALF])
        dBu = sb("dBu", [P, RING, ND, HALF])
        hs = sb("hs", [P, RING, ND, HALF])
        hC = sb("hC", [P, RING, ND, HALF])
        xn_rows = hs[:, :, :, :].rearrange("p r d t -> p (r d t)").rearrange("p (j c) -> p j c", c=C)
        Csb = sb("Csb", [P, RING, HALF])
        Bsb = sb("Bsb", [P, RING, HALF])

        stats = sb("stats", [P, TT, 6])
        mv = sb("mv", [P, TT, 2])
        rstd = sb("rstd", [P, TT])
        expo = sb("expo", [P, TT])
        xnT = sb("xnT", [P, KC, TOK])
        gate_th = xnT
        lg = sb("lg", [P, TT, E1])
        top8 = sb("top8", [P, TT, 8])
        r0 = sb("r0", [P, TT, E1])
        r1 = sb("r1", [P, TT, E1])
        r2 = sb("r2", [P, TT, E1])
        rsum = sb("rsum", [P, TT])
        need = sb("need", [P, TT])
        first1 = sb("first1", [P, TT, E1])
        first0 = sb("first0", [P, TT, E0])
        maskb = sb("maskb", [P, TT, E1], BF16)
        w2x = dBu[:, 0, :, :].rearrange("p d (j a e) -> p (d j) a e", a=2, e=E1)

        th, pg, hx, hT = (sb(n, [P, RING, BANK]) for n in ("th", "pg", "hx", "hT"))
        xd_sb = sb("xd_sb", [P, RING, C])
        xdT = sb("xdT", [P, RING, KC, P])
        ysb = sb("ysb", [P, RING, C])
        steps = sb("steps", [P, 96])
        slot_f = sb("slot_f", [P, TOPK0, TT])
        slot_u = sb("slot_u", [P, TOPK0, TT], mybir.dt.uint32)
        wk = sb("wk", [P, TOPK0, TT])
        nblk = sb("nblk", [P, E0])
        endb = sb("endb", [P, E0])
        startb = sb("startb", [P, E0])
        big = dBu[:, :, :, :].rearrange("p r d t -> p (r d t)")
        blk_f = sb("blk_f", [P, 3, 64])
        I32 = mybir.dt.int32
        blk_rank = sb("blk_rank", [1, 64], I32)
        end_g = sb("end_g", [1, E0], I32)
        blk_need = sb("blk_need", [1, 64], I32)
        blk_ring = sb("blk_ring", [1, 64], I32)
        end_i = sb("end_i", [1, E0], I32)
        zero = ysb[:, 0, :]
        gb = [t.rearrange("p (j c) -> p j c", c=C) for t in
              (dA[:, :, :, :].rearrange("p r d t -> p (r d t)"), big, hC[:, :, :, :].rearrange("p r d t -> p (r d t)"),
               delta[:, :, :].rearrange("p d t -> p (d t)"))]
        xd = nc.dram_tensor("xd", ((NB + 1 + RING) * P, C), F32, kind="Internal").ap()
        yd = nc.dram_tensor("yd", (NB * P, C), F32, kind="Internal").ap()
        bcd = nc.dram_tensor("bcd", (2, STEPS + RING, HALF), F32, kind="Internal").ap()
        GR = 4
        GN = grp1.shape[2]
        with (nc.sbuf_tensor("ug0", [P, WR, KC, 2 * H0], F32) as ug0, nc.sbuf_tensor("dn0", [HP, WR, HK, C], F32) as dn0,
              nc.sbuf_tensor("u", [P, ND, TOK], F32) as u, nc.sbuf_tensor("du", [P, ND, TOK], F32) as du,
              nc.sbuf_tensor("y1", [P, ND, TOK], F32) as y1):
            xb = y1[:, 0, :]
            z0 = y1
        g1w = sb("g1w", [P, GR, GN])
        w_hi, w_lo = sb("w_hi", [P, RING, GN], F32R), sb("w_lo", [P, RING, GN], F32R)
        x_hi, x_lo = sb("x_hi", [P, KC, TOK], F32R), sb("x_lo", [P, KC, TOK], F32R)
        selr, w_of = sb("selr", [P, RING, P], F32R), sb("w_of", [P, TOK], F32R)
        h_hi, h_lo = sb("h_hi", [P, RING, BANK], F32R), sb("h_lo", [P, RING, BANK], F32R)

        s_par, s_ctx = sem("s_par"), sem("s_ctx")
        s_in = [sem(f"s_in{i}") for i in range(6)]
        s_w = [sem(f"s_w{i}") for i in range(WR)]
        s_xd = [sem(f"s_xd{i}") for i in range(RING)]
        s_y = [sem(f"s_y{i}") for i in range(RING)]
        s_gk = [sem(f"s_gk{k}") for k in range(TOPK0 - 1)]
        s_gj = [sem(f"s_gj{j}") for j in range(TT)]
        s_scat = [sem(f"s_scat{k}") for k in range(TOPK0)]
        s_zero, ranks_in, rows_stored = sem("s_zero"), sem("ranks_in"), sem("rows_stored")
        s_g1 = [sem(f"s_g1{i}") for i in range(GR)]
        s_store = sem("s_store")
        pe_s, act_s, dve_s, pool_s = Stage(sem("pe_s")), Stage(sem("act_s")), Stage(sem("dve_s")), Stage(sem("pool_s"))
        b_ready, c_ready = sem("b_ready"), sem("c_ready")
        da_ready, csb_ready = sem("da_ready"), sem("csb_ready")
        dbu_done, scan_done = sem("dbu_done"), sem("scan_done")
        hc_done, y_done = sem("hc_done"), sem("y_done")
        s_bcd = sem("s_bcd")
        s_b, s_c = ([sem(f"s_{n}{q}") for q in range(RING)] for n in "bc")
        w_loaded = sem("w_loaded")
        x_turned, xdT_ready = sem("x_turned"), sem("xdT_ready")
        up_done, th_done, p_done, h_done = sem("up_done"), sem("th_done"), sem("p_done"), sem("h_done")
        h_turned, hT_ready, dn_done, y_evac = sem("h_turned"), sem("hT_ready"), sem("dn_done"), sem("y_evac")
        da1, dbu1, scan1, hc1, add1 = (sem(n) for n in ("da1", "dbu1", "scan1", "hc1", "add1"))
        s_comb = sem("s_comb")
        g_g, g_v, g_w, g_th, g_p, g_q, g_h, g_dn, g_hhi, g_hlo, g_whi, g_wlo = (sem(f"g_{n}") for n in
            ("g", "v", "w", "th", "p", "q", "h", "dn", "hhi", "hlo", "whi", "wlo"))

        block = ctx.enter_context(nc.Block())

        x_t = x.rearrange("(j p) c -> p j c", p=P)
        out_t = out.rearrange("(j p) c -> p j c", p=P)

        def places(*names):
            return {n: i + 1 for i, n in enumerate(" ".join(names).split())}

        PE = places("xin0_0 xin0_1 xdbl0_0 xdbl0_1 dtp0_0 dtp0_1 y_init0 y_init1 yT0_0 yT0_1 xnT0_0 xnT0_1 logit0_0 logit0_1 pos0 xin1",
                    "xdbl1_0 xdbl1_1 dtp1_0_0 dtp1_0_1 dtp1_1_0 dtp1_1_1",
                    "yT1_0 yT1_1 xnT1_0 xnT1_1 logit1_0 logit1_1 sh_up0 sh_up1 pos1 sh_dn0 wT1_0 wT1_1 sh_dn1")
        AC = places("negA tap0_0 tap0_1 th_u0_0 th_u0_1 bc0_0 bc0_1 abs0_0 e0_0 zth0 abs0_1 e0_1 ln0_0 ln0_1 negA1 xnT0_0 xnT0_1 ex0 xin1 th_u1_0 th_u1_1 xdbl1_0 xdbl1_1",
                    "v1_0_0 v1_0_1 abs1_0 e1_0 v1_1_0 v1_1_1 abs1_1 e1_1 ln1 y1_0 y1_1",
                    "zth1_0 zth1_1 xnT1_0 xnT1_1 xhi1_0 xhi1_1 ex1_0 ex1_1 sh_th0 sh_th1 whi1_0 whi1_1")
        DVE = places("zero hpar conv0_0 conv0_1 u0_0 u0_1 zstat0 consts bc0_0 zh0 bc0_1 max0_0 w0_0 max0_1 w0_1",
                     "delta0_0 du0_0 G0 yz0_0 nstat0_0 yz0_1 nstat0_1 xn0_0 xn0_1",
                     "lsub0 sel0 slots0 blocks0 route0 conv1_0 conv1_1 u1 negA1 w1_0 w1_1 delta1 du1",
                     "zstat1_0 zstat1_1 zh1_0 zh1_1 yz1_0 yz1_1 nstat1_0 nstat1_1 xn1_0 xn1_1 sel1 sh_h0 sh_h1 route1",
                    "wlo1_0 wlo1_1 out0 out1")
        POOL = places("zero zr0 l0_1 delta0_1 du0_1 nr0_0 nr0_1 y1 zr1_0 zr1_1 nr1_0 nr1_1 xlo1_0 xlo1_1")

        def has(i, c):
            return not isinstance(i, int) or 0 <= BODY * i + c < NB

        def nth(i, c):
            return i * BODY + c

        def per(i, c, ring):
            return i * (BODY // ring) + c // ring

        BODIES = 2 * NS // BSTEP
        SLOTS = (NB - LEAD + BODY - 1) // BODY * BODY + LEAD

        def bodies(eng, body):
            for h in range(2):
                first = h * BODIES // 2
                with eng.Fori(first, first + BODIES // 2) as i:
                    body(i, h, (i - first) * BSTEP)
            with eng.Fori(BODIES, (SLOTS - LEAD) // BODY) as i:
                body(i, None, None)

        @block.sync
        def _(sp):
            sp.dma_start(ctx_sb[:, 0:HALF], ctxT[:, 0:HALF]).then_inc(s_in[0], 16)
            sp.dma_start(inp[:, :, :], in_projT.rearrange("k p d -> p k d")).then_inc(s_in[0], 16)
            sp.dma_start(par[:, :, :, :], ssm_par[:, :, :, 0:8]).then_inc(s_par, 16)
            sp.dma_start(ctx_sb[:, HALF:TOK], ctxT[:, HALF:TOK]).then_inc(s_ctx, 16)
            sp.dma_start(xs[:, :, :], x_t).then_inc(s_in[3], 16)
            sp.dma_start(alog[:, :, :, :], ssm_par[:, :, :, 8:8 + NS]).then_inc(s_in[1], 16)
            sp.dma_start(xpr[:, :, :, :], x_projT).then_inc(s_in[1], 16)
            sp.dma_start(dtp_w[:, :, :], dt_projT.rearrange("k r d -> r k d")).then_inc(s_in[1], 16)
            sp.dma_start(ident[:, :], ident_in).then_inc(s_in[2], 16)
            sp.dma_start(sel3[:, :], sel3_in).then_inc(s_in[2], 16)
            sp.dma_start(tri[:, :, :], tri_in).then_inc(s_in[4], 16)
            sp.dma_start(sel64[:, :], sel64_in).then_inc(s_in[4], 16)
            sp.dma_start(gate0[:, :, :], gate0T).then_inc(s_in[4], 16)
            sp.dma_start(gate1[:, :, :], gate1T).then_inc(s_in[4], 16)
            sp.dma_start(shu[:, :, :], sh_upT).then_inc(s_in[4], 16)
            sp.dma_start(shd[:, :], sh_down).then_inc(s_in[4], 16)
            sp.dma_start(steps[:, :], steps_in).then_inc(s_in[5], 16)
            sp.wait_ge(dve_s.sem, DVE["zero"])
            sp.dma_start(xd.rearrange("(b p) c -> p b c", p=P), zero[:, :].unsqueeze(1).to_broadcast([P, NB + 1 + RING, C])).then_inc(s_zero, 16)

            def load_expert(e, q):
                sp.dma_start(ug0[:, q, :, :], up0T[bass.ds(e, 1), :, :, :].rearrange("o p k n -> (o p) k n")).then_inc(s_w[q], 16)
                sp.dma_start(dn0[:, q, :, :], down0T[bass.ds(e, 1), :, :, :].rearrange("o p k n -> (o p) k n")).then_inc(s_w[q], 16)

            for q in range(WR):
                load_expert(q, q)
            sp.dma_start(yd.rearrange("(b p) c -> p b c", p=P), zero[:, :].unsqueeze(1).to_broadcast([P, NB, C])).then_inc(s_zero, 16)
            for q in range(WR):
                sp.wait_ge(s_w[q], 32)
                sp.sem_inc(w_loaded, 1)
            sp.wait_ge(dve_s.sem, DVE["blocks0"])
            for k in range(TOPK0):
                sp.wait_ge(s_scat[k], TT * 16)
                sp.sem_inc(ranks_in, 1)

            def next_expert(i, q):
                e = i * WR + q
                sp.wait_ge(dn_done, sp.value_load(end_i[0:1, bass.ds(e - WR, 1)], min_val=1, max_val=NB + 1))
                load_expert(e, q)
                sp.wait_ge(s_w[q], i * 32 + 32)
                sp.sem_inc(w_loaded, 1)

            with sp.Fori(1, E0 // WR) as i:
                for q in range(WR):
                    next_expert(i, q)
            for e in range(E0 // WR * WR, E0):
                next_expert(E0 // WR, e % WR)
            sp.wait_ge(dn_done, NB + 1)
            for q in range(GR):
                sp.dma_start(g1w[:, q, :], grp1[q]).then_inc(s_g1[q], 16)
            with sp.Fori(1, NG // GR) as i:
                for q in range(GR):
                    sp.wait_ge(g_wlo, i * GR + q - GR + 1)
                    sp.dma_start(g1w[:, q, :], grp1[bass.ds(i * GR + q, 1), :, :].rearrange("o p n -> (o p) n")).then_inc(s_g1[q], 16)
            for h in range(2):
                tiles = slice(h * TT // 2, (h + 1) * TT // 2)
                sp.wait_ge(dve_s.sem, DVE[f"out{h}"])
                sp.dma_start(out_t[:, tiles, :], xs[:, tiles, :]).then_inc(s_store, 16)
            sp.wait_ge(s_store, 32)

        @block.tensor
        def _(pe):
            def mark(ins, name):
                assert PE[name] == pe_s.n + 1, name
                pe_s.mark(ins)

            def project_in(k, h):
                for d in range(ND):
                    ins = pe.matmul(ps[:, 2 * d + h, :], inp[:, k, d * P:(d + 1) * P],
                                    ctx_sb[:, h * HALF:(h + 1) * HALF], start=True, stop=True)
                return ins

            def prep0():
                pe.wait_ge(s_in[0], 32)
                mark(project_in(0, 0), "xin0_0")
                pe.wait_ge(s_ctx, 16)
                mark(project_in(0, 1), "xin0_1")
                pe.wait_ge(s_in[1], 48)
                for h in range(2):
                    pe.wait_ge(dve_s.sem, DVE[f"u0_{h}"])
                    for d in range(ND):
                        ins = pe.matmul(ps[:, 4 + h, :], xpr[:, 0, d, :], u[:, d, h * HALF:(h + 1) * HALF],
                                        start=(d == 0), stop=(d == ND - 1))
                    mark(ins, f"xdbl0_{h}")
                for h in range(2):
                    pe.wait_ge(act_s.sem, AC[f"bc0_{h}"])
                    for d in range(ND):
                        ins = pe.matmul(ps[:, 2 * d + h, :], dtp_w[:, 0, d * P:(d + 1) * P],
                                        dtlo[:, h * HALF:(h + 1) * HALF], start=True, stop=True)
                    mark(ins, f"dtp0_{h}")

            def xdbl1(h):
                pe.wait_ge(act_s.sem, AC["xdbl1_0"] if h else AC["th_u1_1"])
                pe.wait_ge(dve_s.sem, DVE["u1"])
                for d in range(ND):
                    ins = pe.matmul(ps[:, 7, :], xpr[:, 1, d, :], u[:, d, h * HALF:(h + 1) * HALF],
                                    start=(d == 0), stop=(d == ND - 1))
                mark(ins, f"xdbl1_{h}")

            def dtp1(d, h):
                before = ("xdbl1_1", "v1_0_0", "v1_0_1", "v1_1_0")[2 * d + h]
                pe.wait_ge(act_s.sem, AC[before])
                mark(pe.matmul(ps[:, 7, :], dtp_w[:, 1, d * P:(d + 1) * P], xb[0:DR, h * HALF:(h + 1) * HALF],
                               start=True, stop=True), f"dtp1_{d}_{h}")

            def rep(h, n, q, S):
                rhs = bc3[:, h * HALF:(h + 1) * HALF]
                pe.wait_ge(dbu_done, S + 1)
                pe.matmul(ps[:, 4 + q, :], sel3[:, bass.ds(n, 1)].to_broadcast([P, P]), rhs,
                          start=True, stop=True).then_inc(b_ready, 1)
                pe.wait_ge(csb_ready, S + 1)
                pe.matmul(ps[:, 6 + q, :], sel3[:, bass.ds(n + NS, 1)].to_broadcast([P, P]), rhs,
                          start=True, stop=True).then_inc(c_ready, 1)

            def ysum(h, q, S):
                pe.wait_ge(hc_done, S + RING + 1)
                for d in range(ND):
                    ins = pe.matmul(ps[:, 2 * h + d, :], ident[:, :], hC[:, q, d, :],
                                    start=False, stop=True, skip_group_check=True)
                ins.then_inc(y_done, 1)

            def mixer0():
                pe.wait_ge(dve_s.sem, DVE["bc0_1"])
                for q in range(RING):
                    rep(0, q, q, q)
                pe.wait_ge(dve_s.sem, DVE["consts"])
                pe.wait_ge(dve_s.sem, DVE["max0_1"])
                for h in range(2):
                    for d in range(ND):
                        ins = pe.matmul(ps[:, 2 * h + d, :], diagD[:, d, :],
                                        u[:, d, h * HALF:(h + 1) * HALF], start=True, stop=True)
                    mark(ins, f"y_init{h}")
                for h in range(2):
                    base = h * NS
                    with pe.Fori(1, NS // RING) as j:
                        for q in range(RING):
                            rep(h, j * RING + q, q, base + j * RING + q)
                            ysum(h, q, base + j * RING + q - RING)
                    for q in range(RING):
                        if h == 0:
                            rep(1, q, q, NS + q)
                        elif q == RING - 1:
                            turn_y(0, 0)
                        ysum(h, q, base + NS - RING + q)

            def transpose_in(k):
                for h in range(k == 0, 2):
                    turn_y(k, h)
                turn_xn(k)

            def turn_y(k, h):
                    pe.wait_ge(dve_s.sem, DVE[f"yz{k}_{h}"])
                    for j in range(h * TT // 2, (h + 1) * TT // 2):
                        for d in range(ND):
                            ins = pe.transpose(ps[:, 4 + j // 2, (j % 2) * C + d * P:(j % 2) * C + (d + 1) * P],
                                               t0[:, d, j * P:(j + 1) * P], ident[:, :])
                    mark(ins, f"yT{k}_{h}")
            def turn_xn(k):
                for h in range(2):
                    pe.wait_ge(dve_s.sem, DVE[f"xn{k}_{h}"])
                    for j in range(h * TT // 2, (h + 1) * TT // 2):
                        for c in range(KC):
                            ins = pe.transpose(ps[:, 2 * h + c, (j % 4) * P:(j % 4 + 1) * P],
                                               xn_rows[:, j, c * P:(c + 1) * P],
                                               ident[:, :])
                    mark(ins, f"xnT{k}_{h}")

            def logits(k, gate, E):
                pe.wait_ge(s_in[4], 6 * 16)
                for h in range(2):
                    pe.wait_ge(act_s.sem, AC[f"xnT{k}_{h}"])
                    for j in range(TT // 2):
                        t = (h * TT // 2 + j) * P
                        for c in range(KC):
                            ins = pe.matmul(ps[:, 4 + h, j * E:(j + 1) * E], xnT[:, c, t:t + P], gate[:, c, :],
                                            start=(c == 0), stop=(c == KC - 1))
                    mark(ins, f"logit{k}_{h}")

            def table(t, i, c, high):
                return pe.value_load(t[0:1, bass.ds(nth(i, c), 1)], min_val=0, max_val=high)

            ug_flat = ug0[:, :, :, :].rearrange("p w k n -> p (w k n)")
            dn_flat = dn0[:, :, :, :].rearrange("p w k n -> p (w k n)")

            def expert_of(i, c):
                if not has(i, c):
                    return None
                return table(blk_need, i, c, E0), table(blk_ring, i, c, WR - 1)

            def up(i, c, held, w):
                if c >= RING or not isinstance(i, int):
                    pe.wait_ge(h_done, nth(i, c) - RING + 1)
                pe.wait_ge(xdT_ready, nth(i, c) + 1)
                pe.wait_ge(w_loaded, held)
                for part in range(2):
                    for kc in range(KC):
                        ins = pe.matmul(ps[:, 2 * part + c % 2, 0:H0], xdT[:, c % 2, kc, :],
                                        ug_flat[:, bass.ds(w * (KC * 2 * H0) + (kc * 2 + part) * H0, H0)],
                                        start=(kc == 0), stop=(kc == KC - 1))
                ins.then_inc(up_done, 1)

            def turn_x(i, c):
                if not has(i, c):
                    return
                pe.wait_ge(s_xd[c % RING], per(i, c, RING) * 16 + 16)
                if c >= 1 or not isinstance(i, int):
                    pe.wait_ge(xdT_ready, nth(i, c))
                for kc in range(KC):
                    ins = pe.transpose(ps[:, 6, kc * P:(kc + 1) * P], xd_sb[:, c % RING, kc * P:(kc + 1) * P], ident[:, :])
                ins.then_inc(x_turned, 1)

            def turn_h(i, c):
                if not has(i, c):
                    return
                pe.wait_ge(h_done, nth(i, c) + 1)
                if c >= 1 or not isinstance(i, int):
                    pe.wait_ge(hT_ready, nth(i, c))
                for m in range(HK):
                    ins = pe.transpose(ps[0:HP, 4, m * P:(m + 1) * P], hx[:, c % 2, m * HP:(m + 1) * HP], ident[:, :])
                ins.then_inc(h_turned, 1)

            def down(i, c, w):
                pe.wait_ge(hT_ready, nth(i, c) + 1)
                pe.wait_ge(y_evac, nth(i, c) + 1)
                for m in range(HK):
                    ins = pe.matmul(ps[:, 5, 0:C], hT[0:HP, c % 2, m * P:(m + 1) * P],
                                    dn_flat[:, bass.ds(w * (HK * C) + m * C, C)],
                                    start=(m == 0), stop=(m == HK - 1))
                ins.then_inc(dn_done, 1)

            def body(i, h, n):
                this = expert_of(i, LEAD)
                for r in range(BODY):
                    c = r + LEAD
                    up(i, c, *this)
                    if r < BODY - 1:
                        this = expert_of(i, c + 1)
                    w = table(blk_ring, i, c - 2, WR - 1)
                    turn_x(i, c + 1)
                    turn_h(i, c - 1)
                    down(i, c - 2, w)

            def ffn0():
                prepare = {(1, 0): (xdbl1, 0), (1, 1): (xdbl1, 1), (2, 0): (dtp1, 0, 0), (2, 1): (dtp1, 0, 1),
                           (3, 0): (dtp1, 1, 0), (3, 1): (dtp1, 1, 1)}

                def also(s, at):
                    if (s, at) in prepare:
                        prepare[s, at][0](*prepare[s, at][1:])

                pe.wait_ge(dve_s.sem, DVE["blocks0"])
                pe.wait_ge(act_s.sem, AC["xin1"])
                pe.sem_inc(dn_done, 1)
                turn_x(0, 0)
                for s in range(LEAD):
                    up(0, s, *expert_of(0, s))
                    also(s, 0)
                    turn_x(0, s + 1)
                    turn_h(0, s - 1)
                    if s >= 2:
                        down(0, s - 2, table(blk_ring, 0, s - 2, WR - 1))
                    also(s, 1)
                bodies(pe, body)
                for s in range(SLOTS, NB + 2):
                    turn_h(0, s - 1)
                    down(0, s - 2, table(blk_ring, 0, s - 2, WR - 1))

            def shared_up1():
                for h in range(2):
                    for c in range(KC):
                        ins = pe.matmul(ps[:, 6 + h, :], shu[:, c, :], xnT[:, c, h * HALF:(h + 1) * HALF],
                                        start=(c == 0), stop=(c == KC - 1))
                    mark(ins, f"sh_up{h}")

            def shared_down1(h):
                pe.wait_ge(dve_s.sem, DVE[f"sh_h{h}"])
                for t in range(4):
                    j = 4 * h + t
                    ins = pe.matmul(ps[:, j // 2, (j % 2) * C:(j % 2 + 1) * C], hT[0:P // 2, h, t * P:(t + 1) * P],
                                    shd[:, :], start=(j % 2 == 0), stop=True, skip_group_check=True)
                mark(ins, f"sh_dn{h}")

            def parts(dst, a_hi, a_lo, b_hi, b_lo, where, start):
                for m, (at_a, at_b) in enumerate(where):
                    for p, (a, b) in enumerate(((a_hi, b_hi), (a_hi, b_lo), (a_lo, b_hi))):
                        ins = pe.matmul(dst, a[at_a], b[at_b], start=start and m + p == 0,
                                        stop=m == len(where) - 1 and p == 2, skip_group_check=not start)
                return ins

            def up1(q, h, n):
                if n is not None:
                    pe.wait_ge(g_p, n)
                for part, done in ((0, g_g), (1, g_v)):
                    if part == 1 and n is not None:
                        pe.wait_ge(g_q, n)
                    ins = parts(ps[:, 4 + part, :], w_hi, w_lo, x_hi, x_lo,
                                [((slice(None), q % RING, slice((2 * c + part) * P, (2 * c + part + 1) * P)),
                                  (slice(None), c, slice(h * HALF, (h + 1) * HALF))) for c in range(KC)], True)
                    ins.then_inc(done, 1)
                if n is not None:
                    pe.wait_ge(g_h, n)
                pe.matmul(ps[:, 6, :], selr[:, q % RING, :], w_of[:, h * HALF:(h + 1) * HALF],
                          start=True, stop=True).then_inc(g_w, 1)

            def down1(q, h, n):
                pe.wait_ge(g_hlo, n)
                for t in range(4):
                    j = 4 * h + t
                    ins = parts(ps[:, j // 2, (j % 2) * C:(j % 2 + 1) * C], h_hi, h_lo, w_hi, w_lo,
                                [((slice(None), h, slice(t * P, (t + 1) * P)),
                                  (slice(None), q % RING, slice(4 * P, 4 * P + C)))], False)
                ins.then_inc(g_dn, 1)

            def ffn1():
                pe.wait_ge(pool_s.sem, POOL["xlo1_1"])
                pe.wait_ge(dve_s.sem, DVE["wlo1_1"])
                def group(i, q):
                    pe.wait_ge(g_wlo, i * GR + q + 1)
                    for h in range(2):
                        n = (i * GR + q) * 2 + h
                        up1(q, h, n + 1)
                        if not isinstance(n, int) or n > 0:
                            down1((q + h - 1) % GR, 1 - h, n)

                for q in range(GR):
                    group(0, q)
                with pe.Fori(1, NG // GR) as i:
                    for q in range(GR):
                        group(i, q)
                down1(GR - 1, 1, 2 * NG)

            def earlier(k, E):
                pe.wait_ge(dve_s.sem, DVE[f"sel{k}"])
                mk = maskb[:, :, :].rearrange("p j e -> p (j e)")
                for j in range(TT):
                    for i in range(j + 1):
                        ins = pe.matmul(ps[:, 5, j * E:(j + 1) * E], tri[:, 0 if i == j else 1, :], mk[:, i * E:(i + 1) * E],
                                        start=(i == 0), stop=(i == j))
                if k == 0:
                    for i in range(TT):
                        ins = pe.matmul(ps[:, 5, TT * E:(TT + 1) * E], tri[:, 1, :], mk[:, i * E:(i + 1) * E],
                                        start=(i == 0), stop=(i == TT - 1))
                mark(ins, f"pos{k}")

            prep0()
            pe.sem_inc(y_done, RING)
            mixer0()
            transpose_in(0)
            logits(0, gate0, E0)
            earlier(0, E0)
            project_in(1, 0)
            mark(project_in(1, 1), "xin1")
            ffn0()
            transpose_in(1)
            logits(1, gate1, E1)
            shared_up1()
            earlier(1, E1)
            shared_down1(0)
            pe.wait_ge(dve_s.sem, DVE["route1"])
            for h in range(2):
                for j in range(4):
                    ins = pe.transpose(ps[:, 6 + h, j * P:(j + 1) * P],
                                       w2x[:, 4 * h + j, :, :].rearrange("p a e -> p (a e)"), ident[:, :])
                mark(ins, f"wT1_{h}")
            shared_down1(1)
            ffn1()

        @block.scalar
        def _(act):
            def mark(ins, name):
                assert AC[name] == act_s.n + 1, name
                act_s.mark(ins)

            def prep0():
                halves = [slice(h * HALF, (h + 1) * HALF) for h in range(2)]
                act.wait_ge(dve_s.sem, DVE["hpar"])
                for h, t in enumerate(halves):
                    act.wait_ge(pe_s.sem, PE[f"xin0_{h}"])
                    for d in range(ND):
                        ins = act.activation(u[:, d, t], ps[:, 2 * d + h, :], ACT.Identity, scale=hpar[:, 0, d, 3:4],
                                             bias=hpar[:, 0, d, 4:5])
                    mark(ins, f"tap0_{h}")
                for h, t in enumerate(halves):
                    act.wait_ge(dve_s.sem, DVE[f"conv0_{h}"])
                    mark(act.activation(t0[:, :, t], u[:, :, t], ACT.Tanh), f"th_u0_{h}")
                for h, t in enumerate(halves):
                    act.wait_ge(pe_s.sem, PE[f"xdbl0_{h}"])
                    act.activation(dtlo[:, t], ps[0:DR, 4 + h, :], ACT.Copy)
                    mark(act.activation(bc3[:, t], ps[:, 4 + h, :], ACT.Copy), f"bc0_{h}")
                for h, t in enumerate(halves):
                    act.wait_ge(pe_s.sem, PE[f"dtp0_{h}"])
                    for d in range(ND):
                        ins = act.activation(t1[:, d, t], ps[:, 2 * d + h, :], ACT.Abs, bias=par[:, 0, d, 5:6])
                    mark(ins, f"abs0_{h}")
                    act.wait_ge(act_s.sem, AC[f"abs0_{h}"])
                    mark(act.activation(t0[:, :, t], t1[:, :, t], ACT.Exp, scale=-1.0), f"e0_{h}")
                    if h == 0:
                        act.wait_ge(dve_s.sem, DVE["zh0"])
                        mark(act.activation(gate_th[:, :, :], z0[:, :, :], ACT.Tanh), "zth0")
                for h, t in enumerate(halves):
                    act.wait_ge(act_s.sem, AC[f"e0_{h}"])
                    mark(act.activation(t1[:, :, t], t0[:, :, t], ACT.Ln, bias=1.0), f"ln0_{h}")

            def mixer0():
                for h in range(2):
                    if h == 1:
                        act.wait_ge(pool_s.sem, POOL["delta0_1"])
                    base = h * NS
                    with act.Fori(0, NS // RING) as j:
                        for q in range(RING):
                            n = j * RING + q
                            S = n + base
                            act.wait_ge(scan_done, S + 1)
                            decay(0, h, n, q).then_inc(da_ready, 1)
                            act.wait_ge(c_ready, S + 1)
                            act.wait_ge(hc_done, S + 1)
                            act.activation(Csb[:, q, :], ps[:, 6 + q, :], ACT.Copy).then_inc(csb_ready, 1)

            def decay(k, h, n, q):
                for d in range(ND):
                    ins = act.activation(
                        dA[:, q, d, :].rearrange("p (b l) -> p b l", b=2)[:, :, 1:L],
                        delta[:, d, h * HALF:(h + 1) * HALF].rearrange("p (b l) -> p b l", b=2)[:, :, 1:L],
                        ACT.Exp, scale=negA[:, k, d, bass.ds(n, 1)])
                return ins

            def take_xn(k):
                for h in range(2):
                    act.wait_ge(pe_s.sem, PE[f"xnT{k}_{h}"])
                    mark(act.activation(xnT[:, :, h * HALF:(h + 1) * HALF], ps[:, 2 * h:2 * h + 2, :], ACT.Copy), f"xnT{k}_{h}")

            act.wait_ge(s_in[1], 48)
            ins = act.activation(negA[:, 0, :, :], alog[:, 0, :, :], ACT.Exp)
            mark(ins, "negA")
            prep0()
            mark(act.activation(negA[:, 1, :, :], alog[:, 1, :, :], ACT.Exp), "negA1")
            act.wait_ge(dve_s.sem, DVE["delta0_0"])
            act.sem_inc(csb_ready, RING)
            act.wait_ge(dve_s.sem, DVE["consts"])
            act.wait_ge(pool_s.sem, POOL["zero"])
            mixer0()

            take_xn(0)
            act.wait_ge(dve_s.sem, DVE["lsub0"])
            mark(act.activation(r0[:, :, :].rearrange("p j e -> p (j e)")[:, 0:TT * E0],
                                r1[:, :, :].rearrange("p j e -> p (j e)")[:, 0:TT * E0], ACT.Exp), "ex0")

            def take_xin1():
                act.wait_ge(pe_s.sem, PE["xin1"])
                mark(act.activation(t0[:, :, :].rearrange("p d (h t) -> p (d h) t", h=2), ps[:, 0:4, :], ACT.Copy), "xin1")

            def tanh_u1(d):
                act.wait_ge(dve_s.sem, DVE[f"conv1_{d}"])
                mark(act.activation(t1[:, d, :], u[:, d, :], ACT.Tanh), f"th_u1_{d}")

            def take_xdbl1(h):
                act.wait_ge(pe_s.sem, PE[f"xdbl1_{h}"])
                mark(act.activation(xb[:, h * HALF:(h + 1) * HALF], ps[:, 7, :], ACT.Copy), f"xdbl1_{h}")

            def take_dtp1(d, h):
                act.wait_ge(pe_s.sem, PE[f"dtp1_{d}_{h}"])
                mark(act.activation(delta[:, d, h * HALF:(h + 1) * HALF], ps[:, 7, :], ACT.Identity,
                                    bias=par[:, 1, d, 5:6]), f"v1_{d}_{h}")

            def exp1(d):
                act.wait_ge(act_s.sem, AC[f"v1_{d}_1"])
                mark(act.activation(t1[:, d, :], delta[:, d, :], ACT.Abs), f"abs1_{d}")
                act.wait_ge(act_s.sem, AC[f"abs1_{d}"])
                mark(act.activation(t0[:, d, :], t1[:, d, :], ACT.Exp, scale=-1.0), f"e1_{d}")

            def ln1():
                act.wait_ge(act_s.sem, AC["e1_1"])
                mark(act.activation(t1[:, :, :], t0[:, :, :], ACT.Ln, bias=1.0), "ln1")

            def y_start1(d):
                act.wait_ge(s_bcd, 4 * 16)
                act.wait_ge(pe_s.sem, PE["dtp1_1_1"])
                mark(act.activation(y1[:, d, :], u[:, d, :], ACT.Copy, scale=par[:, 1, d, 6:7]), f"y1_{d}")

            def load_rows(i, c):
                if isinstance(i, int):
                    act.wait_ge(ranks_in, act.value_load(blk_rank[0:1, c:c + 1], min_val=1, max_val=TOPK0))
                act.dma_start(xd_sb[:, c % RING, :], xd[bass.ds(nth(i, c) * P, P), :]).then_inc(s_xd[c % RING], 16)

            def gate(i, c):
                if not has(i, c):
                    return
                act.wait_ge(up_done, nth(i, c) + 1)
                if c >= RING or not isinstance(i, int):
                    act.wait_ge(p_done, nth(i, c) - RING + 1)
                act.activation(th[:, c % 2, 0:H0], ps[:, 2 + c % 2, 0:H0], ACT.Tanh, scale=0.5).then_inc(th_done, 1)

            def take_xT(i, c):
                if not has(i, c):
                    return
                act.wait_ge(x_turned, nth(i, c) + 1)
                if c >= RING or not isinstance(i, int):
                    act.wait_ge(up_done, nth(i, c) - RING + 1)
                act.activation(xdT[:, c % 2, :, :].rearrange("p k t -> p (k t)"), ps[:, 6, 0:C], ACT.Copy).then_inc(xdT_ready, 1)
                if not isinstance(i, int):
                    load_rows(i, c + RING)

            def take_hT(i, c):
                if not has(i, c):
                    return
                act.wait_ge(h_turned, nth(i, c) + 1)
                if c >= 1 or not isinstance(i, int):
                    act.wait_ge(dn_done, nth(i, c))
                act.activation(hT[0:HP, c % 2, :], ps[0:HP, 4, :], ACT.Copy).then_inc(hT_ready, 1)

            def take_y(i, c):
                if not has(i, c):
                    return
                act.wait_ge(dn_done, nth(i, c) + 2)
                act.wait_ge(s_y[c % 2], per(i, c, 2) * 16 + 16)
                act.activation(ysb[:, c % 2, :], ps[:, 5, 0:C], ACT.Copy).then_inc(y_evac, 1)
                act.wait_ge(y_evac, nth(i, c) + 2)
                act.dma_start(yd[bass.ds(nth(i, c) * P, P), :], ysb[:, c % 2, :]).then_inc(s_y[c % 2], 16)

            def load_row(row, t, q):
                dst, done = ((Bsb, s_b), (Csb, s_c))[row]
                act.dma_start(dst[:, q, :], bcd[row, bass.ds(t, 1), :].to_broadcast([P, HALF])).then_inc(done[q], 16)

            def decay1(i, h, n, m):
                act.wait_ge(scan1, i * BSTEP + m + 1)
                decay(1, h, n + m, m % 2).then_inc(da1, 1)

            def body(i, h, n):
                for r in range(BODY):
                    c = r + LEAD
                    gate(i, c)
                    take_xT(i, c + 1)
                    take_hT(i, c - 1)
                    if h is not None:
                        decay1(i, h, n, r)
                    take_y(i, c - 2)
                    if h is not None:
                        t = i * BSTEP + r
                        act.wait_ge(hc1, t + 2)
                        load_row(1, t + 1, (r + 1) % RING)
                        act.wait_ge(dbu1, t + RING + 1)
                        load_row(0, t + RING, r % RING)

            def first_rows():
                act.wait_ge(s_bcd, 4 * 16)
                load_row(0, 0, 0)
                load_row(1, 0, 0)
                load_row(0, 1, 1)

            prepare = {(0, 0): [(tanh_u1, 0), (tanh_u1, 1)], (1, 0): [(take_xdbl1, 0)], (1, 1): [(take_xdbl1, 1)],
                       (2, 0): [(take_dtp1, 0, 0)], (2, 1): [(take_dtp1, 0, 1), (exp1, 0)], (3, 0): [(take_dtp1, 1, 0)],
                       (3, 1): [(take_dtp1, 1, 1), (exp1, 1)], (4, 1): [(ln1,)], (5, 1): [(first_rows,), (y_start1, 0)], (6, 1): [(y_start1, 1)]}

            def also(s, at):
                for f, *where in prepare.get((s, at), ()):
                    f(*where)

            take_xin1()
            act.sem_inc(y_evac, 1)
            for q in range(RING):
                act.sem_inc(s_y[q], 16)
            act.wait_ge(dve_s.sem, DVE["blocks0"])
            act.wait_ge(s_zero, 32)
            EARLY = 2
            load_rows(0, 0)
            take_xT(0, 0)
            load_rows(0, 1)
            for s in range(LEAD):
                gate(0, s)
                also(s, 0)
                take_xT(0, s + 1)
                if s == EARLY:
                    load_rows(0, s + RING)
                if s >= EARLY:
                    load_rows(0, s + 1 + RING)
                take_hT(0, s - 1)
                take_y(0, s - 2)
                also(s, 1)
                if s < EARLY:
                    load_rows(0, s + RING)
            act.wait_ge(ranks_in, TOPK0)
            act.wait_ge(dve_s.sem, DVE["delta1"])
            bodies(act, body)
            for s in range(SLOTS, NB + 2):
                take_hT(0, s - 1)
                take_y(0, s - 2)
            for q in range(RING):
                act.wait_ge(s_y[q], ((NB + 1 - q) // 2) * 16 + 16)
            act.sem_inc(y_evac, 2)

            def weights_hi(i, q, free=None):
                act.wait_ge(s_g1[q], i * 16 + 16)
                if free is not None:
                    act.wait_ge(g_dn, free)
                act.activation(selr[:, q % RING, :], sel64[:, bass.ds((i * GR + q) * P, P)], ACT.Copy)
                act.activation(w_hi[:, q % RING, :], g1w[:, q, :], ACT.Copy).then_inc(g_whi, 1)

            weights_hi(0, 0)
            weights_hi(0, 1)
            for h in range(2):
                t = slice(h * HALF, (h + 1) * HALF)
                act.wait_ge(dve_s.sem, DVE[f"zh1_{h}"])
                mark(act.activation(t1[:, :, t], t0[:, :, t], ACT.Tanh), f"zth1_{h}")
            take_xn(1)
            for h in range(2):
                t = slice(h * HALF, (h + 1) * HALF)
                act.wait_ge(act_s.sem, AC[f"xnT1_{h}"])
                mark(act.activation(x_hi[:, :, t], xnT[:, :, t], ACT.Copy), f"xhi1_{h}")
            for h in range(2):
                act.wait_ge(pe_s.sem, PE[f"logit1_{h}"])
                mark(act.activation(r0[:, 4 * h:4 * h + 4, :].rearrange("p j e -> p (j e)"), ps[:, 4 + h, 0:4 * E1],
                                    ACT.Exp, scale=-1.0), f"ex1_{h}")
            for h in range(2):
                act.wait_ge(pe_s.sem, PE[f"sh_up{h}"])
                mark(act.activation(th[P // 2:P, h, :], ps[P // 2:P, 6 + h, :], ACT.Tanh, scale=0.5), f"sh_th{h}")
            for h in range(2):
                act.wait_ge(pe_s.sem, PE[f"wT1_{h}"])
                mark(act.activation(w_of[:, h * HALF:(h + 1) * HALF], ps[:, 6 + h, :], ACT.Copy), f"whi1_{h}")

            def half_group(h, n):
                act.wait_ge(g_g, n + 1)
                act.wait_ge(g_p, n + 1)
                act.activation(th[:, h, :], ps[:, 4, :], ACT.Tanh, scale=0.5).then_inc(g_th, 1)
                act.wait_ge(g_h, n + 2)
                if not isinstance(n, int) or n >= RING:
                    act.wait_ge(g_dn, n - RING + 1)
                act.activation(h_hi[:, h, :], hT[:, h, :], ACT.Copy).then_inc(g_hhi, 1)

            def group(i, q):
                for h in range(2):
                    half_group(h, (i * GR + q) * 2 + h)
                    if h == 0 and (not isinstance(i, int) or i or q):
                        weights_hi(i + (q + 1) // GR, (q + 1) % GR, (i * GR + q) * 2)

            for q in range(GR):
                group(0, q)
            with act.Fori(1, NG // GR - 1) as i:
                for q in range(GR):
                    group(i, q)
            last = NG // GR - 1
            for q in range(GR - 1):
                group(last, q)
            for h in range(2):
                half_group(h, (NG - 1) * 2 + h)

        @block.gpsimd
        def _(pool):
            for q in range(RING):
                for d in range(ND):
                    ins = pool.memset(dA[:, q, d, :].rearrange("p (b l) -> p b l", b=2)[:, :, 0:1], 0.0)
            pool.memset(expo[:, :], -0.5)
            pool.memset(first0[:, :, :], 1.0)
            pool.memset(first1[:, :, :], 1.0).then_inc(pool_s.sem, 1)
            pool.sem_inc(hc_done, RING)

            def rstd_of(stat, tiles=slice(0, TT)):
                pool.wait_ge(dve_s.sem, DVE[stat])
                pool.wait_ge(pool_s.sem, POOL["zero"])
                pool.tensor_tensor(rstd[:, tiles], mv[:, tiles, 1], expo[:, tiles], ALU.pow).then_inc(pool_s.sem, 1)

            def times_c(q):
                return pool.tensor_tensor(hC[:, q, :, :], hs[:, q, :, :],
                                          Csb[:, q, :].unsqueeze(1).to_broadcast([P, ND, HALF]), ALU.mult)

            rstd_of("zstat0")
            t = slice(HALF, TOK)
            pool.wait_ge(dve_s.sem, DVE["w0_1"])
            pool.wait_ge(act_s.sem, AC["ln0_1"])
            pool.tensor_tensor(t1[:, :, t], t1[:, :, t], du[:, :, t], ALU.subtract).then_inc(pool_s.sem, 1)
            pool.wait_ge(pool_s.sem, POOL["l0_1"])
            pool.tensor_tensor(delta[:, :, t], delta[:, :, t], t1[:, :, t], ALU.add).then_inc(pool_s.sem, 1)
            pool.wait_ge(pool_s.sem, POOL["delta0_1"])
            pool.tensor_tensor(du[:, :, t], delta[:, :, t], u[:, :, t], ALU.mult).then_inc(pool_s.sem, 1)
            with pool.Fori(0, STEPS // RING) as i:
                for q in range(RING):
                    S = i * RING + q
                    pool.wait_ge(scan_done, S + RING + 1)
                    pool.wait_ge(csb_ready, S + RING + 1)
                    pool.wait_ge(y_done, S + 1)
                    times_c(q).then_inc(hc_done, 1)
            for h in range(2):
                rstd_of(f"nstat0_{h}", slice(4 * h, 4 * h + 4))
            pool.wait_ge(dve_s.sem, DVE["slots0"])
            pool.wait_ge(s_zero, 32)
            for k in range(TOPK0):
                for j in range(TT):
                    pool.indirect_dma_start(xd, bass.IndirectOffsetOnAxis(ap=slot_u[:, k, j:j + 1], axis=0),
                                            xn_rows[:, j, :], None).then_inc(s_scat[k], 16)
            pool.wait_ge(act_s.sem, AC["xdbl1_1"])
            for row in range(2):
                src = xb[32 + NS * row:32 + NS * (row + 1)]
                pool.dma_start(bcd[row, 0:STEPS].rearrange("(h n) t -> n h t", h=2),
                               src.rearrange("n (h t) -> n h t", h=2)).then_inc(s_bcd, 16)
                pool.dma_start(bcd[row, STEPS:STEPS + RING], src[0:RING, 0:HALF]).then_inc(s_bcd, 16)
            pool.sem_inc(hc1, RING)
            pool.wait_ge(act_s.sem, AC["y1_1"])
            for h in range(2):
                with pool.Fori(0, NS // RING) as i:
                    for q in range(RING):
                        t = i * RING + q + h * NS
                        pool.wait_ge(scan1, t + RING + 1)
                        pool.wait_ge(s_c[q], (i + h * (NS // RING)) * 16 + 16)
                        times_c(q).then_inc(hc1, 1)
                        pool.wait_ge(hc1, t + RING + 1)
                        y = y1[:, :, h * HALF:(h + 1) * HALF]
                        pool.tensor_tensor(y, y, hC[:, q, :, :], ALU.add).then_inc(add1, 1)
                        pool.wait_ge(add1, t + 1)
            pool.sem_inc(pool_s.sem, 1)
            stored = [pool.value_load(end_g[0:1, e:e + 1], min_val=3, max_val=NB + 3) for e in range(E0 - TOPK0, E0 - 1)]
            for k in range(TOPK0):
                pool.wait_ge(y_evac, stored[k] if k < TOPK0 - 1 else NB + 3)
                pool.sem_inc(rows_stored, 1)
                pool.wait_ge(rows_stored, k + 1)
                for j in range(TT):
                    pool.indirect_dma_start(gb[k][:, j, :], None, yd,
                                            bass.IndirectOffsetOnAxis(ap=slot_u[:, k, j:j + 1], axis=0)
                                            ).then_inc(s_gk[k] if k < TOPK0 - 1 else s_gj[j], 16)
            for h in range(2):
                rstd_of(f"zstat1_{h}", slice(4 * h, 4 * h + 4))
            for h in range(2):
                rstd_of(f"nstat1_{h}", slice(4 * h, 4 * h + 4))
            for h in range(2):
                t = slice(h * HALF, (h + 1) * HALF)
                pool.wait_ge(act_s.sem, AC[f"xhi1_{h}"])
                pool.tensor_tensor(x_lo[:, :, t], xnT[:, :, t], x_hi[:, :, t].bitcast(F32), ALU.subtract).then_inc(pool_s.sem, 1)
            with pool.Fori(0, NG // GR) as i:
                for q in range(GR):
                    pool.wait_ge(g_whi, i * GR + q + 1)
                    pool.tensor_tensor(w_lo[:, q % RING, :], g1w[:, q, :], w_hi[:, q % RING, :].bitcast(F32), ALU.subtract).then_inc(g_wlo, 1)

        @block.vector
        def _(dve):
            dch = Stage(sem("dch"))

            def link(ins):
                dch.mark(ins)
                dve.wait_ge(dch.sem, dch.n)

            def mark(ins, name, wait=False):
                assert DVE[name] == dve_s.n + 1, name
                dve_s.mark(ins)
                if wait:
                    dve.wait_ge(dve_s.sem, dve_s.n)

            def taps(k, d, dst, src):
                for s in range(1, 4):
                    ins = dve.scalar_tensor_tensor(dst[:, :, s:L], src[:, :, 0:L - s], hpar[:, k, d, 3 - s:4 - s],
                                                   dst[:, :, s:L], ALU.mult, ALU.add)
                    if s < 3:
                        link(ins)
                return ins

            halves = [slice(h * HALF, (h + 1) * HALF) for h in range(2)]

            def prep0():
                dve.wait_ge(s_in[3], 16)
                for j in range(TT // 2):
                    dve.bn_stats(stats[:, j, :], xs[:, j, :])
                for h, t in enumerate(halves):
                    dve.wait_ge(act_s.sem, AC[f"tap0_{h}"])
                    for d in range(ND):
                        ins = taps(0, d, u[:, d, t].rearrange("p (b l) -> p b l", b=2),
                                   ps[:, 2 * d + h, :].rearrange("p (b l) -> p b l", b=2))
                    mark(ins, f"conv0_{h}")
                for h, t in enumerate(halves):
                    dve.wait_ge(act_s.sem, AC[f"th_u0_{h}"])
                    mark(dve.scalar_tensor_tensor(u[:, :, t], t0[:, :, t], 1.0, u[:, :, t], ALU.add, ALU.mult), f"u0_{h}")
                norm_stats("zstat0", range(TT), TT // 2)
                constants()
                for h, t in enumerate(halves):
                    if h == 1:
                        dve.wait_ge(pool_s.sem, POOL["zr0"])
                        link(dve.tensor_scalar(rstd[:, :], rstd[:, :], 0.5, None, ALU.mult))
                        for j in range(TT):
                            ins = half_norm(z0, j)
                        mark(ins, "zh0")
                    dve.wait_ge(act_s.sem, AC[f"bc0_{h}"])
                    link(dve.tensor_tensor(du[64:P, 0, t], ps[64:P, 4 + h, :], bc3[64:P, t], ALU.subtract))
                    link(dve.tensor_copy(bc3[64:P, t], du[64:P, 0, t]))
                    mark(dve.tensor_tensor(bc3[96:P, t], du[96:P, 0, t], bc3[96:P, t], ALU.subtract), f"bc0_{h}")
                for h, t in enumerate(halves):
                    dve.wait_ge(act_s.sem, AC[f"abs0_{h}"])
                    for d in range(ND):
                        ins = dve.tensor_scalar(delta[:, d, t], ps[:, 2 * d + h, :], par[:, 0, d, 5:6], 0.0, ALU.add, ALU.max)
                    mark(ins, f"max0_{h}")
                    dve.wait_ge(act_s.sem, AC[f"e0_{h}"])
                    link(dve.tensor_scalar(du[:, :, t], t0[:, :, t], 1.0, None, ALU.add))
                    mark(dve.scalar_tensor_tensor(du[:, :, t], du[:, :, t], 1.0, t0[:, :, t], ALU.subtract, ALU.subtract), f"w0_{h}")
                t = halves[0]
                dve.wait_ge(act_s.sem, AC["ln0_0"])
                link(dve.tensor_tensor(t1[:, :, t], t1[:, :, t], du[:, :, t], ALU.subtract))
                mark(dve.tensor_tensor(delta[:, :, t], delta[:, :, t], t1[:, :, t], ALU.add), "delta0_0", True)
                mark(dve.tensor_tensor(du[:, :, t], delta[:, :, t], u[:, :, t], ALU.mult), "du0_0", True)
                dve.wait_ge(act_s.sem, AC["zth0"])
                mark(dve.scalar_tensor_tensor(gate_th[:, :, :], gate_th[:, :, :], 1.0, z0[:, :, :], ALU.add, ALU.mult), "G0")

            def conv1(d):
                dve.wait_ge(act_s.sem, AC["xin1"])
                dst, src = (a[:, d, :].rearrange("p (b l) -> p b l", b=B) for a in (u, t0))
                link(dve.tensor_scalar(dst, src, hpar[:, 1, d, 3:4], hpar[:, 1, d, 4:5], ALU.mult, ALU.add))
                mark(taps(1, d, dst, src), f"conv1_{d}")

            def negA1():
                dve.wait_ge(act_s.sem, AC["negA1"])
                mark(dve.tensor_scalar(negA[:, 1, :, :], negA[:, 1, :, :], -1.0, None, ALU.mult), "negA1")

            def u1():
                for d in range(ND):
                    dve.wait_ge(act_s.sem, AC[f"th_u1_{d}"])
                    ins = dve.scalar_tensor_tensor(u[:, d, :], t1[:, d, :], 1.0, u[:, d, :], ALU.add, ALU.mult)
                mark(ins, "u1")

            def w1(d):
                dve.wait_ge(act_s.sem, AC[f"e1_{d}"])
                link(dve.tensor_scalar(du[:, d, :], t0[:, d, :], 1.0, None, ALU.add))
                mark(dve.scalar_tensor_tensor(du[:, d, :], du[:, d, :], 1.0, t0[:, d, :], ALU.subtract, ALU.subtract), f"w1_{d}", True)

            def delta1():
                dve.wait_ge(act_s.sem, AC["ln1"])
                link(dve.tensor_tensor(t1[:, :, :], t1[:, :, :], du[:, :, :], ALU.subtract))
                mark(dve.scalar_tensor_tensor(delta[:, :, :], delta[:, :, :], 0.0, t1[:, :, :], ALU.max, ALU.add), "delta1", True)

            def du1():
                mark(dve.tensor_tensor(du[:, :, :], delta[:, :, :], u[:, :, :], ALU.mult), "du1", True)

            def constants():
                dve.wait_ge(s_in[2], 32)
                for d in range(ND):
                    dve.tensor_scalar(diagD[:, d, :], ident[:, :], par[:, 0, d, 6:7], None, ALU.mult)
                dve.wait_ge(act_s.sem, AC["negA"])
                dve.wait_ge(pool_s.sem, POOL["zero"])
                dve.memset(first0[:, :, 0:1], 0.0)
                dve.memset(first1[:, :, 0:1], 0.0)
                mark(dve.tensor_scalar(negA[:, 0, :, :], negA[:, 0, :, :], -1.0, None, ALU.mult), "consts")

            def drive(h, q, row):
                return dve.tensor_tensor(dBu[:, q, :, :], du[:, :, h * HALF:(h + 1) * HALF],
                                         row.unsqueeze(1).to_broadcast([P, ND, HALF]), ALU.mult)

            def scan(q):
                return dve.tensor_tensor_scan(hs[:, q, :, :].rearrange("p a b -> p (a b)"),
                                              dA[:, q, :, :].rearrange("p a b -> p (a b)"),
                                              dBu[:, q, :, :].rearrange("p a b -> p (a b)"), 0.0, ALU.mult, ALU.add)

            def mixer0():
                for h in range(2):
                    if h == 1:
                        dve.wait_ge(pool_s.sem, POOL["du0_1"])
                    base = h * NS
                    with dve.Fori(0, NS // RING) as j:
                        for q in range(RING):
                            S = j * RING + q + base
                            dve.wait_ge(b_ready, S + 1)
                            drive(h, q, ps[:, 4 + q, :]).then_inc(dbu_done, 1)
                            dve.wait_ge(da_ready, S + 1)
                            dve.wait_ge(dbu_done, S + RING + 1)
                            dve.wait_ge(hc_done, S + 1)
                            scan(q).then_inc(scan_done, 1)

            def norm_stats(name, tiles, seen=0):
                for j in tiles[seen:]:
                    ins = dve.bn_stats(stats[:, j, :], xs[:, j, :])
                link(ins)
                for j in tiles:
                    ins = dve.bn_aggr(mv[:, j, :], stats[:, j, :])
                link(ins)
                v = mv[:, tiles[0]:tiles[-1] + 1, 1]
                mark(dve.tensor_scalar(v, v, EPS, None, ALU.add), name)

            def half_norm(z, j):
                return dve.tensor_scalar(z[:, j % 2, (j // 2) * L:(j // 2 + 1) * L], xs[:, j, :], mv[:, j, 0:1],
                                         rstd[:, j:j + 1], ALU.subtract, ALU.mult)

            def times_gate0(h):
                    dve.wait_ge(y_done, (h + 1) * NS + RING)
                    t = halves[h]
                    mark(dve.tensor_tensor(t0[:, :, t], ps[:, 2 * h:2 * h + 2, :], gate_th[:, :, t], ALU.mult), f"yz0_{h}")

            def times_gate1():
                for h in range(2):
                    dve.wait_ge(pool_s.sem, POOL[f"zr1_{h}"])
                    link(dve.tensor_scalar(rstd[:, 4 * h:4 * h + 4], rstd[:, 4 * h:4 * h + 4], 0.5, None, ALU.mult))
                    for j in range(4 * h, 4 * h + 4):
                        ins = half_norm(t0, j)
                    mark(ins, f"zh1_{h}", True)
                dve.wait_ge(pool_s.sem, POOL["y1"])
                for h in range(2):
                    t = slice(h * HALF, (h + 1) * HALF)
                    link(dve.tensor_tensor(y1[:, :, t], y1[:, :, t], t0[:, :, t], ALU.mult))
                    dve.wait_ge(act_s.sem, AC[f"zth1_{h}"])
                    mark(dve.scalar_tensor_tensor(t0[:, :, t], t1[:, :, t], 1.0, y1[:, :, t], ALU.add, ALU.mult), f"yz1_{h}")

            def norm_out(k):
                xf = xs[:, :, :].rearrange("p j c -> p (j c)")
                for h in range(2):
                    part = xf[:, h * 2 * BANK:(h + 1) * 2 * BANK]
                    if k == 0:
                        times_gate0(h)
                    dve.wait_ge(pe_s.sem, PE[f"yT{k}_{h}"])
                    link(dve.tensor_tensor(part, part, ps[:, 4 + 2 * h:6 + 2 * h, :].rearrange("p h t -> p (h t)"), ALU.add))
                    norm_stats(f"nstat{k}_{h}", range(4 * h, 4 * h + 4))
                for h in range(2):
                    dve.wait_ge(pool_s.sem, POOL[f"nr{k}_{h}"])
                    for j in range(4 * h, 4 * h + 4):
                        ins = dve.tensor_scalar(xn_rows[:, j, :], xs[:, j, :], mv[:, j, 0:1],
                                                rstd[:, j:j + 1], ALU.subtract, ALU.mult)
                    mark(ins, f"xn{k}_{h}")

            def by_e(t, E):
                return t[:, :, :].rearrange("p j e -> p (j e)")[:, 0:TT * E].rearrange("p (j e) -> p j e", e=E)

            def flat(t, E):
                return t[:, :, :].rearrange("p j e -> p (j e)")[:, 0:TT * E]

            def pick(score, E, top, tiles=slice(0, TT)):
                for j in range(tiles.start, tiles.stop):
                    ins = dve.max(top8[:, j, :], score[:, j, :])
                link(ins)
                n = tiles.stop - tiles.start
                kth = top8[:, tiles, top - 1:top].to_broadcast([P, n, E])
                gt, eq, cum = (by_e(r, E)[:, tiles, :] for r in (r2, r1, r0))
                dve.tensor_tensor(gt, score[:, tiles, :], kth, ALU.is_gt)
                link(dve.tensor_tensor(eq, score[:, tiles, :], kth, ALU.is_equal))
                dve.tensor_reduce(need[:, tiles], gt, AX_X, ALU.add)
                at = slice(tiles.start * E, tiles.stop * E)
                link(dve.tensor_tensor_scan(flat(r0, E)[:, at], flat(first0 if E == E0 else first1, E)[:, at],
                                            flat(r1, E)[:, at], 0.0, ALU.mult, ALU.add))
                link(dve.tensor_scalar(need[:, tiles], need[:, tiles], -1.0, float(top), ALU.mult, ALU.add))
                link(dve.tensor_tensor(cum, cum, need[:, tiles].unsqueeze(2).to_broadcast([P, n, E]), ALU.is_le))
                link(dve.tensor_tensor(eq, eq, cum, ALU.mult))
                link(dve.tensor_tensor(gt, gt, eq, ALU.add))

            mark(dve.memset(zero[:, :], 0.0), "zero")
            dve.wait_ge(s_par, 16)
            mark(dve.tensor_scalar(hpar[:, :, :, :], par[:, :, :, :], 0.5, None, ALU.mult), "hpar", True)
            dve.sem_inc(dbu_done, RING)
            dve.sem_inc(scan_done, RING)
            prep0()
            mixer0()
            norm_out(0)

            dve.wait_ge(pe_s.sem, PE["logit0_1"])
            l0 = by_e(lg, E0)
            link(dve.tensor_copy(flat(lg, E0).rearrange("p (h n) -> p h n", h=2), ps[:, 4:6, 0:TT // 2 * E0]))
            pick(l0, E0, TOPK0)
            mark(dve.tensor_tensor(by_e(r1, E0), l0, top8[:, :, 0:1].to_broadcast([P, TT, E0]), ALU.subtract), "lsub0")
            mark(dve.tensor_copy(flat(maskb, E0), flat(r2, E0)), "sel0")
            NE = TT * E0
            rank, place = big[:, 0:NE], big[:, NE:2 * NE]
            sel = big[:, 2 * NE:(2 + TOPK0) * NE].rearrange("p (k n) -> p k n", k=TOPK0)
            prod = big[:, (2 + TOPK0) * NE:(2 + 2 * TOPK0) * NE].rearrange("p (k n) -> p k n", k=TOPK0)
            by_sum = big[:, (2 + TOPK0) * NE:(2 + 2 * TOPK0) * NE].rearrange("p (a e) -> p a e", e=E0)
            ks = steps[:, 8:8 + TOPK0]

            def over_k(t):
                return t.unsqueeze(1).to_broadcast([P, TOPK0, NE])

            dve.wait_ge(s_in[5], 16)
            link(dve.tensor_tensor_scan(rank, flat(first0, E0), flat(r2, E0), 0.0, ALU.mult, ALU.add))
            link(dve.tensor_tensor(sel, over_k(rank), ks.unsqueeze(2).to_broadcast([P, TOPK0, NE]), ALU.is_equal))
            link(dve.tensor_tensor(sel, sel, over_k(flat(r2, E0)), ALU.mult))
            dve.wait_ge(pe_s.sem, PE["pos0"])
            cmp = prod.rearrange("p k n -> p (k n)")[:, 0:E0 * 8].rearrange("p (e m) -> p e m", m=8)
            link(dve.tensor_tensor(cmp, ps[:, 5, NE:NE + E0].unsqueeze(2).to_broadcast([P, E0, 8]),
                                   steps[:, 0:8].unsqueeze(1).to_broadcast([P, E0, 8]), ALU.is_gt))
            link(dve.tensor_reduce(nblk[:, :], cmp, AX_X, ALU.add))
            link(dve.tensor_tensor_scan(endb[:, :], first1[:, 0, 1:1 + E0], nblk[:, :], 0.0, ALU.mult, ALU.add))
            link(dve.tensor_tensor(startb[:, :], endb[:, :], nblk[:, :], ALU.subtract))
            link(dve.scalar_tensor_tensor(place.rearrange("p (j e) -> p j e", e=E0),
                                          startb[:, :].unsqueeze(1).to_broadcast([P, TT, E0]), float(P),
                                          ps[:, 5, 0:NE].rearrange("p (j e) -> p j e", e=E0), ALU.mult, ALU.add))
            link(dve.tensor_tensor(prod, sel, over_k(place), ALU.mult))
            sf = slot_f[:, :, :].rearrange("p k j -> p (k j)")
            link(dve.tensor_reduce(sf, by_sum, AX_X, ALU.add))
            mark(dve.tensor_copy(slot_u[:, :, :].rearrange("p k j -> p (k j)"), sf), "slots0")
            NBP = NB + 1
            eb, m3 = blk_f[0:1, 0, 0:NBP], blk_f[0:1, 1, 0:NBP]
            cmp = big[0:1, (2 + TOPK0) * NE:(2 + TOPK0) * NE + NBP * 8].rearrange("p (b e) -> p b e", e=8)
            ids = steps[0:1, 32:32 + NBP].unsqueeze(2)
            for part in range(2):
                link(dve.tensor_tensor(cmp, endb[0:1, 8 * part:8 * part + 8].unsqueeze(1).to_broadcast([1, NBP, 8]),
                                       ids.to_broadcast([1, NBP, 8]), ALU.is_le))
                link(dve.tensor_reduce(blk_f[0:1, part, 0:NBP], cmp, AX_X, ALU.add))
            link(dve.tensor_tensor(eb, eb, m3, ALU.add))
            link(dve.tensor_scalar(eb, eb, float(E0 - 1), None, ALU.min))
            dve.tensor_scalar(blk_need[:, 0:NBP], eb, 1.0, None, ALU.add)
            dve.tensor_scalar(blk_rank[:, 0:NBP], eb, 1.0, float(TOPK0), ALU.add, ALU.min)
            dve.tensor_scalar(end_g[:, :], endb[0:1, :], 3.0, None, ALU.add)
            NM = (E0 - 1) // WR
            cmp = big[0:1, (2 + TOPK0) * NE:(2 + TOPK0) * NE + NBP * NM].rearrange("p (b e) -> p b e", e=NM)
            link(dve.tensor_tensor(cmp, eb.unsqueeze(2).to_broadcast([1, NBP, NM]),
                                   steps[0:1, 16:16 + NM].unsqueeze(1).to_broadcast([1, NBP, NM]), ALU.is_ge))
            link(dve.tensor_reduce(m3, cmp, AX_X, ALU.add))
            dve.scalar_tensor_tensor(blk_ring[:, 0:NBP], m3, -float(WR), eb, ALU.mult, ALU.add)
            mark(dve.tensor_scalar(end_i[:, :], endb[0:1, :], 1.0, None, ALU.add), "blocks0")
            dve.wait_ge(act_s.sem, AC["ex0"])
            link(dve.tensor_tensor(flat(r0, E0), flat(r0, E0), flat(r2, E0), ALU.mult))
            link(dve.tensor_reduce(need[:, :], by_e(r0, E0), AX_X, ALU.add))
            link(dve.reciprocal(need[:, :], need[:, :]))
            link(dve.tensor_tensor(by_e(r0, E0), by_e(r0, E0), need[:, :].unsqueeze(2).to_broadcast([P, TT, E0]), ALU.mult))
            link(dve.tensor_tensor(prod, sel, over_k(flat(r0, E0)), ALU.mult))
            mark(dve.tensor_reduce(wk[:, :, :].rearrange("p k j -> p (k j)"), by_sum, AX_X, ALU.add), "route0", True)

            for s in (dbu1, scan1):
                dve.sem_inc(s, RING)

            def hidden(i, c):
                if not has(i, c):
                    return
                dve.wait_ge(th_done, nth(i, c) + 1)
                dve.scalar_tensor_tensor(pg[:, c % 2, 0:H0], th[:, c % 2, 0:H0], 1.0, ps[:, 2 + c % 2, 0:H0],
                                         ALU.add, ALU.mult).then_inc(p_done, 1)
                dve.wait_ge(p_done, nth(i, c) + 1)
                if c >= RING or not isinstance(i, int):
                    dve.wait_ge(h_turned, nth(i, c) - RING + 1)
                dve.scalar_tensor_tensor(hx[:, c % 2, 0:H0], pg[:, c % 2, 0:H0], 0.5, ps[:, c % 2, 0:H0],
                                         ALU.mult, ALU.mult).then_inc(h_done, 1)

            def body(i, h, n):
                for r in range(BODY):
                    hidden(i, r + LEAD)
                    if h is not None:
                        t = i * BSTEP + r
                        dve.wait_ge(s_b[r % RING], (i * (BSTEP // RING) + r // RING) * 16 + 16)
                        drive(h, r % 2, Bsb[:, r % 2, :]).then_inc(dbu1, 1)
                        dve.wait_ge(dbu1, t + RING + 1)
                        dve.wait_ge(da1, t + 1)
                        dve.wait_ge(hc1, t + 1)
                        scan(r % 2).then_inc(scan1, 1)

            prepare = {0: [(u1,)], 1: [(negA1,)], 3: [(w1, 0)], 4: [(w1, 1)], 5: [(delta1,)], 6: [(du1,)]}
            for d in range(ND):
                conv1(d)
            for s in range(LEAD):
                hidden(0, s)
                for f, *where in prepare.get(s, ()):
                    f(*where)
            dve.wait_ge(ranks_in, TOPK0)
            bodies(dve, body)
            for k in range(TOPK0):
                if k < TOPK0 - 1:
                    dve.wait_ge(s_gk[k], TT * 16)
                for j in range(TT):
                    if k == TOPK0 - 1:
                        dve.wait_ge(s_gj[j], 16)
                    if k:
                        dve.wait_ge(s_comb, (k - 1) * TT + j + 1)
                    dve.scalar_tensor_tensor(xs[:, j, :], gb[k][:, j, :], wk[:, k, j:j + 1], xs[:, j, :],
                                             ALU.mult, ALU.add).then_inc(s_comb, 1)
                    if k == TOPK0 - 1 and j:
                        dve.wait_ge(s_comb, k * TT + j)
                        if j != TT // 2:
                            dve.bn_stats(stats[:, j - 1, :], xs[:, j - 1, :])
                    if k == TOPK0 - 1 and j == TT // 2:
                        norm_stats("zstat1_0", range(TT // 2), TT // 2 - 1)
            dve.wait_ge(s_comb, TT * TOPK0)
            norm_stats("zstat1_1", range(TT // 2, TT), TT // 2 - 1)
            times_gate1()
            norm_out(1)
            for h in range(2):
                tiles = slice(4 * h, 4 * h + 4)
                dve.wait_ge(act_s.sem, AC[f"ex1_{h}"])
                link(dve.tensor_scalar(r0[:, tiles, :], r0[:, tiles, :], 1.0, None, ALU.add))
                link(dve.reciprocal(lg[:, tiles, :], r0[:, tiles, :]))
                pick(lg[:, :, :], E1, TOPK1, tiles)
            mark(dve.tensor_copy(maskb[:, :, :], r2[:, :, :]), "sel1")
            for h in range(2):
                dve.wait_ge(act_s.sem, AC[f"sh_th{h}"])
                link(dve.scalar_tensor_tensor(pg[P // 2:P, h, :], th[P // 2:P, h, :], 1.0, ps[P // 2:P, 6 + h, :], ALU.add, ALU.mult))
                mark(dve.scalar_tensor_tensor(hT[0:P // 2, h, :], pg[P // 2:P, h, :], 0.5, ps[0:P // 2, 6 + h, :], ALU.mult, ALU.mult), f"sh_h{h}")
            link(dve.tensor_tensor(r0[:, :, :], lg[:, :, :], r2[:, :, :], ALU.mult))
            link(dve.tensor_reduce(need[:, :], r0[:, :, :], AX_X, ALU.add))
            link(dve.reciprocal(need[:, :], need[:, :]))
            link(dve.tensor_tensor(r0[:, :, :], r0[:, :, :], need[:, :].unsqueeze(2).to_broadcast([P, TT, E1]), ALU.mult))
            dve.wait_ge(pe_s.sem, PE["pos1"])
            for a in range(2):
                ins = dve.scalar_tensor_tensor(w2x[:, :, a, :], ps[:, 5, :].rearrange("p (j e) -> p j e", j=TT), float(CAP),
                                               r0[:, :, :], ALU.is_lt, ALU.mult)
            mark(ins, "route1")
            for h in range(2):
                t = slice(h * HALF, (h + 1) * HALF)
                dve.wait_ge(act_s.sem, AC[f"whi1_{h}"])
                mark(dve.tensor_tensor(w_of[E1:P, t], ps[E1:P, 6 + h, :], w_of[E1:P, t].bitcast(F32), ALU.subtract), f"wlo1_{h}")
            for s in (g_p, g_q, g_h):
                dve.sem_inc(s, 1)
            with dve.Fori(0, NG) as i:
                for h in range(2):
                    n = i * 2 + h
                    dve.wait_ge(g_th, n + 1)
                    dve.scalar_tensor_tensor(pg[:, h, :], th[:, h, :], 1.0, ps[:, 4, :], ALU.add, ALU.mult).then_inc(g_p, 1)
                    dve.wait_ge(g_v, n + 1)
                    dve.wait_ge(g_p, n + 2)
                    dve.scalar_tensor_tensor(hx[:, h, :], pg[:, h, :], 0.5, ps[:, 5, :], ALU.mult, ALU.mult).then_inc(g_q, 1)
                    dve.wait_ge(g_w, n + 1)
                    dve.wait_ge(g_q, n + 2)
                    dve.tensor_tensor(hT[:, h, :], hx[:, h, :], ps[:, 6, :], ALU.mult).then_inc(g_h, 1)
                    dve.wait_ge(g_hhi, n + 1)
                    dve.tensor_tensor(h_lo[:, h, :], hT[:, h, :], h_hi[:, h, :].bitcast(F32), ALU.subtract).then_inc(g_hlo, 1)
            xf = xs[:, :, :].rearrange("p j c -> p (j c)")
            for h in range(2):
                part = xf[:, h * 2 * BANK:(h + 1) * 2 * BANK]
                dve.wait_ge(g_dn, 2 * NG - 1 + h)
                mark(dve.tensor_tensor(part, part, ps[:, 2 * h:2 * h + 2, :].rearrange("p h t -> p (h t)"), ALU.add), f"out{h}")


def lay_out(inp):
    import numpy as np

    g = {k: np.asarray(v) for k, v in inp.items()}
    f = np.float32
    P = 128
    x = g["x"]
    B, L, C = x.shape
    ctxt = g["ctx_1024"].reshape(B * L, -1).T
    par = np.zeros((P, 2, 2, 24), f)
    xpr = np.zeros((P, 2, 2, P), f)
    inpT, dtT = [], []
    for k in range(2):
        p = f"L{k}_xattn_"
        di = g[p + "in_proj_w"].shape[0]
        inpT.append(g[p + "in_proj_w"].T)
        dtT.append(g[p + "dt_proj_w"].T)
        cw = g[p + "conv_w"].reshape(di, 4)
        for d in range(2):
            r = slice(d * P, (d + 1) * P)
            par[:, k, d, 0:4] = cw[r]
            par[:, k, d, 4] = g[p + "conv_b"][r]
            par[:, k, d, 5] = g[p + "dt_proj_b"][r]
            par[:, k, d, 6] = g[p + "D"][r]
            par[:, k, d, 8:24] = g[p + "A_log"][r]
            xw = g[p + "x_proj_w"][:, r].T
            xpr[:, k, d, 0:8] = xw[:, 0:8]
            for c in range(3):
                xpr[:, k, d, 32 + 32 * c:64 + 32 * c] = xw[:, 8:40]
    up, gt, dn = g["L0_ffn_W_up"], g["L0_ffn_W_gate"], g["L0_ffn_W_down"]
    E, H, _ = up.shape
    ug = np.concatenate([up, gt], axis=1).transpose(0, 2, 1).reshape(E, 2, P, 2 * H).transpose(0, 2, 1, 3)
    dT = dn.transpose(0, 2, 1).reshape(E, 4, H // 4, C).transpose(0, 2, 1, 3)
    gate0 = g["L0_ffn_gate_inp"].T.reshape(2, P, E).transpose(1, 0, 2)
    gate1 = g["L1_ffn_w_gate"].reshape(2, P, -1).transpose(1, 0, 2)
    shu = g["L1_ffn_w_shared_up"].reshape(2, P, P).transpose(1, 0, 2)
    wu, wd = g["L1_ffn_w_up"], g["L1_ffn_w_down"]
    E1, _, H2 = wu.shape
    H1 = H2 // 2
    EG = P // H1
    NG = E1 // EG
    w = wu.reshape(NG, EG, 2, P, 2, H1).transpose(0, 3, 2, 4, 1, 5).reshape(NG, P, 4 * P)
    grp = np.concatenate([w, wd.reshape(NG, P, C)], axis=2)
    sel3 = np.zeros((P, 32), f)
    for c in range(1, 4):
        sel3[32 * c:32 * c + 32] = np.eye(32)
    tri = np.zeros((P, 2, P), f)
    tri[:, 0] = np.triu(np.ones((P, P)), 1)
    tri[:, 1] = 1
    steps = np.zeros((P, 96), f)
    steps[:, 0:8] = P * np.arange(8)
    steps[:, 0] = -1
    steps[:, 8:12] = np.arange(1, 5)
    steps[:, 16:24] = 3 * np.arange(1, 9)
    steps[:, 32:96] = np.arange(64)
    sel64 = np.repeat(np.concatenate([np.eye(E1), np.eye(E1)]), P // EG, axis=1).astype(f)
    bf = mybir.dt.np(mybir.dt.bfloat16)
    return {
        "x": x.reshape(B * L, C), "ctxT": ctxt, "in_projT": np.stack(inpT), "ssm_par": par, "x_projT": xpr,
        "dt_projT": np.stack(dtT), "gate0T": gate0, "up0T": ug, "down0T": dT, "gate1T": gate1, "sh_upT": shu,
        "sh_down": g["L1_ffn_w_shared_down"], "grp1": grp, "ident": np.eye(P, dtype=f),
        "sel3": sel3.astype(bf), "tri": tri.astype(bf), "sel64": sel64.astype(bf), "steps": steps,
    }


def kernel(**inputs):
    import numpy as np
    import concourse.bacc as bacc
    from concourse.bass_utils import run_bass_kernel_spmd

    nc = bacc.Bacc("TRN2", target_bir_lowering=False, num_devices=1)
    arrays, args = {}, []
    for name, a in lay_out(inputs).items():
        a = np.ascontiguousarray(a)
        arrays[f"in_{name}"] = a
        args.append(nc.dram_tensor(f"in_{name}", a.shape, mybir.dt.from_np(a.dtype), kind="ExternalInput").ap())
    shape = inputs["x"].shape
    out = nc.dram_tensor("out_0", (shape[0] * shape[1], shape[2]), F32, kind="ExternalOutput").ap()
    build(nc, *args, out)
    r = run_bass_kernel_spmd(nc, [arrays], core_ids=[0])
    return r.results[0]["out_0"].reshape(shape)
```
